# Optimizing a Trainium2 kernel written in Bass

```python
import numpy as np
import jax
import jax.numpy as jnp

def _softmax(x, axis=-1):
    return jax.nn.softmax(x, axis=axis)

def _gelu(x):
    return jax.nn.gelu(x, approximate=True)

def _silu(x):
    return jax.nn.silu(x)

def _sigmoid(x):
    return jax.nn.sigmoid(x)

def _layernorm(x, axis=-1, eps=1e-05):
    m = jnp.mean(x, axis=axis, keepdims=True)
    v = jnp.var(x, axis=axis, keepdims=True)
    return (x - m) / jnp.sqrt(v + eps)

def _scatter_add(tgt, idx, src, axis=0):
    return tgt.at[idx].add(src)

def _segment_sum(src, seg, n):
    return jax.ops.segment_sum(src, seg, n)
kernel_name = 'mk_gnn_resnorm_d4_gnn_r16_5ee241'

def setup_inputs(seed: int=0):
    np.random.seed(seed)
    _w = jnp.asarray

    def _rec_inputs():
        import jax
        import jax.numpy as jnp
        _gk = jax.random.key(seed)
        x = -0.0004402 + 1 * jax.random.normal(jax.random.fold_in(_gk, 1), (6250, 16), jnp.float32)
        src = jax.random.randint(jax.random.fold_in(_gk, 2), (200000,), 0, 6250, jnp.int32)
        dst = jnp.minimum((6250 * jax.random.uniform(jax.random.fold_in(_gk, 3), (200000,)) ** 2.0).astype(jnp.int32), 99999)
        _o = jnp.argsort(dst, stable=True)
        src = src[_o]
        dst = dst[_o]
        edge_attr_16 = -3.57403e-05 + 0.999761 * jax.random.normal(jax.random.fold_in(_gk, 12), (200000, 16), jnp.float32)
        edge_attr_8 = -5.3897e-05 + 0.999841 * jax.random.normal(jax.random.fold_in(_gk, 13), (200000, 8), jnp.float32)
        edge_type_8 = jax.random.randint(jax.random.fold_in(_gk, 15), (200000,), 0, 8, jnp.int32)
        node_vec1 = -0.00472126 + 0.997171 * jax.random.normal(jax.random.fold_in(_gk, 16), (6250, 1), jnp.float32)
        return (x, src, dst, edge_attr_16, edge_attr_8, edge_type_8, node_vec1)
    x, src, dst, edge_attr_16, edge_attr_8, edge_type_8, node_vec1 = _rec_inputs()

    def _L0_gnn_setup():
        import jax, jax.numpy as jnp
        import numpy as np
        N_NODES = 1875
        N_EDGES = 18750
        IN_FEATS = 16
        OUT_FEATS = 16
        EDGE_DIM = 16
        key = jax.random.key(seed)
        ks = jax.random.split(key, 8)
        feat = jax.random.normal(ks[0], (N_NODES, IN_FEATS), dtype=jnp.float32)
        efeat = jax.random.normal(ks[1], (N_EDGES, EDGE_DIM), dtype=jnp.float32)
        W_msg = jax.random.normal(ks[2], (EDGE_DIM, IN_FEATS * OUT_FEATS), dtype=jnp.float32) * 0.1
        b_msg = jnp.zeros((IN_FEATS * OUT_FEATS,), dtype=jnp.float32)
        W_attn = jax.random.normal(ks[3], (EDGE_DIM, IN_FEATS * OUT_FEATS), dtype=jnp.float32) * 0.1
        b_attn = jnp.zeros((IN_FEATS * OUT_FEATS,), dtype=jnp.float32)
        src = jax.random.randint(ks[4], (N_EDGES,), 0, N_NODES, dtype=jnp.int32)
        dst = jax.random.randint(ks[5], (N_EDGES,), 0, N_NODES, dtype=jnp.int32)
        return {'feat': feat, 'efeat': efeat, 'W_msg': W_msg, 'b_msg': b_msg, 'W_attn': W_attn, 'b_attn': b_attn, 'src': src, 'dst': dst}
    _L0_gnn_all = _L0_gnn_setup()
    _L0_gnn_in = {k: v for k, v in _L0_gnn_all.items() if k in ('W_msg', 'b_msg', 'W_attn', 'b_attn')}
    del _L0_gnn_all

    def _L1_gnn_setup():
        import jax, jax.numpy as jnp
        import numpy as np
        NUM_ENTITIES = 6250
        NUM_RELATIONS = 8
        NUM_CLASSES = 16
        HIDDEN = 16
        NUM_EDGES = 200000

        def rgcn_conv(x, src, dst, edge_type, W, root, bias):
            num_nodes = x.shape[0]
            x_src = x[src]
            msg = jnp.zeros((src.shape[0], W.shape[2]), x.dtype)
            for r in range(NUM_RELATIONS):
                msg = msg + jnp.where((edge_type == r)[:, None], x_src @ W[r], jnp.zeros((), x.dtype))
            cnt = jnp.zeros((num_nodes, NUM_RELATIONS), x.dtype).at[dst, edge_type].add(1.0)
            norm = 1.0 / jnp.maximum(cnt[dst, edge_type], 1.0)
            agg = jax.ops.segment_sum(msg * norm[:, None], dst, num_segments=num_nodes)
            return agg + x @ root + bias
        key = jax.random.key(seed)
        ks = jax.random.split(key, 9)
        s = 1.0 / np.sqrt(HIDDEN)
        edge_index = jax.random.randint(ks[0], (2, NUM_EDGES), 0, NUM_ENTITIES, dtype=jnp.int32)
        edge_type = jax.random.randint(ks[1], (NUM_EDGES,), 0, NUM_RELATIONS, dtype=jnp.int32)
        return {'embed': jax.random.normal(ks[2], (NUM_ENTITIES, HIDDEN), jnp.float32), 'W1': jax.random.normal(ks[3], (NUM_RELATIONS, HIDDEN, HIDDEN), jnp.float32) * s, 'root1': jax.random.normal(ks[4], (HIDDEN, HIDDEN), jnp.float32) * s, 'b1': jnp.zeros((HIDDEN,), jnp.float32), 'W2': jax.random.normal(ks[5], (NUM_RELATIONS, HIDDEN, NUM_CLASSES), jnp.float32) * s, 'root2': jax.random.normal(ks[6], (HIDDEN, NUM_CLASSES), jnp.float32) * s, 'b2': jnp.zeros((NUM_CLASSES,), jnp.float32), 'edge_index': edge_index, 'edge_type': edge_type}
    _L1_gnn_all = _L1_gnn_setup()
    _L1_gnn_in = {k: v for k, v in _L1_gnn_all.items() if k in ('W1', 'root1', 'b1', 'W2', 'root2', 'b2')}
    del _L1_gnn_all

    def _L2_gnn_setup():
        import jax, jax.numpy as jnp
        import numpy as np
        N_NODES = 6250
        N_EDGES = 200000
        D_NODE = 16
        D_EDGE = 8
        D_HIDDEN = 16
        key = jax.random.key(seed)
        ks = jax.random.split(key, 8)
        node_features = jax.random.normal(ks[0], (N_NODES, D_NODE), dtype=jnp.float32)
        edge_attr_e3nn = jax.random.normal(ks[1], (N_EDGES, D_EDGE), dtype=jnp.float32)
        node_attr_scalar_raw = jax.random.normal(ks[2], (N_NODES, 1), dtype=jnp.float32)
        W_msg_tp = jax.random.normal(ks[3], (D_NODE, D_EDGE, D_HIDDEN), dtype=jnp.float32)
        W_msg_lin = jax.random.normal(ks[4], (D_HIDDEN, D_HIDDEN), dtype=jnp.float32)
        W_upd_tp = jax.random.normal(ks[5], (D_NODE, D_HIDDEN, D_HIDDEN), dtype=jnp.float32)
        W_upd_lin = jax.random.normal(ks[6], (D_HIDDEN, D_NODE), dtype=jnp.float32)
        edge_index = jax.random.randint(ks[7], (2, N_EDGES), 0, N_NODES, dtype=jnp.int64)
        return {'node_features': node_features, 'edge_attr_e3nn': edge_attr_e3nn, 'node_attr_scalar_raw': node_attr_scalar_raw, 'W_msg_tp': W_msg_tp, 'W_msg_lin': W_msg_lin, 'W_upd_tp': W_upd_tp, 'W_upd_lin': W_upd_lin, 'edge_index': edge_index}
    _L2_gnn_all = _L2_gnn_setup()
    _L2_gnn_in = {k: v for k, v in _L2_gnn_all.items() if k in ('W_msg_tp', 'W_msg_lin', 'W_upd_tp', 'W_upd_lin')}
    del _L2_gnn_all

    def _L3_gnn_setup():
        import jax, jax.numpy as jnp
        import numpy as np
        N_NODES = 3125
        N_EDGES = 25000
        D = 16
        E_FEAT = 8
        N_LAYERS = 3
        BN_EPS = 1e-05

        def _nnconv(x, src, dst, edge_attr, ew, eb, rw, rb):
            W = (edge_attr @ ew + eb).reshape(edge_attr.shape[0], x.shape[1], rw.shape[1])
            xj = x[src]
            msg = jnp.einsum('ei,eio->eo', xj, W)
            agg = jax.ops.segment_sum(msg, dst, num_segments=x.shape[0])
            return agg + x @ rw + rb

        def _batchnorm(x, gamma, beta):
            mean = jnp.mean(x, axis=0)
            var = jnp.mean(jnp.square(x - mean), axis=0)
            return (x - mean) * jax.lax.rsqrt(var + BN_EPS) * gamma + beta
        key = jax.random.key(seed)
        ks = jax.random.split(key, 12)
        x = jax.random.normal(ks[0], (N_NODES, D), dtype=jnp.float32)
        edge_index = jax.random.randint(ks[1], (2, N_EDGES), 0, N_NODES, dtype=jnp.int64)
        edge_attr = jax.random.normal(ks[2], (N_EDGES, E_FEAT), dtype=jnp.float32)
        s = 0.1
        edge_w = jax.random.normal(ks[3], (N_LAYERS, E_FEAT, D * D), dtype=jnp.float32) * s
        edge_b = jax.random.normal(ks[4], (N_LAYERS, D * D), dtype=jnp.float32) * s
        root_w = jax.random.normal(ks[5], (N_LAYERS, D, D), dtype=jnp.float32) * s
        root_b = jax.random.normal(ks[6], (N_LAYERS, D), dtype=jnp.float32) * s
        bn_gamma = jnp.ones((N_LAYERS - 1, D), dtype=jnp.float32)
        bn_beta = jnp.zeros((N_LAYERS - 1, D), dtype=jnp.float32)
        pred_w = jax.random.normal(ks[7], (D, D), dtype=jnp.float32) * s
        pred_b = jax.random.normal(ks[8], (D,), dtype=jnp.float32) * s
        return {'x': x, 'edge_index': edge_index, 'edge_attr': edge_attr, 'edge_w': edge_w, 'edge_b': edge_b, 'root_w': root_w, 'root_b': root_b, 'bn_gamma': bn_gamma, 'bn_beta': bn_beta, 'pred_w': pred_w, 'pred_b': pred_b}
    _L3_gnn_all = _L3_gnn_setup()
    _L3_gnn_in = {k: v for k, v in _L3_gnn_all.items() if k in ('edge_w', 'edge_b', 'root_w', 'root_b', 'bn_gamma', 'bn_beta', 'pred_w', 'pred_b')}
    del _L3_gnn_all
    return {'x': x, 'src': src, 'dst': dst, 'edge_attr_16': edge_attr_16, 'edge_attr_8': edge_attr_8, 'edge_type_8': edge_type_8, 'node_vec1': node_vec1, 'L0_gnn_W_msg': _L0_gnn_in['W_msg'], 'L0_gnn_b_msg': _L0_gnn_in['b_msg'], 'L0_gnn_W_attn': _L0_gnn_in['W_attn'], 'L0_gnn_b_attn': _L0_gnn_in['b_attn'], 'L1_gnn_W1': _L1_gnn_in['W1'], 'L1_gnn_root1': _L1_gnn_in['root1'], 'L1_gnn_b1': _L1_gnn_in['b1'], 'L1_gnn_W2': _L1_gnn_in['W2'], 'L1_gnn_root2': _L1_gnn_in['root2'], 'L1_gnn_b2': _L1_gnn_in['b2'], 'L2_gnn_W_msg_tp': _L2_gnn_in['W_msg_tp'], 'L2_gnn_W_msg_lin': _L2_gnn_in['W_msg_lin'], 'L2_gnn_W_upd_tp': _L2_gnn_in['W_upd_tp'], 'L2_gnn_W_upd_lin': _L2_gnn_in['W_upd_lin'], 'L3_gnn_edge_w': _L3_gnn_in['edge_w'], 'L3_gnn_edge_b': _L3_gnn_in['edge_b'], 'L3_gnn_root_w': _L3_gnn_in['root_w'], 'L3_gnn_root_b': _L3_gnn_in['root_b'], 'L3_gnn_bn_gamma': _L3_gnn_in['bn_gamma'], 'L3_gnn_bn_beta': _L3_gnn_in['bn_beta'], 'L3_gnn_pred_w': _L3_gnn_in['pred_w'], 'L3_gnn_pred_b': _L3_gnn_in['pred_b']}

def reference(x, src, dst, edge_attr_16, edge_attr_8, edge_type_8, node_vec1, L0_gnn_W_msg, L0_gnn_b_msg, L0_gnn_W_attn, L0_gnn_b_attn, L1_gnn_W1, L1_gnn_root1, L1_gnn_b1, L1_gnn_W2, L1_gnn_root2, L1_gnn_b2, L2_gnn_W_msg_tp, L2_gnn_W_msg_lin, L2_gnn_W_upd_tp, L2_gnn_W_upd_lin, L3_gnn_edge_w, L3_gnn_edge_b, L3_gnn_root_w, L3_gnn_root_b, L3_gnn_bn_gamma, L3_gnn_bn_beta, L3_gnn_pred_w, L3_gnn_pred_b):
    import jax
    import jax.numpy as jnp

    def _L0_gnn_ref(feat, efeat, W_msg, b_msg, W_attn, b_attn, src, dst):
        import jax, jax.numpy as jnp
        import numpy as np
        N_NODES = 1875
        N_EDGES = 18750
        IN_FEATS = 16
        OUT_FEATS = 16
        EDGE_DIM = 16
        N, in_f = feat.shape
        E = efeat.shape[0]
        w_m = (efeat @ W_msg + b_msg).reshape(E, in_f, -1)
        w_a = (efeat @ W_attn + b_attn).reshape(E, in_f, -1)
        h_src = feat[src][:, :, None]
        e1 = w_m * h_src
        e2 = w_a * h_src
        seg_max = jax.ops.segment_max(e2, dst, num_segments=N)
        ex = jnp.exp(e2 - seg_max[dst])
        denom = jax.ops.segment_sum(ex, dst, num_segments=N)
        attn = ex / denom[dst]
        ft = jax.ops.segment_sum(e1 * attn, dst, num_segments=N)
        return ft.sum(axis=1)

    def _L1_gnn_ref(embed, W1, root1, b1, W2, root2, b2, edge_index, edge_type):
        import jax, jax.numpy as jnp
        import numpy as np
        NUM_ENTITIES = 6250
        NUM_RELATIONS = 8
        NUM_CLASSES = 16
        HIDDEN = 16
        NUM_EDGES = 200000

        def rgcn_conv(x, src, dst, edge_type, W, root, bias):
            num_nodes = x.shape[0]
            x_src = x[src]
            msg = jnp.zeros((src.shape[0], W.shape[2]), x.dtype)
            for r in range(NUM_RELATIONS):
                msg = msg + jnp.where((edge_type == r)[:, None], x_src @ W[r], jnp.zeros((), x.dtype))
            cnt = jnp.zeros((num_nodes, NUM_RELATIONS), x.dtype).at[dst, edge_type].add(1.0)
            norm = 1.0 / jnp.maximum(cnt[dst, edge_type], 1.0)
            agg = jax.ops.segment_sum(msg * norm[:, None], dst, num_segments=num_nodes)
            return agg + x @ root + bias
        src, dst = (edge_index[0], edge_index[1])
        h = rgcn_conv(embed, src, dst, edge_type, W1, root1, b1)
        h = jax.nn.relu(h)
        h = rgcn_conv(h, src, dst, edge_type, W2, root2, b2)
        return jax.nn.log_softmax(h, axis=1)

    def _L2_gnn_ref(node_features, edge_attr_e3nn, node_attr_scalar_raw, W_msg_tp, W_msg_lin, W_upd_tp, W_upd_lin, edge_index):
        import jax, jax.numpy as jnp
        import numpy as np
        N_NODES = 6250
        N_EDGES = 200000
        D_NODE = 16
        D_EDGE = 8
        D_HIDDEN = 16
        n_nodes = node_features.shape[0]
        row = edge_index[0]
        col = edge_index[1]
        norm_msg_tp = 1.0 / np.float32(np.sqrt(D_NODE * D_EDGE))
        norm_upd_tp = 1.0 / np.float32(np.sqrt(D_NODE * D_HIDDEN))
        norm_lin = 1.0 / np.float32(np.sqrt(D_HIDDEN))
        x_j = node_features[col]
        m = jnp.einsum('ei,ej,ijh->eh', x_j, edge_attr_e3nn, W_msg_tp) * norm_msg_tp
        m = jax.nn.silu(m)
        m = m @ W_msg_lin * norm_lin
        agg = jax.ops.segment_sum(m, row, num_segments=n_nodes)
        u = jnp.einsum('ni,nh,ihk->nk', node_features, agg, W_upd_tp) * norm_upd_tp
        u = jax.nn.silu(u)
        u = u @ W_upd_lin * norm_lin
        return node_features + u

    def _L3_gnn_ref(x, edge_index, edge_attr, edge_w, edge_b, root_w, root_b, bn_gamma, bn_beta, pred_w, pred_b):
        import jax, jax.numpy as jnp
        import numpy as np
        N_NODES = 3125
        N_EDGES = 25000
        D = 16
        E_FEAT = 8
        N_LAYERS = 3
        BN_EPS = 1e-05

        def _nnconv(x, src, dst, edge_attr, ew, eb, rw, rb):
            W = (edge_attr @ ew + eb).reshape(edge_attr.shape[0], x.shape[1], rw.shape[1])
            xj = x[src]
            msg = jnp.einsum('ei,eio->eo', xj, W)
            agg = jax.ops.segment_sum(msg, dst, num_segments=x.shape[0])
            return agg + x @ rw + rb

        def _batchnorm(x, gamma, beta):
            mean = jnp.mean(x, axis=0)
            var = jnp.mean(jnp.square(x - mean), axis=0)
            return (x - mean) * jax.lax.rsqrt(var + BN_EPS) * gamma + beta
        src, dst = (edge_index[0], edge_index[1])
        h = x
        for i in range(N_LAYERS - 1):
            h = _nnconv(h, src, dst, edge_attr, edge_w[i], edge_b[i], root_w[i], root_b[i])
            h = _batchnorm(h, bn_gamma[i], bn_beta[i])
            h = jax.nn.relu(h)
        h = _nnconv(h, src, dst, edge_attr, edge_w[-1], edge_b[-1], root_w[-1], root_b[-1])
        h = jax.nn.relu(h)
        return h @ pred_w + pred_b
    edge_index = jnp.stack([src, dst])
    x = _layernorm(x + _L0_gnn_ref(x, edge_attr_16, L0_gnn_W_msg, L0_gnn_b_msg, L0_gnn_W_attn, L0_gnn_b_attn, src, dst), axis=-1)
    x = _layernorm(x + _L1_gnn_ref(x, L1_gnn_W1, L1_gnn_root1, L1_gnn_b1, L1_gnn_W2, L1_gnn_root2, L1_gnn_b2, edge_index, edge_type_8), axis=-1)
    x = _layernorm(x + _L2_gnn_ref(x, edge_attr_8, node_vec1, L2_gnn_W_msg_tp, L2_gnn_W_msg_lin, L2_gnn_W_upd_tp, L2_gnn_W_upd_lin, edge_index), axis=-1)
    x = _layernorm(x + _L3_gnn_ref(x, edge_index, edge_attr_8, L3_gnn_edge_w, L3_gnn_edge_b, L3_gnn_root_w, L3_gnn_root_b, L3_gnn_bn_gamma, L3_gnn_bn_beta, L3_gnn_pred_w, L3_gnn_pred_b), axis=-1)
    return x

_drawn_inputs = setup_inputs


def setup_inputs(seed=0):
    import zlib

    import numpy as np

    out = dict(_drawn_inputs(seed))
    spreads = {'L0_gnn_b_msg': (0.0, 0.1),
     'L0_gnn_b_attn': (0.0, 0.1),
     'L1_gnn_b1': (0.0, 0.1),
     'L1_gnn_b2': (0.0, 0.469),
     'L3_gnn_bn_gamma': (1.0, 0.2),
     'L3_gnn_bn_beta': (0.0, 0.1)}
    factors = {'L3_gnn_root_b': 5.091}
    for name, (base, spread) in spreads.items():
        noise = np.random.default_rng([zlib.crc32(name.encode()), seed]).standard_normal(out[name].shape)
        drawn = base * np.exp(spread * noise) if base else spread * noise
        out[name] = jnp.asarray(drawn.astype(out[name].dtype))
    for name, factor in factors.items():
        out[name] = (out[name] * factor).astype(out[name].dtype)
    return out
```

```python
from contextlib import ExitStack

import concourse.bass as bass
from concourse import mybir

F32 = mybir.dt.float32
I32 = mybir.dt.int32
ALU = mybir.AluOpType
ACT = mybir.ActivationFunctionType
X = mybir.AxisListType.X

N, E, D = 6250, 200000, 16
NP, NJ, JT = 6272, 56, 49
CH, T = 125, 1600
C2 = D * D
ROW = 772
TB0, NB0 = 8, 200
TB, NB = 32, 50
BIG = 1e30
SKIP = 1 << 20
A7 = 784
EPS = 1e-5


class Chain:

    def __init__(self, nc, sem):
        self.nc, self.last = nc, None
        self.sems = {e: sem("chain_" + e) for e in ("vector", "scalar", "tensor", "gpsimd", "sync", "rows")}
        self.n = dict.fromkeys(self.sems, 0)
        self.engines = {"vector": nc.vector, "scalar": nc.scalar, "tensor": nc.tensor,
                        "gpsimd": nc.gpsimd, "sync": nc.sync, "rows": nc.gpsimd}

    def wait(self, eng):
        if self.last:
            eng.wait_ge(*self.last)

    def step(self, name, instrs, inc=1):
        eng = self.engines[name]
        self.wait(eng)
        for f in instrs:
            f(eng).then_inc(self.sems[name], inc)
            self.n[name] += inc
        self.last = (self.sems[name], self.n[name])

    def v(self, *fs):
        self.step("vector", fs)

    def a(self, *fs):
        self.step("scalar", fs)

    def t(self, *fs):
        self.step("tensor", fs)

    def g(self, *fs):
        self.step("gpsimd", fs)

    def dma(self, *fs):
        self.step("sync", fs, 16)


def program(nc, io, out):
    ctx = ExitStack()
    with ctx:
        def sem(name):
            return ctx.enter_context(nc.semaphore(name))

        def sb(name, shape, dt=F32, c=ctx):
            return c.enter_context(nc.sbuf_tensor(name, shape, dt))

        def dram(name, shape, dt=F32):
            return nc.dram_tensor(name, shape, dt, kind="Internal").ap()

        table = dram("node_table", (NP, D))
        table2 = dram("node_table2", (NP, 2 * D))
        sums = dram("running_sums", (E + 8, D))
        rows0 = dram("rows0", (NP, ROW))
        flags = dram("edge_flags", (CH, T, 4))
        ends = dram("end_rows", (CH, T), I32)
        aggd = dram("agg_by_source", (8 * A7, D))

        keep = sb("keep", [CH, T + 1])
        dstf = sb("dstf", [CH, T])
        first_of = sb("chunk_first", [CH, 1])
        last_of = sb("chunk_last", [CH, 1])
        ident = sb("ident", [128, 128])
        ones = sb("ones", [128, 128])
        before = sb("chain_mask", [CH, CH])
        cc_row = sb("chain_keep_row", [128, CH])
        patch_row = sb("patch_row", [CH, 1], I32)
        patch_src = sb("patch_src", [CH, 1], I32)
        patch_sum = sb("patch_sum", [CH, 1], I32)
        patch_sum_src = sb("patch_sum_src", [CH, 1], I32)
        end_idx = sb("end_idx", [128, NJ], I32)
        valid = sb("valid", [128, NJ])
        xn = sb("xn", [128, NJ, D])
        hn = sb("hn", [128, NJ, D])
        agg = sb("agg", [128, NJ, D])
        tn = sb("tn", [128, NJ, D])
        red = sb("red", [128, NJ])
        group_mask = sb("group_mask", [128, 8])
        wstage = sb("wstage", [128, D])
        blockdiag = sb("blockdiag", [128, 8, D])
        xT = sb("xT", [128, 7 * 128])
        row_b = sb("row_b", [128, D])
        PS = ctx.enter_context(nc.psum_tensor("PS", [128, 8, 512], F32))
        ch = Chain(nc, sem)
        v, a, t, g, dma = ch.v, ch.a, ch.t, ch.g, ch.dma

        def bc(ap, n, at):
            x = ap.unsqueeze(at)
            shape = list(x.shape)
            shape[at] = n
            return x.to_broadcast(shape)

        def together():
            for eng in (nc.sync, nc.gpsimd, nc.tensor, nc.scalar, nc.vector):
                ch.wait(eng)
            nc.all_engine_barrier()

        setup = ExitStack()
        iop = sb("iop", [128, 1], F32, setup)
        iorow = sb("iorow", [128, CH], F32, setup)
        tri = sb("tri", [CH, CH], F32, setup)
        v(lambda e: e.memset(ones[:, :], 1.0), lambda e: e.memset(ident[:, :], 0.0),
          lambda e: e.memset(xn[:, :, :], 0.0), lambda e: e.memset(valid[:, :], 1.0),
          lambda e: e.memset(group_mask[:, :], 1.0), lambda e: e.memset(agg[:, :, :], 0.0),
          lambda e: e.memset(end_idx[:, :], 0), lambda e: e.memset(hn[:, :, :], 0.0))
        g(lambda e: e.affine_select(out=ident[:, :], in_=ident[:, :], compare_op=ALU.not_equal, fill=1.0,
                                    base=0, pattern=[[-1, 128]], channel_multiplier=1),
          lambda e: e.affine_select(out=valid[:, :], in_=valid[:, :], compare_op=ALU.is_ge, fill=0.0,
                                    base=N - 1, pattern=[[-128, NJ]], channel_multiplier=-1),
          lambda e: e.affine_select(out=group_mask[:, :], in_=group_mask[:, :], compare_op=ALU.is_ge, fill=0.0,
                                    base=0, pattern=[[-16, 8]], channel_multiplier=1),
          lambda e: e.iota(iop[:, :], pattern=[[0, 1]], base=0, channel_multiplier=1,
                           allow_small_or_imprecise_dtypes=True),
          lambda e: e.iota(iorow[:, :], pattern=[[1, CH]], base=0, channel_multiplier=0,
                           allow_small_or_imprecise_dtypes=True))
        g(lambda e: e.affine_select(out=group_mask[:, :], in_=group_mask[:, :], compare_op=ALU.is_ge, fill=0.0,
                                    base=15, pattern=[[16, 8]], channel_multiplier=-1))
        v(lambda e: e.tensor_scalar(tri[:, :], iorow[0:CH, :], iop[0:CH, 0:1], None, ALU.is_gt))

        dsti = sb("dsti", [CH, T], I32, setup)
        nbi = sb("nbi", [CH, 2], I32, setup)
        nb = sb("nb", [CH, 2], F32, setup)
        fl = sb("fl", [CH, T, 4], F32, setup)
        st = sb("st", [CH, T + 1], F32, setup)
        sidx = sb("sidx", [CH, T], I32, setup)
        tmp = sb("tmp", [CH, T], F32, setup)
        small = sb("small", [CH, 12], F32, setup)
        diag = sb("diag", [CH, CH], F32, setup)
        frow = sb("frow", [CH, CH], F32, setup)
        dst_c = io["dst"].rearrange("(p t) -> p t", p=CH)
        v(lambda e: e.memset(nbi[:, :], -1))
        with nc.allow_non_contiguous_dma(reason="one word per chunk"):
            dma(lambda e: e.dma_start(dsti[:, :], dst_c),
                lambda e: e.dma_start(nbi[1:CH, 0:1], dst_c[0:CH - 1, T - 1:T]),
                lambda e: e.dma_start(nbi[0:CH - 1, 1:2], dst_c[1:CH, 0:1]),
                lambda e: e.dma_start(xn[:, 0:48, :], io["x"][0:6144, :].rearrange("(j p) f -> p j f", p=128)),
                lambda e: e.dma_start(xn[0:N - 6144, 48, :], io["x"][6144:N, :]))
        v(lambda e: e.tensor_copy(dstf[:, :], dsti[:, :]), lambda e: e.tensor_copy(nb[:, :], nbi[:, :]),
          lambda e: e.memset(st[:, 0:1], 1.0))
        s = lambda k: small[:, k:k + 1]
        FIRST, LAST, CONT, CHIN, SAME, OK, EF, CCK, LEN, T0, T1 = range(11)
        v(lambda e: e.tensor_tensor(st[:, 1:T], dstf[:, 1:T], dstf[:, 0:T - 1], ALU.not_equal),
          lambda e: e.tensor_copy(first_of[:, :], dstf[:, 0:1]),
          lambda e: e.tensor_copy(last_of[:, :], dstf[:, T - 1:T]))
        v(lambda e: e.tensor_tensor(s(CONT), nb[:, 1:2], last_of[:, :], ALU.is_equal),
          lambda e: e.tensor_tensor(s(CHIN), nb[:, 0:1], first_of[:, :], ALU.is_equal),
          lambda e: e.tensor_tensor(s(SAME), first_of[:, :], last_of[:, :], ALU.is_equal),
          lambda e: e.tensor_tensor(st[:, T:T + 1], nb[:, 1:2], last_of[:, :], ALU.not_equal),
          lambda e: e.tensor_scalar(tmp[:, :], dstf[:, :], first_of[:, 0:1], None, ALU.is_equal))
        v(lambda e: e.tensor_reduce(s(LEN), tmp[:, :], X, ALU.add),
          lambda e: e.tensor_tensor(s(T0), s(SAME), s(CONT), ALU.mult),
          lambda e: e.tensor_tensor(s(CCK), s(SAME), s(CHIN), ALU.mult),
          lambda e: e.tensor_scalar(keep[:, 0:T], st[:, 0:T], -1.0, 1.0, ALU.mult, ALU.add),
          lambda e: e.memset(keep[:, T:T + 1], 0.0),
          lambda e: e.tensor_scalar(fl[:, :, 0], st[:, 0:T], -BIG, None, ALU.mult),
          lambda e: e.tensor_scalar(fl[:, :, 2], st[:, 1:T + 1], -BIG, None, ALU.mult))
        v(lambda e: e.tensor_scalar(s(T0), s(T0), -1.0, 1.0, ALU.mult, ALU.add),
          lambda e: e.tensor_copy(fl[:, :, 1], keep[:, 0:T]))
        v(lambda e: e.tensor_tensor(s(OK), s(CHIN), s(T0), ALU.mult),
          lambda e: e.tensor_scalar(s(EF), iop[0:CH, :], float(T), -1.0, ALU.mult, ALU.add),
          lambda e: e.tensor_scalar(tmp[:, :], dstf[:, :], float(-SKIP), None, ALU.add))
        v(lambda e: e.tensor_tensor(s(EF), s(EF), s(LEN), ALU.add),
          lambda e: e.tensor_tensor(tmp[:, :], tmp[:, :], st[:, 1:T + 1], ALU.mult),
          lambda e: e.tensor_scalar(s(T0), first_of[:, :], float(-SKIP), None, ALU.add))
        v(lambda e: e.tensor_scalar(s(T1), s(EF), float(-SKIP), None, ALU.add),
          lambda e: e.tensor_tensor(s(T0), s(T0), s(OK), ALU.mult),
          lambda e: e.tensor_scalar(sidx[:, :], tmp[:, :], float(SKIP), None, ALU.add),
          lambda e: e.tensor_copy(patch_sum_src[:, :], s(EF)),
          lambda e: e.tensor_copy(patch_src[:, :], first_of[:, :]))
        v(lambda e: e.tensor_tensor(s(T1), s(T1), s(OK), ALU.mult),
          lambda e: e.tensor_scalar(patch_row[:, :], s(T0), float(SKIP), None, ALU.add))
        v(lambda e: e.tensor_scalar(patch_sum[:, :], s(T1), float(SKIP), None, ALU.add),
          lambda e: e.tensor_scalar(diag[:, :], ident[0:CH, 0:CH], first_of[:, 0:1], None, ALU.mult))
        g(lambda e: e.iota(fl[:, :, 3], pattern=[[1, T]], base=0, channel_multiplier=T,
                           allow_small_or_imprecise_dtypes=True))

        def over_partitions(dst_ap, rows):
            t(lambda e: e.matmul(PS[0:rows, 0, 0:CH], ones[0:CH, 0:rows], diag[:, :]))
            v(lambda e: e.tensor_copy(dst_ap, PS[0:rows, 0, 0:CH]))

        over_partitions(frow[:, :], CH)
        v(lambda e: e.tensor_scalar(diag[:, :], ident[0:CH, 0:CH], s(CCK), None, ALU.mult))
        over_partitions(cc_row[:, :], 128)
        v(lambda e: e.tensor_scalar(before[:, :], frow[:, :], last_of[:, 0:1], None, ALU.is_equal))
        v(lambda e: e.tensor_tensor(before[:, :], before[:, :], tri[:, :], ALU.mult))

        initrow = sb("initrow", [128, 7, ROW], F32, setup)
        zrow = sb("zrow", [1, 8 * D], F32, setup)
        v(lambda e: e.memset(initrow[:, :, :], 0.0), lambda e: e.memset(zrow[:, :], 0.0))
        v(lambda e: e.memset(initrow[:, :, C2:2 * C2], 1.0), lambda e: e.memset(initrow[:, :, 3 * C2:], float(E)))
        rows0_j = rows0.rearrange("(j p) c -> p j c", p=128)
        dma(*[lambda e, k=k: e.dma_start(rows0_j[:, 7 * k:7 * k + 7, :], initrow[:, :, :]) for k in range(7)],
            lambda e: e.dma_start(flags, fl[:, :, :]),
            lambda e: e.dma_start(ends, sidx[:, :]),
            lambda e: e.dma_start(sums[E:E + 8, :].rearrange("(a e) f -> a (e f)", a=1), zrow[:, :]))
        together()
        setup.close()

        L = ExitStack()
        lsem = lambda n: L.enter_context(nc.semaphore(n))
        two = range(2)
        waug = sb("waug", [128, 2 * C2], F32, L)
        idx = [sb(f"idx{k}", [CH, TB0], I32, L) for k in two]
        sid = [sb(f"sid{k}", [CH, TB0], I32, L) for k in two]
        flb = [sb(f"flb{k}", [CH, TB0, 4], F32, L) for k in two]
        ef = [sb(f"ef{k}", [CH, TB0, 32], F32, L) for k in two]
        h = [sb(f"h{k}", [CH, TB0, D], F32, L) for k in two]
        efT = [sb(f"efT{k}", [128, 128], F32, L) for k in two]
        e2 = [sb(f"e2{k}", [CH, TB0, C2], F32, L) for k in two]
        M = [sb(f"M{k}", [CH, TB0, C2], F32, L) for k in two]
        PX = [sb(f"PX{k}", [CH, TB0, 2 * C2], F32, L) for k in two]
        ST = [sb(f"ST{k}", [CH, TB0, ROW], F32, L) for k in two]
        cf = [sb(f"cf{k}", [CH, C2], F32, L) for k in two]
        v(lambda e: e.memset(waug[:, :], 0.0), lambda e: e.memset(M[1][:, :, :], 0.0),
          lambda e: e.memset(ST[0][:, :, :], 0.0), lambda e: e.memset(ST[1][:, :, :], 0.0),
          *[lambda e, k=k: e.memset(ef[k][:, :, :], 0.0) for k in two])
        v(*[lambda e, k=k: e.memset(ef[k][:, :, D:D + 1], 1.0) for k in two])
        dma(*[lambda e, q=q, o=o, w=w: e.dma_start(waug[32 * q:32 * q + D, o:o + C2], io[w])
              for q in range(4) for o, w in ((0, "L0_gnn_W_attn"), (C2, "L0_gnn_W_msg"))],
            *[lambda e, q=q, o=o, w=w: e.dma_start(waug[32 * q + D:32 * q + D + 1, o:o + C2],
                                                   io[w].rearrange("(a n) -> a n", a=1))
              for q in range(4) for o, w in ((0, "L0_gnn_b_attn"), (C2, "L0_gnn_b_msg"))])
        together()

        l_in = [lsem(f"l_in{k}") for k in two]
        l_fl = [lsem(f"l_fl{k}") for k in two]
        l_si = [lsem(f"l_si{k}") for k in two]
        l_g = [lsem(f"l_g{k}") for k in two]
        l_tr, l_et, l_mm, l_use = lsem("l_tr"), lsem("l_et"), lsem("l_mm"), lsem("l_use")
        l_e2, l_fw, l_bw, l_a = lsem("l_e2"), lsem("l_fw"), lsem("l_bw"), lsem("l_a")
        l_ex, l_mc, l_p, l_q, l_s = lsem("l_ex"), lsem("l_mc"), lsem("l_p"), lsem("l_q"), lsem("l_s")
        l_sc = [lsem(f"l_sc{k}") for k in two]
        src_c = io["src"].rearrange("(p t) -> p t", p=CH)
        ea16 = io["edge_attr_16"].rearrange("(p t) f -> p t f", p=CH)

        def sp_load(dst, src, sm):
            nc.sync.dma_start(dst, src).then_inc(sm, 16)

        class Blk:

            def __init__(self, i, k, n, tb):
                while not isinstance(i, int) and k > 1 or k < 0:
                    i, k = (i + 1, k - 2) if k > 1 else (i - 1, k + 2)
                if isinstance(i, int):
                    i, k = (2 * i + k) // 2, k % 2
                self.i, self.k, self.n, self.tb = i, k, n, tb

            def exists(self):
                return not isinstance(self.i, int) or 0 <= 2 * self.i + self.k < self.n

            def next(self, d):
                return Blk(self.i, self.k + d, self.n, self.tb)

            def count(self, per, more):
                return self.i * (2 * per) + (self.k * per + more)

            def slot(self, per, more):
                return self.i * per + more

            def cols(self):
                return bass.ds(self.i * (2 * self.tb) + self.k * self.tb, self.tb)

        def wait(e, sm, val):
            if not isinstance(val, int) or val > 0:
                e.wait_ge(sm, val)
                if e in (nc.sync, nc.gpsimd):
                    e.nop(nofuse=True)

        def loop(eng, body, n, tb, before=None, after=None):
            if before:
                before(Blk(0, 0, n, tb))
            for k in two:
                body(Blk(0, k, n, tb))
            with eng.Fori(1, n // 2 - 1) as i:
                for k in two:
                    body(Blk(i, k, n, tb))
            for k in two:
                body(Blk(n // 2 - 1, k, n, tb))
            if after:
                after(Blk(n // 2 - 1, 1, n, tb))

        e = nc.sync

        def load_in(b):
            wait(nc.sync, l_g[b.k], b.slot(16 * TB0, 0))
            wait(nc.sync, l_tr, b.next(-2).count(2, 2))
            sp_load(idx[b.k][:, :], src_c[:, b.cols()], l_in[b.k])
            sp_load(ef[b.k][:, :, 0:D], ea16[:, b.cols(), :], l_in[b.k])

        def load_fl(b):
            wait(nc.sync, l_s, b.next(-1).count(TB0, 0))
            wait(nc.sync, l_mc, b.next(-1).count(2, 0))
            sp_load(flb[b.k][:, :, :], flags[:, b.cols(), :], l_fl[b.k])

        def load_si(b):
            wait(nc.sync, l_sc[b.k], b.slot(16 * TB0, 0))
            sp_load(sid[b.k][:, :], ends[:, b.cols()], l_si[b.k])

        def sp_body(b):
            if b.next(1).exists():
                load_in(b.next(1))
            load_fl(b)
            if b.next(-1).exists():
                load_si(b.next(-1))

        loop(nc.sync, sp_body, NB0, TB0, before=load_in, after=load_si)

        lim0 = nc.gpsimd.to_reg(NP - 1)

        def gather0(b):
            wait(nc.gpsimd, l_in[b.k], b.slot(32, 32))
            wait(nc.gpsimd, l_use, b.next(-1).count(2, 0))
            for q in range(TB0):
                nc.gpsimd.indirect_dma_start(h[b.k][:, q, :], None, io["x"],
                                             bass.IndirectOffsetOnAxis(ap=idx[b.k][:, q:q + 1], axis=0))\
                    .then_inc(l_g[b.k], 16)

        def scatter0(b):
            wait(nc.gpsimd, l_s, b.count(TB0, TB0))
            wait(nc.gpsimd, l_mc, b.count(2, 2))
            wait(nc.gpsimd, l_si[b.k], b.slot(16, 16))
            for q in range(TB0):
                nc.gpsimd.indirect_dma_start(rows0, bass.IndirectOffsetOnAxis(ap=sid[b.k][:, q:q + 1], axis=0),
                                             ST[b.k][:, q, :], None, bounds_check=lim0, oob_is_err=False)\
                    .then_inc(l_sc[b.k], 16)

        def pool_body(b):
            if b.next(1).exists():
                gather0(b.next(1))
            if b.next(-1).exists():
                scatter0(b.next(-1))

        loop(nc.gpsimd, pool_body, NB0, TB0, before=gather0, after=scatter0)

        def turn(b):
            for q in two:
                wait(nc.tensor, l_in[b.k], b.slot(32, 32))
                wait(nc.tensor, l_et, b.next(-1).count(2, q + 1))
                nc.tensor.transpose(PS[:, 4 + q, 0:CH], ef[b.k][:, 4 * q:4 * q + 4, :].rearrange("p a c -> p (a c)"),
                                    ident[0:CH, 0:CH]).then_inc(l_tr, 1)

        def weigh(b):
            for q in two:
                wait(nc.tensor, l_et, b.count(2, q + 1))
                wait(nc.tensor, l_use, b.count(2, q))
                for r in range(4):
                    mm = nc.tensor.matmul(PS[0:CH, r, :], efT[q][32 * r:32 * r + D + 1, 0:CH],
                                          waug[32 * r:32 * r + D + 1, :])
                mm.then_inc(l_mm, 1)

        def pe_body(b):
            weigh(b)
            if b.next(1).exists():
                turn(b.next(1))

        loop(nc.tensor, pe_body, NB0, TB0, before=turn)

        def copy_turned(b):
            for q in two:
                wait(nc.scalar, l_tr, b.count(2, q + 1))
                wait(nc.scalar, l_mm, b.next(-1).count(2, q + 1))
                nc.scalar.activation(efT[q][:, 0:CH], PS[:, 4 + q, 0:CH], ACT.Copy).then_inc(l_et, 1)

        def act_body(b):
            if b.next(1).exists():
                copy_turned(b.next(1))
            wait(nc.scalar, l_a, b.count(2, 2))
            nc.scalar.activation(cf[b.k][:, :], cf[b.k][:, :], ACT.Exp).then_inc(l_ex, 1)
            nc.scalar.activation(PX[b.k][:, :, 0:C2], e2[b.k][:, :, :], ACT.Exp).then_inc(l_ex, 1)
            wait(nc.scalar, l_sc[b.k], b.slot(16 * TB0, 0))
            nc.scalar.activation(ST[b.k][:, :, 0:C2], M[b.k][:, :, :], ACT.Copy).then_inc(l_mc, 1)
            nc.scalar.activation(ST[b.k][:, :, 3 * C2:3 * C2 + 1], flb[b.k][:, :, 3:4], ACT.Copy).then_inc(l_mc, 1)

        loop(nc.scalar, act_body, NB0, TB0, before=copy_turned)

        V = nc.vector

        def products(b, q):
            s4 = slice(4 * q, 4 * q + 4)
            hb = bc(h[b.k][:, s4, :], D, 3)
            if q == 0:
                wait(V, l_g[b.k], b.slot(16 * TB0, 16 * TB0))
                wait(V, l_ex, b.next(-2).count(2, 2))
                wait(V, l_p, b.next(-2).count(1, 1))
                wait(V, l_s, b.next(-2).count(TB0, TB0))
            wait(V, l_mm, b.count(2, q + 1))
            V.tensor_tensor(e2[b.k][:, s4, :].rearrange("p t (i o) -> p t i o", i=D),
                            PS[0:CH, 0:4, 0:C2].rearrange("p t (i o) -> p t i o", i=D), hb, ALU.mult).then_inc(l_e2, 1)
            V.tensor_tensor(PX[b.k][:, s4, C2:].rearrange("p t (i o) -> p t i o", i=D),
                            PS[0:CH, 0:4, C2:].rearrange("p t (i o) -> p t i o", i=D), hb, ALU.mult).then_inc(l_use, 1)

        def maxima(b):
            wait(V, l_fl[b.k], b.slot(16, 16))
            wait(V, l_e2, b.count(2, 2))
            wait(V, l_mc, b.next(-1).count(2, 0))
            for q in range(TB0):
                wait(V, l_fw, b.count(TB0, q))
                prev = M[b.k][:, q - 1, :] if q else M[1 - b.k][:, TB0 - 1, :]
                V.scalar_tensor_tensor(out=M[b.k][:, q, :], in0=prev, scalar=flb[b.k][:, q, 0:1],
                                       in1=e2[b.k][:, q, :], op0=ALU.add, op1=ALU.max).then_inc(l_fw, 1)
            wait(V, l_fw, b.count(TB0, TB0))
            for n, q in enumerate(range(TB0 - 2, -1, -1)):
                wait(V, l_bw, b.count(TB0 - 1, n))
                V.scalar_tensor_tensor(out=M[b.k][:, q, :], in0=M[b.k][:, q + 1, :], scalar=flb[b.k][:, q, 2:3],
                                       in1=M[b.k][:, q, :], op0=ALU.add, op1=ALU.max).then_inc(l_bw, 1)
            wait(V, l_bw, b.count(TB0 - 1, TB0 - 1))
            wait(V, l_q, b.next(-1).count(1, 0))
            V.tensor_tensor(e2[b.k][:, :, :], e2[b.k][:, :, :], M[b.k][:, :, :], ALU.subtract).then_inc(l_a, 1)
            V.scalar_tensor_tensor(out=cf[b.k][:, :], in0=M[1 - b.k][:, TB0 - 1, :], scalar=flb[b.k][:, 0, 0:1],
                                   in1=M[b.k][:, 0, :], op0=ALU.add, op1=ALU.subtract).then_inc(l_a, 1)

        def sums0(b):
            S, P = ST[b.k], PX[b.k]
            wait(V, l_ex, b.count(2, 2))
            wait(V, l_sc[b.k], b.slot(16 * TB0, 0))
            V.tensor_tensor(P[:, :, C2:], P[:, :, C2:], P[:, :, 0:C2], ALU.mult).then_inc(l_p, 1)
            wait(V, l_s, b.count(TB0, 0))
            V.tensor_tensor(S[:, 0, C2:3 * C2].rearrange("p (a c) -> p a c", a=2),
                            ST[1 - b.k][:, TB0 - 1, C2:3 * C2].rearrange("p (a c) -> p a c", a=2),
                            bc(cf[b.k][:, :], 2, 1), ALU.mult).then_inc(l_q, 1)
            wait(V, l_p, b.count(1, 1))
            wait(V, l_q, b.count(1, 1))
            V.tensor_tensor(S[:, 0, C2:3 * C2], S[:, 0, C2:3 * C2], P[:, 0, :], ALU.add).then_inc(l_s, 1)
            for q in range(1, TB0):
                wait(V, l_s, b.count(TB0, q))
                V.scalar_tensor_tensor(out=S[:, q, C2:3 * C2], in0=S[:, q - 1, C2:3 * C2],
                                       scalar=flb[b.k][:, q, 1:2], in1=P[:, q, :],
                                       op0=ALU.mult, op1=ALU.add).then_inc(l_s, 1)

        def dve_body(b):
            products(b, 0)
            if b.next(-1).exists():
                sums0(b.next(-1))
            products(b, 1)
            maxima(b)

        loop(V, dve_body, NB0, TB0, after=sums0)
        for k in two:
            for eng in (nc.gpsimd, nc.sync):
                eng.wait_ge(l_sc[k], 16 * TB0 * NB0 // 2)
        together()

        CI = PX[0]
        lastrow = ST[1][:, TB0 - 1, :]
        mT = [sb(f"mT{k}", [128, 3, CH + 1], F32, L) for k in two]
        w1 = sb("w1", [128, CH], F32, L)
        w2 = sb("w2", [128, CH], F32, L)
        rsc = sb("rsc", [128, CH], F32, L)
        inT = sb("inT", [128, 3, CH], F32, L)
        carry = sb("carry", [CH, 3 * C2], F32, L)
        got = sb("got", [CH, ROW], F32, L)
        mt = sb("mt", [CH, C2], F32, L)
        ea = sb("ea", [CH, 2, C2], F32, L)
        v(lambda e: e.tensor_scalar(rsc[:, :], cc_row[:, :], BIG, -BIG, ALU.mult, ALU.add),
          *[lambda e, k=k: e.memset(mT[k][:, :, :], 0.0) for k in two])
        for k in two:
            t(*[lambda e, c=c: e.transpose(PS[:, c, 0:CH], lastrow[:, c * C2 + 128 * k:c * C2 + 128 * k + 128],
                                           ident[0:CH, 0:CH]) for c in range(3)])
            v(lambda e: e.tensor_copy(inT[:, :, :], PS[:, 0:3, 0:CH]))
            v(lambda e: e.tensor_tensor_scan(mT[k][:, 0, 1:], rsc[:, :], inT[:, 0, :], 0.0, ALU.add, ALU.max))
            v(lambda e: e.tensor_tensor(w1[:, :], inT[:, 0, :], mT[k][:, 0, 1:], ALU.subtract),
              lambda e: e.tensor_tensor(w2[:, :], mT[k][:, 0, 0:CH], rsc[:, :], ALU.add))
            v(lambda e: e.tensor_tensor(w2[:, :], w2[:, :], mT[k][:, 0, 1:], ALU.subtract))
            a(lambda e: e.activation(w1[:, :], w1[:, :], ACT.Exp), lambda e: e.activation(w2[:, :], w2[:, :], ACT.Exp))
            v(lambda e: e.tensor_tensor(inT[:, 1:3, :], inT[:, 1:3, :], bc(w1[:, :], 2, 1), ALU.mult))
            v(*[lambda e, c=c: e.tensor_tensor_scan(mT[k][:, c, 1:], w2[:, :], inT[:, c, :], 0.0, ALU.mult, ALU.add)
                for c in (1, 2)])
            t(*[lambda e, c=c: e.transpose(PS[0:CH, 4 + c, 0:128], mT[k][:, c, 0:CH], ident[:, :]) for c in range(3)])
            v(lambda e: e.tensor_copy(carry[:, :].rearrange("p (c h n) -> p c h n", c=3, h=2)[:, :, k, :],
                                      PS[0:CH, 4:7, 0:128]))
        ch.step("rows", [lambda e: e.indirect_dma_start(got[:, :], None, rows0,
                                                          bass.IndirectOffsetOnAxis(ap=patch_src[:, 0:1], axis=0))], 16)
        v(lambda e: e.tensor_tensor(mt[:, :], got[:, 0:C2], carry[:, 0:C2], ALU.max))
        v(lambda e: e.tensor_tensor(ea[:, 0, :], got[:, 0:C2], mt[:, :], ALU.subtract),
          lambda e: e.tensor_tensor(ea[:, 1, :], carry[:, 0:C2], mt[:, :], ALU.subtract))
        a(lambda e: e.activation(ea[:, :, :], ea[:, :, :], ACT.Exp))
        two_of = lambda ap: ap.rearrange("p (a c) -> p a c", a=2)
        v(lambda e: e.tensor_tensor(two_of(got[:, C2:3 * C2]), two_of(got[:, C2:3 * C2]), bc(ea[:, 0, :], 2, 1), ALU.mult),
          lambda e: e.tensor_tensor(two_of(carry[:, C2:]), two_of(carry[:, C2:]), bc(ea[:, 1, :], 2, 1), ALU.mult))
        v(lambda e: e.tensor_tensor(got[:, C2:3 * C2], got[:, C2:3 * C2], carry[:, C2:], ALU.add),
          lambda e: e.tensor_copy(got[:, 0:C2], mt[:, :]))
        ch.wait(nc.gpsimd)
        nc.gpsimd.nop(nofuse=True)
        ch.step("rows", [lambda e: e.indirect_dma_start(rows0, bass.IndirectOffsetOnAxis(ap=patch_row[:, 0:1], axis=0),
                                                          got[:, :], None, bounds_check=lim0, oob_is_err=False)], 16)
        together()
        L.close()

        L = ExitStack()
        rb = sb("rb", [128, 7, ROW], F32, L)
        for k in range(7):
            js = slice(7 * k, 7 * k + 7)
            dma(lambda e: e.dma_start(rb[:, :, :], rows0_j[:, js, :]))
            v(lambda e: e.reciprocal(rb[:, :, C2:2 * C2], rb[:, :, C2:2 * C2]),
              lambda e: e.tensor_copy(end_idx[:, js], rb[:, :, 3 * C2]))
            v(lambda e: e.tensor_tensor(rb[:, :, C2:2 * C2], rb[:, :, C2:2 * C2], rb[:, :, 2 * C2:3 * C2], ALU.mult))
            v(lambda e: e.tensor_reduce(agg[:, js, :], rb[:, :, C2:2 * C2].rearrange("p j (i o) -> p j o i", i=D),
                                        X, ALU.add))
        L.close()

        def flat(ap):
            return ap.rearrange("p j f -> p (j f)")

        def add_to(dst, src):
            v(lambda e: e.tensor_tensor(flat(dst[:, :, :]), flat(dst[:, :, :]), flat(src[:, :, :]), ALU.add))

        def layernorm(x, y):
            add_to(x, y)
            v(lambda e: e.tensor_reduce(red[:, :], x[:, :, :], X, ALU.add))
            v(lambda e: e.tensor_scalar(red[:, :], red[:, :], 1.0 / D, None, ALU.mult))
            v(lambda e: e.tensor_tensor(x[:, :, :], x[:, :, :], bc(red[:, :], D, 2), ALU.subtract))
            v(lambda e: e.tensor_tensor(tn[:, :, :], x[:, :, :], x[:, :, :], ALU.mult))
            v(lambda e: e.tensor_reduce(red[:, :], tn[:, :, :], X, ALU.add))
            v(lambda e: e.tensor_scalar(red[:, :], red[:, :], 1.0 / D, EPS, ALU.mult, ALU.add))
            a(lambda e: e.activation(red[:, :], red[:, :], ACT.Sqrt))
            v(lambda e: e.reciprocal(red[:, :], red[:, :]))
            v(lambda e: e.tensor_tensor(x[:, :, :], x[:, :, :], bc(red[:, :], D, 2), ALU.mult))

        def turned(x):
            t(*[lambda e, k=k: e.transpose(PS[:, k // 4, 128 * (k % 4):128 * (k % 4) + 128],
                                           flat(x[:, 8 * k:8 * k + 8, :]), ident[:, :]) for k in range(7)])
            v(lambda e: e.tensor_copy(xT[:, :], PS[:, 0:2, :].rearrange("p b c -> p (b c)")[:, 0:896]))

        def times(w):
            dma(*[lambda e, q=q: e.dma_start(wstage[D * q:D * q + D, :], w) for q in range(8)])
            v(lambda e: e.tensor_tensor(blockdiag[:, :, :], bc(wstage[:, :], 8, 1), bc(group_mask[:, :], D, 2), ALU.mult))
            t(*[lambda e, k=k: e.matmul(PS[:, 2 + k // 4, 128 * (k % 4):128 * (k % 4) + 128],
                                        xT[:, 128 * k:128 * k + 128], blockdiag[:, :, :].rearrange("p g o -> p (g o)"))
                for k in range(7)])
            return PS[:, 2:4, :].rearrange("p b c -> p (b c)")[:, 0:896]

        def row_of(w):
            dma(lambda e: e.dma_start(row_b[:, :], w.rearrange("(a n) -> a n", a=1).to_broadcast([128, D])))
            return bc(row_b[:, :], NJ, 1)

        def put_table(tab, x, at=0):
            dma(lambda e: e.dma_start(tab.rearrange("(j p) f -> p j f", p=128)[:, :, at:at + D], x[:, 0:JT, :]))

        layernorm(xn, agg)

        coef_sb = sb("coef", [CH, T, 8])
        L = ExitStack()
        tyi = sb("tyi", [CH, T], I32, L)
        ty = sb("ty", [CH, T], F32, L)
        isf = sb("isf", [CH, T], F32, L)
        isl = sb("isl", [CH, T], F32, L)
        cnt = sb("cnt", [CH, T], F32, L)
        lastp = sb("lastp", [CH, 8], F32, L)
        firstp = sb("firstp", [CH, 8], F32, L)
        more = sb("more", [CH, 2, 8], F32, L)
        q_ = [sb(f"q{k}", [CH, CH], F32, L) for k in range(4)]
        lt = sb("lt", [CH, CH], F32, L)
        gt = sb("gt", [CH, CH], F32, L)
        fr = sb("fr", [CH, CH], F32, L)
        lr = sb("lr", [CH, CH], F32, L)
        dg = sb("dg", [CH, CH], F32, L)
        v(lambda e: e.memset(lt[:, :], 1.0), lambda e: e.memset(gt[:, :], 1.0))
        g(lambda e: e.affine_select(out=lt[:, :], in_=lt[:, :], compare_op=ALU.is_gt, fill=0.0,
                                    base=0, pattern=[[1, CH]], channel_multiplier=-1),
          lambda e: e.affine_select(out=gt[:, :], in_=gt[:, :], compare_op=ALU.is_gt, fill=0.0,
                                    base=0, pattern=[[-1, CH]], channel_multiplier=1))
        dma(lambda e: e.dma_start(tyi[:, :], io["edge_type_8"].rearrange("(p t) -> p t", p=CH)))
        for src_, dst_ in ((first_of, fr), (last_of, lr)):
            v(lambda e: e.tensor_scalar(dg[:, :], ident[0:CH, 0:CH], src_[:, 0:1], None, ALU.mult))
            t(lambda e: e.matmul(PS[0:CH, 0, 0:CH], ones[0:CH, 0:CH], dg[:, :]))
            v(lambda e: e.tensor_copy(dst_[:, :], PS[0:CH, 0, 0:CH]))
        spec = [(fr, last_of, lt), (fr, first_of, gt), (lr, last_of, lt), (lr, first_of, gt)]
        v(*[lambda e, k=k: e.tensor_scalar(q_[k][:, :], spec[k][0][:, :], spec[k][1][:, 0:1], None, ALU.is_equal)
            for k in range(4)], lambda e: e.tensor_copy(ty[:, :], tyi[:, :]),
          lambda e: e.tensor_scalar(isf[:, :], dstf[:, :], first_of[:, 0:1], None, ALU.is_equal),
          lambda e: e.tensor_scalar(isl[:, :], dstf[:, :], last_of[:, 0:1], None, ALU.is_equal))
        v(*[lambda e, k=k: e.tensor_tensor(q_[k][:, :], q_[k][:, :], spec[k][2][:, :], ALU.mult) for k in range(4)],
          lambda e: e.tensor_tensor(isl[:, :], isl[:, :], isf[:, :], ALU.is_gt))
        for r in range(8):
            cr = coef_sb[:, :, r]
            v(lambda e: e.tensor_scalar(cnt[:, :], ty[:, :], float(r), None, ALU.is_equal))
            v(lambda e: e.tensor_tensor_scan(cnt[:, :], keep[:, 0:T], cnt[:, :], 0.0, ALU.mult, ALU.add))
            v(lambda e: e.tensor_copy(lastp[:, r:r + 1], cnt[:, T - 1:T]),
              lambda e: e.tensor_tensor_scan(cr[:, ::-1], keep[:, 1:T + 1][:, ::-1], cnt[:, ::-1], 0.0, ALU.mult, ALU.max))
            v(lambda e: e.tensor_copy(firstp[:, r:r + 1], cr[:, 0:1]))
        t(lambda e: e.matmul(PS[0:CH, 0, 0:8], q_[0][:, :], lastp[:, :], start=True, stop=False),
          lambda e: e.matmul(PS[0:CH, 1, 0:8], q_[2][:, :], lastp[:, :], start=True, stop=False))
        t(lambda e: e.matmul(PS[0:CH, 0, 0:8], q_[1][:, :], firstp[:, :], start=False, stop=True),
          lambda e: e.matmul(PS[0:CH, 1, 0:8], q_[3][:, :], firstp[:, :], start=False, stop=True))
        v(lambda e: e.tensor_copy(more[:, :, :], PS[0:CH, 0:2, 0:8]))
        for r in range(8):
            cr = coef_sb[:, :, r]
            v(lambda e: e.scalar_tensor_tensor(out=cr, in0=isf[:, :], scalar=more[:, 0, r:r + 1], in1=cr,
                                               op0=ALU.mult, op1=ALU.add))
            v(lambda e: e.scalar_tensor_tensor(out=cr, in0=isl[:, :], scalar=more[:, 1, r:r + 1], in1=cr,
                                               op0=ALU.mult, op1=ALU.add))
            v(lambda e: e.tensor_scalar(cnt[:, :], cr, 1.0, None, ALU.max))
            v(lambda e: e.reciprocal(cnt[:, :], cnt[:, :]))
            v(lambda e: e.scalar_tensor_tensor(out=cr, in0=ty[:, :], scalar=float(r), in1=cnt[:, :],
                                               op0=ALU.is_equal, op1=ALU.mult))
        together()
        L.close()

        wc = sb("wc", [128, D])
        patch_g = sb("patch_g", [CH, D])
        lim_s = nc.gpsimd.to_reg(E - 1)

        def conv(name, tab, width, index, by_source=None):
            L = ExitStack()
            lsem = lambda n: L.enter_context(nc.semaphore(f"{name}_{n}"))
            ix = [sb(f"{name}ix{k}", [CH, TB], I32, L) for k in two]
            gt_ = [sb(f"{name}g{k}", [CH, TB, width], F32, L) for k in two]
            z = [sb(f"{name}z{k}", [CH, 4, 128], F32, L) for k in two]
            zt = [sb(f"{name}zt{k}", [128, 4 * CH], F32, L) for k in two]
            ms = sb(f"{name}ms", [CH, TB, D], F32, L)
            run = [sb(f"{name}run{k}", [CH, TB, D], F32, L) for k in two]
            c_ix = [lsem(f"ix{k}") for k in two]
            c_g = [lsem(f"g{k}") for k in two]
            c_st = [lsem(f"st{k}") for k in two]
            c_z, c_tr, c_zt, c_mm = lsem("z"), lsem("tr"), lsem("zt"), lsem("mm")
            c_ms, c_run = lsem("ms"), lsem("run")
            G = TB // 4
            index_c = index.rearrange("(p t) -> p t", p=CH)
            sums_c = sums[0:E, :].rearrange("(p t) f -> p t f", p=CH)
            if by_source is None:
                v(*[lambda e, k=k: e.memset(run[k][:, :, :], 0.0) for k in two])
            else:
                av, bv = by_source
                mk = sb("mk", [CH, TB, 8], F32, L)
                bst = sb("bst", [CH, TB], F32, L)
                lhs = [sb(f"lhs{k}", [CH, 4, 128], F32, L) for k in two]
                hot = [sb(f"hot{k}", [CH, A7], F32, L) for k in range(4)]
                io8 = sb("io8", [CH, 8], F32, L)
                iob = sb("iob", [CH, A7], F32, L)
                zz = sb("zz", [CH, A7], F32, L)
                c_bk, c_lhs, c_hot, c_ag = lsem("bk"), lsem("lhs"), lsem("hot"), lsem("ag")
                g(lambda e: e.iota(io8[:, :], pattern=[[1, 8]], base=0, channel_multiplier=0,
                                   allow_small_or_imprecise_dtypes=True),
                  lambda e: e.iota(iob[:, :], pattern=[[1, A7]], base=0, channel_multiplier=0,
                                   allow_small_or_imprecise_dtypes=True))
                v(lambda e: e.memset(zz[:, :], 0.0))
                t(*[lambda e, k=k: e.matmul(PS[:, 6 + k, 0:A7 // 2], zz[:, 0:128], zz[:, 0:A7 // 2],
                                            start=True, stop=False) for k in two])
            together()

            def used_up(b):
                return (c_run, b.next(-1).count(D, 0)) if by_source is None else (c_hot, b.next(-1).count(TB, 0))

            def load_ix(b):
                wait(nc.sync, c_g[b.k], b.slot(16 * TB, 0))
                sp_load(ix[b.k][:, :], index_c[:, b.cols()], c_ix[b.k])

            def sp(b):
                if b.next(1).exists():
                    load_ix(b.next(1))
                if by_source is None:
                    wait(nc.sync, c_run, b.count(D, D))
                    sp_load(sums_c[:, b.cols(), :], run[b.k][:, :, :], c_st[b.k])

            loop(nc.sync, sp, NB, TB, before=load_ix)

            def gather(b):
                wait(nc.gpsimd, c_ix[b.k], b.slot(16, 16))
                wait(nc.gpsimd, *used_up(b))
                for q in range(TB):
                    nc.gpsimd.indirect_dma_start(gt_[b.k][:, q, :], None, tab,
                                                 bass.IndirectOffsetOnAxis(ap=ix[b.k][:, q:q + 1], axis=0))\
                        .then_inc(c_g[b.k], 16)

            loop(nc.gpsimd, gather, NB, TB)

            def multiply(b, q):
                wait(nc.tensor, c_zt, b.count(G, q + 1))
                if q == 0:
                    wait(nc.tensor, *used_up(b))
                for r in range(4):
                    o = (4 * q + r) * D
                    mm = nc.tensor.matmul(PS[0:CH, 2 + b.k, o:o + D], zt[q % 2][:, r * CH:r * CH + CH], wc[:, :])
                mm.then_inc(c_mm, 1)

            def pe(b):
                for q in range(G):
                    wait(nc.tensor, c_z, b.count(G, q + 1))
                    wait(nc.tensor, c_zt, b.count(G, q - 1))
                    for r in range(4):
                        mm = nc.tensor.transpose(PS[:, q % 2, r * CH:r * CH + CH], z[q % 2][:, r, :], ident[0:CH, 0:CH])
                    mm.then_inc(c_tr, 1)
                    if q:
                        multiply(b, q - 1)
                multiply(b, G - 1)
                if by_source is not None:
                    for q in range(G):
                        wait(nc.tensor, c_lhs, b.count(G, q + 1))
                        for r in range(4):
                            wait(nc.tensor, c_hot, b.count(TB, 4 * q + r + 1))
                            for k in two:
                                mm = nc.tensor.matmul(PS[:, 6 + k, 0:A7 // 2], lhs[q % 2][:, r, :],
                                                      hot[r][:, k * A7 // 2:(k + 1) * A7 // 2],
                                                      start=False, stop=False)
                            mm.then_inc(c_ag, 1)

            loop(nc.tensor, pe, NB, TB)

            def act(b):
                for q in range(G):
                    wait(nc.scalar, c_tr, b.count(G, q + 1))
                    wait(nc.scalar, c_mm, b.count(G, q - 1))
                    nc.scalar.activation(zt[q % 2][:, :], PS[:, q % 2, 0:4 * CH], ACT.Copy).then_inc(c_zt, 1)
                if by_source is not None:
                    wait(nc.scalar, c_mm, b.count(G, G))
                    wait(nc.scalar, c_lhs, b.count(G, 0))
                    nc.scalar.activation(ms[:, :, :].rearrange("p t f -> p (t f)"), PS[0:CH, 2 + b.k, :], ACT.Silu,
                                         scale=(D * 8) ** -0.5).then_inc(c_ms, 1)

            loop(nc.scalar, act, NB, TB)

            def dve(b):
                wait(V, c_g[b.k], b.slot(16 * TB, 16 * TB))
                for q in range(G):
                    wait(V, c_tr, b.count(G, q - 1))
                    rows = gt_[b.k][:, 4 * q:4 * q + 4, 0:D]
                    co = coef_sb[:, bass.ds(b.i * (2 * TB) + (b.k * TB + 4 * q), 4), :]
                    V.tensor_tensor(z[q % 2][:, :, :].rearrange("p t (r i) -> p t r i", r=8),
                                    bc(rows, 8, 2), bc(co, D, 3), ALU.mult).then_inc(c_z, 1)
                if by_source is None:
                    wait(V, c_mm, b.count(G, G))
                    if width > D:
                        wait(V, c_run, b.count(D, 0))
                        V.tensor_tensor(ms[:, :, :], PS[0:CH, 2 + b.k, :].rearrange("p (t f) -> p t f", f=D),
                                        gt_[b.k][:, :, D:2 * D], ALU.add).then_inc(c_ms, 1)
                        wait(V, c_ms, b.count(1, 1))
                    wait(V, c_run, b.count(D, 0))
                    wait(V, c_st[b.k], b.slot(16, 0))
                    msg = ms[:, :, :] if width > D else PS[0:CH, 2 + b.k, :].rearrange("p (t f) -> p t f", f=D)
                    for f in range(D):
                        V.tensor_tensor_scan(run[b.k][:, :, f], keep[:, b.cols()], msg[:, :, f],
                                             run[1 - b.k][:, TB - 1, f:f + 1], ALU.mult, ALU.add).then_inc(c_run, 1)
                else:
                    wait(V, c_hot, b.count(TB, 0))
                    V.tensor_copy(bst[:, :], bv[:, b.cols()]).then_inc(c_bk, 1)
                    wait(V, c_lhs, b.count(G, 0))
                    V.tensor_tensor(mk[:, :, :], bc(av[:, b.cols()], 8, 2), bc(io8[:, :], TB, 1), ALU.is_equal)\
                        .then_inc(c_bk, 1)
                    wait(V, c_ms, b.count(1, 1))
                    wait(V, c_bk, b.count(2, 2))
                    for q in range(G):
                        wait(V, c_ag, b.count(TB, 4 * q - 4))
                        V.tensor_tensor(lhs[q % 2][:, :, :].rearrange("p t (a f) -> p t a f", a=8),
                                        bc(mk[:, 4 * q:4 * q + 4, :], D, 3), bc(ms[:, 4 * q:4 * q + 4, :], 8, 2),
                                        ALU.mult).then_inc(c_lhs, 1)
                        for r in range(4):
                            wait(V, c_ag, b.count(TB, 4 * q + r - 3))
                            V.tensor_scalar(hot[r][:, :], iob[:, :], bst[:, 4 * q + r:4 * q + r + 1], None,
                                            ALU.is_equal).then_inc(c_hot, 1)

            loop(V, dve, NB, TB)
            if by_source is None:
                for k in two:
                    nc.sync.wait_ge(c_st[k], 16 * NB // 2)
            together()

            if by_source is None:
                t(lambda e: e.matmul(PS[0:CH, 0, 0:D], before[:, :], run[1][:, TB - 1, :]))
                ch.step("rows", [lambda e: e.indirect_dma_start(
                    patch_g[:, :], None, sums, bass.IndirectOffsetOnAxis(ap=patch_sum_src[:, 0:1], axis=0))], 16)
                v(lambda e: e.tensor_tensor(patch_g[:, :], patch_g[:, :], PS[0:CH, 0, 0:D], ALU.add))
                ch.wait(nc.gpsimd)
                nc.gpsimd.nop(nofuse=True)
                ch.step("rows", [lambda e: e.indirect_dma_start(
                    sums, bass.IndirectOffsetOnAxis(ap=patch_sum[:, 0:1], axis=0), patch_g[:, :], None,
                    bounds_check=lim_s, oob_is_err=False)], 16)
                ch.wait(nc.gpsimd)
                nc.gpsimd.nop(nofuse=True)
                ch.step("rows", [lambda e, j=j: e.indirect_dma_start(
                    agg[:, j, :], None, sums, bass.IndirectOffsetOnAxis(ap=end_idx[:, j:j + 1], axis=0))
                    for j in range(JT)], 16)
            else:
                t(*[lambda e, k=k: e.matmul(PS[:, 6 + k, 0:A7 // 2], zz[:, 0:128], zz[:, 0:A7 // 2],
                                            start=False, stop=True) for k in two])
                by_af = hot[0]
                big = sb("big", [128, A7], F32, L)
                nm = sb("nm", [128, 7, 128], F32, L)
                v(*[lambda e, k=k: e.tensor_copy(big[:, k * A7 // 2:(k + 1) * A7 // 2], PS[:, 6 + k, 0:A7 // 2])
                    for k in two])
                sizes = [min(128, A7 - 128 * k) for k in range(7)]
                t(*[lambda e, k=k: e.transpose(PS[0:sizes[k], k // 4, 128 * (k % 4):128 * (k % 4) + 128],
                                               big[:, 128 * k:128 * k + sizes[k]], ident[:, :]) for k in range(7)])
                v(*[lambda e, k=k: e.tensor_copy(nm[0:sizes[k], k, :],
                                                 PS[0:sizes[k], k // 4, 128 * (k % 4):128 * (k % 4) + 128])
                    for k in range(7)])
                aggd_v = aggd.rearrange("(a b) f -> b a f", a=8)
                dma(*[lambda e, k=k: e.dma_start(aggd_v[128 * k:128 * k + sizes[k], :, :],
                                                 nm[0:sizes[k], k, :].rearrange("p (a f) -> p a f", a=8))
                      for k in range(7)])
                dma(lambda e: e.dma_start(agg[:, 0:JT, :], aggd.rearrange("(j p) f -> p j f", p=128)))
            together()
            L.close()

        def log_softmax(x):
            v(lambda e: e.tensor_reduce(red[:, :], x[:, :, :], X, ALU.max))
            v(lambda e: e.tensor_tensor(x[:, :, :], x[:, :, :], bc(red[:, :], D, 2), ALU.subtract))
            a(lambda e: e.activation(tn[:, :, :], x[:, :, :], ACT.Exp))
            v(lambda e: e.tensor_reduce(red[:, :], tn[:, :, :], X, ALU.add))
            a(lambda e: e.activation(red[:, :], red[:, :], ACT.Ln))
            v(lambda e: e.tensor_tensor(x[:, :, :], x[:, :, :], bc(red[:, :], D, 2), ALU.subtract))

        h1 = xn
        for n, (W, root, bias) in enumerate((("W1", "root1", "b1"), ("W2", "root2", "b2"))):
            put_table(table, h1)
            dma(lambda e: e.dma_start(wc[:, :], io["L1_gnn_" + W].rearrange("r i o -> (r i) o")))
            conv(f"r{n}", table, D, io["src"])
            turned(h1)
            ps = times(io["L1_gnn_" + root])
            v(lambda e: e.tensor_tensor(flat(hn[:, :, :]), flat(agg[:, :, :]), ps, ALU.add))
            rb_ = row_of(io["L1_gnn_" + bias])
            v(lambda e: e.tensor_tensor(hn[:, :, :], hn[:, :, :], rb_, ALU.add))
            if n == 0:
                v(lambda e: e.tensor_scalar(hn[:, :, :], hn[:, :, :], 0.0, None, ALU.max))
            h1 = hn
        log_softmax(hn)
        layernorm(xn, hn)

        dma(lambda e: e.dma_start(coef_sb[:, :, :], io["edge_attr_8"].rearrange("(p t) f -> p t f", p=CH)))
        L2 = ExitStack()
        av = sb("av", [CH, T], F32, L2)
        bv = sb("bv", [CH, T], F32, L2)
        sr = ExitStack()
        si = sb("si", [CH, T], I32, sr)
        dma(lambda e: e.dma_start(si[:, :], src_c))
        v(lambda e: e.tensor_copy(bv[:, :], si[:, :]))
        v(lambda e: e.tensor_scalar(av[:, :], bv[:, :], float(A7), None, ALU.is_ge))
        for k in range(2, 8):
            v(lambda e: e.scalar_tensor_tensor(out=av[:, :], in0=bv[:, :], scalar=float(k * A7), in1=av[:, :],
                                               op0=ALU.is_ge, op1=ALU.add))
        v(lambda e: e.scalar_tensor_tensor(out=bv[:, :], in0=av[:, :], scalar=-float(A7), in1=bv[:, :],
                                           op0=ALU.mult, op1=ALU.add))
        sr.close()
        put_table(table, xn)
        dma(*[lambda e, j=j: e.dma_start(wc[D * j:D * j + D, :], io["L2_gnn_W_msg_tp"][:, j, :]) for j in range(8)])
        conv("m", table, D, io["dst"], by_source=(av, bv))
        turned(agg)
        ps = times(io["L2_gnn_W_msg_lin"])
        v(lambda e: e.tensor_scalar(flat(agg[:, :, :]), ps, D ** -0.5, None, ALU.mult))
        zu = sb("zu", [128, 2 * C2], F32, L2)
        zuT = sb("zuT", [128, 4, 128], F32, L2)
        wu = sb("wu", [128, 2, D], F32, L2)
        dma(lambda e: e.dma_start(wu[:, :, :], io["L2_gnn_W_upd_tp"].rearrange("(a i) h k -> (i h) a k", a=2)))
        for j in range(0, NJ, 2):
            v(lambda e: e.tensor_tensor(zu[:, :].rearrange("p (j i h) -> p j i h", j=2, i=D),
                                        bc(xn[:, j:j + 2, :], D, 3), bc(agg[:, j:j + 2, :], D, 2), ALU.mult))
            t(*[lambda e, k=k: e.transpose(PS[:, 0, 128 * k:128 * k + 128], zu[:, 128 * k:128 * k + 128], ident[:, :])
                for k in range(4)])
            v(lambda e: e.tensor_copy(zuT[:, :, :].rearrange("p a c -> p (a c)"), PS[:, 0, :]))
            t(*[lambda e, k=k: e.matmul(PS[:, 4 + k // 2, (j // 2) * D:(j // 2) * D + D], zuT[:, k, :], wu[:, k % 2, :],
                                        start=(k % 2 == 0), stop=(k % 2 == 1)) for k in range(4)])
        v(*[lambda e, k=k: e.tensor_copy(hn[:, k::2, :], PS[:, 4 + k, 0:NJ // 2 * D].rearrange("p (j f) -> p j f", f=D))
            for k in two])
        a(lambda e: e.activation(hn[:, :, :], hn[:, :, :], ACT.Silu, scale=1.0 / 16))
        turned(hn)
        ps = times(io["L2_gnn_W_upd_lin"])
        v(lambda e: e.scalar_tensor_tensor(out=flat(hn[:, :, :]), in0=ps, scalar=D ** -0.5, in1=flat(xn[:, :, :]),
                                           op0=ALU.mult, op1=ALU.add))
        layernorm(xn, hn)
        together()
        L2.close()

        h3 = xn
        part = sb("part", [128, D])
        mean = sb("mean", [128, D])
        for n in range(3):
            turned(h3)
            ps = times(io["L3_gnn_edge_b"][n, :].rearrange("(i o) -> i o", i=D))
            v(lambda e: e.tensor_copy(flat(tn[:, :, :]), ps))
            put_table(table2, h3)
            put_table(table2, tn, D)
            dma(lambda e: e.dma_start(wc[:, :], io["L3_gnn_edge_w"][n, :, :].rearrange("j (i o) -> (j i) o", i=D)))
            conv(f"c{n}", table2, 2 * D, io["src"])
            ps = times(io["L3_gnn_root_w"][n, :, :])
            v(lambda e: e.tensor_tensor(flat(hn[:, :, :]), flat(agg[:, :, :]), ps, ALU.add))
            rb_ = row_of(io["L3_gnn_root_b"][n, :])
            v(lambda e: e.tensor_tensor(hn[:, :, :], hn[:, :, :], rb_, ALU.add))

            def column_mean():
                v(lambda e: e.tensor_tensor(tn[:, :, :], tn[:, :, :], bc(valid[:, :], D, 2), ALU.mult))
                v(lambda e: e.tensor_reduce(part[:, :], tn[:, :, :].rearrange("p j f -> p f j"), X, ALU.add))
                t(lambda e: e.matmul(PS[:, 0, 0:D], ones[:, :], part[:, :]))
                v(lambda e: e.tensor_scalar(mean[:, :], PS[:, 0, 0:D], 1.0 / N, None, ALU.mult))

            if n < 2:
                v(lambda e: e.tensor_copy(tn[:, :, :], hn[:, :, :]))
                column_mean()
                v(lambda e: e.tensor_tensor(hn[:, :, :], hn[:, :, :], bc(mean[:, :], NJ, 1), ALU.subtract))
                v(lambda e: e.tensor_tensor(tn[:, :, :], hn[:, :, :], hn[:, :, :], ALU.mult))
                column_mean()
                v(lambda e: e.tensor_scalar(mean[:, :], mean[:, :], EPS, None, ALU.add))
                a(lambda e: e.activation(mean[:, :], mean[:, :], ACT.Sqrt))
                v(lambda e: e.reciprocal(mean[:, :], mean[:, :]))
                row_of(io["L3_gnn_bn_gamma"][n, :])
                v(lambda e: e.tensor_tensor(mean[:, :], mean[:, :], row_b[:, :], ALU.mult))
                v(lambda e: e.tensor_tensor(hn[:, :, :], hn[:, :, :], bc(mean[:, :], NJ, 1), ALU.mult))
                rb_ = row_of(io["L3_gnn_bn_beta"][n, :])
                v(lambda e: e.tensor_tensor(hn[:, :, :], hn[:, :, :], rb_, ALU.add))
            v(lambda e: e.tensor_scalar(hn[:, :, :], hn[:, :, :], 0.0, None, ALU.max))
            h3 = hn
        turned(hn)
        ps = times(io["L3_gnn_pred_w"])
        rb_ = row_of(io["L3_gnn_pred_b"])
        v(lambda e: e.tensor_tensor(hn[:, :, :], ps.rearrange("p (j f) -> p j f", f=D), rb_, ALU.add))
        layernorm(xn, hn)
        dma(lambda e: e.dma_start(out[0:6144, :].rearrange("(j p) f -> p j f", p=128), xn[:, 0:48, :]),
            lambda e: e.dma_start(out[6144:N, :], xn[0:N - 6144, 48, :]))
        ch.wait(nc.sync)


NAMES = ['x', 'src', 'dst', 'edge_attr_16', 'edge_attr_8', 'edge_type_8',
         'L0_gnn_W_msg', 'L0_gnn_b_msg', 'L0_gnn_W_attn', 'L0_gnn_b_attn',
         'L1_gnn_W1', 'L1_gnn_root1', 'L1_gnn_b1', 'L1_gnn_W2', 'L1_gnn_root2', 'L1_gnn_b2',
         'L2_gnn_W_msg_tp', 'L2_gnn_W_msg_lin', 'L2_gnn_W_upd_tp', 'L2_gnn_W_upd_lin',
         'L3_gnn_edge_w', 'L3_gnn_edge_b', 'L3_gnn_root_w', 'L3_gnn_root_b',
         'L3_gnn_bn_gamma', 'L3_gnn_bn_beta', 'L3_gnn_pred_w', 'L3_gnn_pred_b']


def kernel(**inputs):
    import numpy as np
    import concourse.bacc as bacc
    from concourse.bass_utils import run_bass_kernel_spmd

    nc = bacc.Bacc("TRN2", target_bir_lowering=False, num_devices=1)
    arrays, io = {}, {}
    for name in NAMES:
        arr = np.ascontiguousarray(inputs[name])
        arrays["in_" + name] = arr
        io[name] = nc.dram_tensor("in_" + name, arr.shape, mybir.dt.from_np(arr.dtype), kind="ExternalInput").ap()
    out = nc.dram_tensor("out", (N, D), F32, kind="ExternalOutput").ap()
    program(nc, io, out)
    r = run_bass_kernel_spmd(nc, [arrays], core_ids=[0])
    return r.results[0]["out"]
```

```python
from contextlib import ExitStack

import concourse.bass as bass
from concourse import mybir

F32 = mybir.dt.float32
I32 = mybir.dt.int32
I16 = mybir.dt.int16
BF16 = mybir.dt.bfloat16
ALU = mybir.AluOpType
ACT = mybir.ActivationFunctionType
X = mybir.AxisListType.X

N, E, D = 6250, 200000, 16
NP, NJ, JT = 6272, 56, 49
CH, T = 125, 1600
C2 = D * D
ROW = 772
TB0, NB0 = 8, 200
TB, NB = 32, 50
BIG = 1e30
SKIP = 1 << 20
A7 = 784
HB, HG = 12, 3
A9, KT = 7, 7
EPS = 1e-5


class Chain:

    def __init__(self, nc, sem):
        self.nc, self.last = nc, None
        self.sems = {e: sem("chain_" + e) for e in ("vector", "scalar", "tensor", "gpsimd", "sync", "rows")}
        self.n = dict.fromkeys(self.sems, 0)
        self.engines = {"vector": nc.vector, "scalar": nc.scalar, "tensor": nc.tensor,
                        "gpsimd": nc.gpsimd, "sync": nc.sync, "rows": nc.gpsimd}

    def wait(self, eng):
        if self.last:
            eng.wait_ge(*self.last)

    def step(self, name, instrs, inc=1):
        eng = self.engines[name]
        self.wait(eng)
        for f in instrs:
            f(eng).then_inc(self.sems[name], inc)
            self.n[name] += inc
        self.last = (self.sems[name], self.n[name])

    def v(self, *fs):
        self.step("vector", fs)

    def a(self, *fs):
        self.step("scalar", fs)

    def t(self, *fs):
        self.step("tensor", fs)

    def g(self, *fs):
        self.step("gpsimd", fs)

    def dma(self, *fs):
        self.step("sync", fs, 16)


def program(nc, io, out):
    ctx = ExitStack()
    with ctx:
        def sem(name):
            return ctx.enter_context(nc.semaphore(name))

        def sb(name, shape, dt=F32, c=ctx):
            return c.enter_context(nc.sbuf_tensor(name, shape, dt))

        def dram(name, shape, dt=F32):
            return nc.dram_tensor(name, shape, dt, kind="Internal").ap()

        table8 = dram("node_table8", (NP, 8 * D))
        table9 = dram("node_table9", (NP, 9 * D))
        sums = dram("running_sums", (E + 8, D))
        pick_a = dram("pick_a", (T, 128), I16)
        pick_b = dram("pick_b", (T, 128), I16)
        rows0 = dram("rows0", (NP, ROW))
        flags = dram("edge_flags", (CH, T, 4))
        ends = dram("end_rows", (CH, T), I32)
        aggd = dram("agg_by_source", (8 * A7, D))

        keep = sb("keep", [CH, T + 1])
        dstf = sb("dstf", [CH, T])
        first_of = sb("chunk_first", [CH, 1])
        last_of = sb("chunk_last", [CH, 1])
        ident = sb("ident", [128, 128])
        ones = sb("ones", [128, 128])
        before = sb("chain_mask", [CH, CH])
        cc_row = sb("chain_keep_row", [128, CH])
        patch_row = sb("patch_row", [CH, 1], I32)
        patch_src = sb("patch_src", [CH, 1], I32)
        patch_sum = sb("patch_sum", [CH, 1], I32)
        patch_sum_src = sb("patch_sum_src", [CH, 1], I32)
        end_idx = sb("end_idx", [128, NJ], I32)
        valid = sb("valid", [128, NJ])
        xn = sb("xn", [128, NJ, D])
        hn = sb("hn", [128, NJ, D])
        agg = sb("agg", [128, NJ, D])
        tn = sb("tn", [128, NJ, D])
        red = sb("red", [128, NJ])
        group_mask = sb("group_mask", [128, 8])
        wstage = sb("wstage", [128, D])
        blockdiag = sb("blockdiag", [128, 8, D])
        xT = sb("xT", [128, 7 * 128])
        row_b = sb("row_b", [128, D])
        PS = ctx.enter_context(nc.psum_tensor("PS", [128, 8, 512], F32))
        ch = Chain(nc, sem)
        v, a, t, g, dma = ch.v, ch.a, ch.t, ch.g, ch.dma

        def bc(ap, n, at):
            x = ap.unsqueeze(at)
            shape = list(x.shape)
            shape[at] = n
            return x.to_broadcast(shape)

        def together():
            for eng in (nc.sync, nc.gpsimd, nc.tensor, nc.scalar, nc.vector):
                ch.wait(eng)
            nc.all_engine_barrier()

        setup = ExitStack()
        iop = sb("iop", [128, 1], F32, setup)
        iorow = sb("iorow", [128, CH], F32, setup)
        tri = sb("tri", [CH, CH], F32, setup)
        v(lambda e: e.memset(ones[:, :], 1.0), lambda e: e.memset(ident[:, :], 0.0),
          lambda e: e.memset(xn[:, :, :], 0.0), lambda e: e.memset(valid[:, :], 1.0),
          lambda e: e.memset(group_mask[:, :], 1.0), lambda e: e.memset(agg[:, :, :], 0.0),
          lambda e: e.memset(end_idx[:, :], 0), lambda e: e.memset(hn[:, :, :], 0.0))
        g(lambda e: e.affine_select(out=ident[:, :], in_=ident[:, :], compare_op=ALU.not_equal, fill=1.0,
                                    base=0, pattern=[[-1, 128]], channel_multiplier=1),
          lambda e: e.affine_select(out=valid[:, :], in_=valid[:, :], compare_op=ALU.is_ge, fill=0.0,
                                    base=N - 1, pattern=[[-128, NJ]], channel_multiplier=-1),
          lambda e: e.affine_select(out=group_mask[:, :], in_=group_mask[:, :], compare_op=ALU.is_ge, fill=0.0,
                                    base=0, pattern=[[-16, 8]], channel_multiplier=1),
          lambda e: e.iota(iop[:, :], pattern=[[0, 1]], base=0, channel_multiplier=1,
                           allow_small_or_imprecise_dtypes=True),
          lambda e: e.iota(iorow[:, :], pattern=[[1, CH]], base=0, channel_multiplier=0,
                           allow_small_or_imprecise_dtypes=True))
        g(lambda e: e.affine_select(out=group_mask[:, :], in_=group_mask[:, :], compare_op=ALU.is_ge, fill=0.0,
                                    base=15, pattern=[[16, 8]], channel_multiplier=-1))
        v(lambda e: e.tensor_scalar(tri[:, :], iorow[0:CH, :], iop[0:CH, 0:1], None, ALU.is_gt))

        dsti = sb("dsti", [CH, T], I32, setup)
        nbi = sb("nbi", [CH, 2], I32, setup)
        nb = sb("nb", [CH, 2], F32, setup)
        fl = sb("fl", [CH, T, 4], F32, setup)
        st = sb("st", [CH, T + 1], F32, setup)
        sidx = sb("sidx", [CH, T], I32, setup)
        tmp = sb("tmp", [CH, T], F32, setup)
        small = sb("small", [CH, 12], F32, setup)
        diag = sb("diag", [CH, CH], F32, setup)
        frow = sb("frow", [CH, CH], F32, setup)
        dst_c = io["dst"].rearrange("(p t) -> p t", p=CH)
        v(lambda e: e.memset(nbi[:, :], -1))
        with nc.allow_non_contiguous_dma(reason="one word per chunk"):
            dma(lambda e: e.dma_start(dsti[:, :], dst_c),
                lambda e: e.dma_start(nbi[1:CH, 0:1], dst_c[0:CH - 1, T - 1:T]),
                lambda e: e.dma_start(nbi[0:CH - 1, 1:2], dst_c[1:CH, 0:1]),
                lambda e: e.dma_start(xn[:, 0:48, :], io["x"][0:6144, :].rearrange("(j p) f -> p j f", p=128)),
                lambda e: e.dma_start(xn[0:N - 6144, 48, :], io["x"][6144:N, :]))
        v(lambda e: e.tensor_copy(dstf[:, :], dsti[:, :]), lambda e: e.tensor_copy(nb[:, :], nbi[:, :]),
          lambda e: e.memset(st[:, 0:1], 1.0))
        s = lambda k: small[:, k:k + 1]
        FIRST, LAST, CONT, CHIN, SAME, OK, EF, CCK, LEN, T0, T1 = range(11)
        v(lambda e: e.tensor_tensor(st[:, 1:T], dstf[:, 1:T], dstf[:, 0:T - 1], ALU.not_equal),
          lambda e: e.tensor_copy(first_of[:, :], dstf[:, 0:1]),
          lambda e: e.tensor_copy(last_of[:, :], dstf[:, T - 1:T]))
        v(lambda e: e.tensor_tensor(s(CONT), nb[:, 1:2], last_of[:, :], ALU.is_equal),
          lambda e: e.tensor_tensor(s(CHIN), nb[:, 0:1], first_of[:, :], ALU.is_equal),
          lambda e: e.tensor_tensor(s(SAME), first_of[:, :], last_of[:, :], ALU.is_equal),
          lambda e: e.tensor_tensor(st[:, T:T + 1], nb[:, 1:2], last_of[:, :], ALU.not_equal),
          lambda e: e.tensor_scalar(tmp[:, :], dstf[:, :], first_of[:, 0:1], None, ALU.is_equal))
        v(lambda e: e.tensor_reduce(s(LEN), tmp[:, :], X, ALU.add),
          lambda e: e.tensor_tensor(s(T0), s(SAME), s(CONT), ALU.mult),
          lambda e: e.tensor_tensor(s(CCK), s(SAME), s(CHIN), ALU.mult),
          lambda e: e.tensor_scalar(keep[:, 0:T], st[:, 0:T], -1.0, 1.0, ALU.mult, ALU.add),
          lambda e: e.memset(keep[:, T:T + 1], 0.0),
          lambda e: e.tensor_scalar(fl[:, :, 0], st[:, 0:T], -BIG, None, ALU.mult),
          lambda e: e.tensor_scalar(fl[:, :, 2], st[:, 1:T + 1], -BIG, None, ALU.mult))
        v(lambda e: e.tensor_scalar(s(T0), s(T0), -1.0, 1.0, ALU.mult, ALU.add),
          lambda e: e.tensor_copy(fl[:, :, 1], keep[:, 0:T]))
        v(lambda e: e.tensor_tensor(s(OK), s(CHIN), s(T0), ALU.mult),
          lambda e: e.tensor_scalar(s(EF), iop[0:CH, :], float(T), -1.0, ALU.mult, ALU.add),
          lambda e: e.tensor_scalar(tmp[:, :], dstf[:, :], float(-SKIP), None, ALU.add))
        v(lambda e: e.tensor_tensor(s(EF), s(EF), s(LEN), ALU.add),
          lambda e: e.tensor_tensor(tmp[:, :], tmp[:, :], st[:, 1:T + 1], ALU.mult),
          lambda e: e.tensor_scalar(s(T0), first_of[:, :], float(-SKIP), None, ALU.add))
        v(lambda e: e.tensor_scalar(s(T1), s(EF), float(-SKIP), None, ALU.add),
          lambda e: e.tensor_tensor(s(T0), s(T0), s(OK), ALU.mult),
          lambda e: e.tensor_scalar(sidx[:, :], tmp[:, :], float(SKIP), None, ALU.add),
          lambda e: e.tensor_copy(patch_sum_src[:, :], s(EF)),
          lambda e: e.tensor_copy(patch_src[:, :], first_of[:, :]))
        v(lambda e: e.tensor_tensor(s(T1), s(T1), s(OK), ALU.mult),
          lambda e: e.tensor_scalar(patch_row[:, :], s(T0), float(SKIP), None, ALU.add))
        v(lambda e: e.tensor_scalar(patch_sum[:, :], s(T1), float(SKIP), None, ALU.add),
          lambda e: e.tensor_scalar(diag[:, :], ident[0:CH, 0:CH], first_of[:, 0:1], None, ALU.mult))
        g(lambda e: e.iota(fl[:, :, 3], pattern=[[1, T]], base=0, channel_multiplier=T,
                           allow_small_or_imprecise_dtypes=True))

        def over_partitions(dst_ap, rows):
            t(lambda e: e.matmul(PS[0:rows, 0, 0:CH], ones[0:CH, 0:rows], diag[:, :]))
            v(lambda e: e.tensor_copy(dst_ap, PS[0:rows, 0, 0:CH]))

        over_partitions(frow[:, :], CH)
        v(lambda e: e.tensor_scalar(diag[:, :], ident[0:CH, 0:CH], s(CCK), None, ALU.mult))
        over_partitions(cc_row[:, :], 128)
        v(lambda e: e.tensor_scalar(before[:, :], frow[:, :], last_of[:, 0:1], None, ALU.is_equal))
        v(lambda e: e.tensor_tensor(before[:, :], before[:, :], tri[:, :], ALU.mult))

        initrow = sb("initrow", [128, 7, ROW], F32, setup)
        zrow = sb("zrow", [1, 8 * D], F32, setup)
        v(lambda e: e.memset(initrow[:, :, :], 0.0), lambda e: e.memset(zrow[:, :], 0.0))
        v(lambda e: e.memset(initrow[:, :, C2:2 * C2], 1.0), lambda e: e.memset(initrow[:, :, 3 * C2:], float(E)))
        rows0_j = rows0.rearrange("(j p) c -> p j c", p=128)
        si = sb("srci", [CH, T], I32, setup)
        dma(lambda e: e.dma_start(si[:, :], io["src"].rearrange("(p t) -> p t", p=CH)))
        s_init = sem("s_init")
        ch.wait(nc.sync)
        for k in range(7):
            nc.sync.dma_start(rows0_j[:, 7 * k:7 * k + 7, :], initrow[:, :, :]).then_inc(s_init, 16)
        nc.sync.dma_start(flags, fl[:, :, :]).then_inc(s_init, 16)
        nc.sync.dma_start(ends, sidx[:, :]).then_inc(s_init, 16)
        nc.sync.dma_start(sums[E:E + 8, :].rearrange("(a e) f -> a (e f)", a=1), zrow[:, :]).then_inc(s_init, 16)

        pab = [sb(f"pab{k}", [CH, T], F32, setup) for k in range(2)]
        NT = (T + 127) // 128
        pT = sb("pT", [128, NT, 2, 128], I16, setup)
        v(lambda e: e.tensor_copy(pab[1][:, :], si[:, :]), lambda e: e.memset(pT[:, :, :, :], -1))
        v(lambda e: e.tensor_scalar(pab[0][:, :], pab[1][:, :], float(128 * KT), None, ALU.is_ge))
        for k in range(2, A9):
            v(lambda e: e.scalar_tensor_tensor(out=pab[0][:, :], in0=pab[1][:, :], scalar=float(k * 128 * KT),
                                               in1=pab[0][:, :], op0=ALU.is_ge, op1=ALU.add))
        v(lambda e: e.scalar_tensor_tensor(out=pab[1][:, :], in0=pab[0][:, :], scalar=-128.0 * KT, in1=pab[1][:, :],
                                           op0=ALU.mult, op1=ALU.add))
        wd = [min(128, T - 128 * k) for k in range(NT)]
        at = lambda k, n: PS[0:wd[k], (2 * k + n) // 4, 128 * ((2 * k + n) % 4):128 * ((2 * k + n) % 4) + CH]
        t(*[lambda e, n=n, k=k: e.transpose(at(k, n), pab[n][:, 128 * k:128 * k + wd[k]], ident[0:CH, 0:CH])
            for k in range(NT) for n in range(2)])
        v(*[lambda e, n=n, k=k: e.tensor_copy(pT[0:wd[k], k, n, 0:CH], at(k, n)) for k in range(NT) for n in range(2)])
        full = 128 * (NT - 1)
        dma(*[lambda e, n=n, d_=d_: e.dma_start(d_[0:full, :].rearrange("(k q) c -> q k c", q=128), pT[:, 0:NT - 1, n, :])
              for n, d_ in enumerate((pick_a, pick_b))],
            *[lambda e, n=n, d_=d_: e.dma_start(d_[full:T, :], pT[0:T - full, NT - 1, n, :])
              for n, d_ in enumerate((pick_a, pick_b))])
        nc.sync.wait_ge(s_init, 16 * 10)
        together()
        setup.close()

        L = ExitStack()
        lsem = lambda n: L.enter_context(nc.semaphore(n))
        two = range(2)
        waug = sb("waug", [128, 2 * C2], F32, L)
        idx = [sb(f"idx{k}", [CH, TB0], I32, L) for k in two]
        sid = [sb(f"sid{k}", [CH, TB0], I32, L) for k in two]
        flb = [sb(f"flb{k}", [CH, TB0, 4], F32, L) for k in two]
        ef = [sb(f"ef{k}", [CH, TB0, 32], F32, L) for k in two]
        h = [sb(f"h{k}", [CH, TB0, D], F32, L) for k in two]
        efT = [sb(f"efT{k}", [128, 128], F32, L) for k in two]
        e2 = [sb(f"e2{k}", [CH, TB0, C2], F32, L) for k in two]
        M = [sb(f"M{k}", [CH, TB0, C2], F32, L) for k in two]
        PX = [sb(f"PX{k}", [CH, TB0, 2 * C2], F32, L) for k in two]
        ST = [sb(f"ST{k}", [CH, TB0, ROW], F32, L) for k in two]
        cf = [sb(f"cf{k}", [CH, C2], F32, L) for k in two]
        v(lambda e: e.memset(waug[:, :], 0.0), lambda e: e.memset(M[1][:, :, :], 0.0),
          lambda e: e.memset(ST[0][:, :, :], 0.0), lambda e: e.memset(ST[1][:, :, :], 0.0),
          *[lambda e, k=k: e.memset(ef[k][:, :, :], 0.0) for k in two])
        v(*[lambda e, k=k: e.memset(ef[k][:, :, D:D + 1], 1.0) for k in two])
        dma(*[lambda e, q=q, o=o, w=w: e.dma_start(waug[32 * q:32 * q + D, o:o + C2], io[w])
              for q in range(4) for o, w in ((0, "L0_gnn_W_attn"), (C2, "L0_gnn_W_msg"))],
            *[lambda e, q=q, o=o, w=w: e.dma_start(waug[32 * q + D:32 * q + D + 1, o:o + C2],
                                                   io[w].rearrange("(a n) -> a n", a=1))
              for q in range(4) for o, w in ((0, "L0_gnn_b_attn"), (C2, "L0_gnn_b_msg"))])
        together()

        l_in = [lsem(f"l_in{k}") for k in two]
        l_fl = [lsem(f"l_fl{k}") for k in two]
        l_si = [lsem(f"l_si{k}") for k in two]
        l_g = [lsem(f"l_g{k}") for k in two]
        l_tr, l_et, l_mm, l_use = lsem("l_tr"), lsem("l_et"), lsem("l_mm"), lsem("l_use")
        l_e2, l_fw, l_bw, l_a = lsem("l_e2"), lsem("l_fw"), lsem("l_bw"), lsem("l_a")
        l_ex, l_mc, l_p, l_q, l_s = lsem("l_ex"), lsem("l_mc"), lsem("l_p"), lsem("l_q"), lsem("l_s")
        l_sc = [lsem(f"l_sc{k}") for k in two]
        src_c = io["src"].rearrange("(p t) -> p t", p=CH)
        ea16 = io["edge_attr_16"].rearrange("(p t) f -> p t f", p=CH)

        def sp_load(dst, src, sm):
            nc.sync.dma_start(dst, src).then_inc(sm, 16)

        class Blk:

            def __init__(self, i, k, n, tb):
                while not isinstance(i, int) and k > 1 or k < 0:
                    i, k = (i + 1, k - 2) if k > 1 else (i - 1, k + 2)
                if isinstance(i, int):
                    i, k = (2 * i + k) // 2, k % 2
                self.i, self.k, self.n, self.tb = i, k, n, tb

            def exists(self):
                return not isinstance(self.i, int) or 0 <= 2 * self.i + self.k < self.n

            def next(self, d):
                return Blk(self.i, self.k + d, self.n, self.tb)

            def count(self, per, more):
                return self.i * (2 * per) + (self.k * per + more)

            def slot(self, per, more):
                return self.i * per + more

            def cols(self):
                return bass.ds(self.i * (2 * self.tb) + self.k * self.tb, self.tb)

        def wait(e, sm, val):
            if not isinstance(val, int) or val > 0:
                e.wait_ge(sm, val)
                if e in (nc.sync, nc.gpsimd):
                    e.nop(nofuse=True)

        def loop(eng, body, n, tb, before=None, after=None):
            if before:
                before(Blk(0, 0, n, tb))
            for k in two:
                body(Blk(0, k, n, tb))
            with eng.Fori(1, n // 2 - 1) as i:
                for k in two:
                    body(Blk(i, k, n, tb))
            for k in two:
                body(Blk(n // 2 - 1, k, n, tb))
            if after:
                after(Blk(n // 2 - 1, 1, n, tb))

        e = nc.sync

        def load_in(b):
            wait(nc.sync, l_g[b.k], b.slot(16 * TB0, 0))
            wait(nc.sync, l_tr, b.next(-2).count(2, 2))
            sp_load(idx[b.k][:, :], src_c[:, b.cols()], l_in[b.k])
            sp_load(ef[b.k][:, :, 0:D], ea16[:, b.cols(), :], l_in[b.k])

        def load_fl(b):
            wait(nc.sync, l_s, b.next(-1).count(TB0, 0))
            wait(nc.sync, l_mc, b.next(-1).count(2, 0))
            sp_load(flb[b.k][:, :, :], flags[:, b.cols(), :], l_fl[b.k])

        def load_si(b):
            wait(nc.sync, l_sc[b.k], b.slot(16 * TB0, 0))
            sp_load(sid[b.k][:, :], ends[:, b.cols()], l_si[b.k])

        def sp_body(b):
            if b.next(1).exists():
                load_in(b.next(1))
            load_fl(b)
            if b.next(-1).exists():
                load_si(b.next(-1))

        loop(nc.sync, sp_body, NB0, TB0, before=load_in, after=load_si)

        lim0 = nc.gpsimd.to_reg(NP - 1)

        def gather0(b):
            wait(nc.gpsimd, l_in[b.k], b.slot(32, 32))
            wait(nc.gpsimd, l_use, b.next(-1).count(2, 0))
            for q in range(TB0):
                nc.gpsimd.indirect_dma_start(h[b.k][:, q, :], None, io["x"],
                                             bass.IndirectOffsetOnAxis(ap=idx[b.k][:, q:q + 1], axis=0))\
                    .then_inc(l_g[b.k], 16)

        def scatter0(b):
            wait(nc.gpsimd, l_s, b.count(TB0, TB0))
            wait(nc.gpsimd, l_mc, b.count(2, 2))
            wait(nc.gpsimd, l_si[b.k], b.slot(16, 16))
            for q in range(TB0):
                nc.gpsimd.indirect_dma_start(rows0, bass.IndirectOffsetOnAxis(ap=sid[b.k][:, q:q + 1], axis=0),
                                             ST[b.k][:, q, :], None, bounds_check=lim0, oob_is_err=False)\
                    .then_inc(l_sc[b.k], 16)

        def pool_body(b):
            if b.next(1).exists():
                gather0(b.next(1))
            if b.next(-1).exists():
                scatter0(b.next(-1))

        loop(nc.gpsimd, pool_body, NB0, TB0, before=gather0, after=scatter0)

        def turn(b):
            for q in two:
                wait(nc.tensor, l_in[b.k], b.slot(32, 32))
                wait(nc.tensor, l_et, b.next(-1).count(2, q + 1))
                nc.tensor.transpose(PS[:, 4 + q, 0:CH], ef[b.k][:, 4 * q:4 * q + 4, :].rearrange("p a c -> p (a c)"),
                                    ident[0:CH, 0:CH]).then_inc(l_tr, 1)

        def weigh(b):
            for q in two:
                wait(nc.tensor, l_et, b.count(2, q + 1))
                wait(nc.tensor, l_use, b.count(2, q))
                for r in range(4):
                    mm = nc.tensor.matmul(PS[0:CH, r, :], efT[q][32 * r:32 * r + D + 1, 0:CH],
                                          waug[32 * r:32 * r + D + 1, :])
                mm.then_inc(l_mm, 1)

        def pe_body(b):
            weigh(b)
            if b.next(1).exists():
                turn(b.next(1))

        loop(nc.tensor, pe_body, NB0, TB0, before=turn)

        def copy_turned(b):
            for q in two:
                wait(nc.scalar, l_tr, b.count(2, q + 1))
                wait(nc.scalar, l_mm, b.next(-1).count(2, q + 1))
                nc.scalar.activation(efT[q][:, 0:CH], PS[:, 4 + q, 0:CH], ACT.Copy).then_inc(l_et, 1)

        def act_body(b):
            if b.next(1).exists():
                copy_turned(b.next(1))
            wait(nc.scalar, l_a, b.count(2, 2))
            nc.scalar.activation(cf[b.k][:, :], cf[b.k][:, :], ACT.Exp).then_inc(l_ex, 1)
            nc.scalar.activation(PX[b.k][:, :, 0:C2], e2[b.k][:, :, :], ACT.Exp).then_inc(l_ex, 1)
            wait(nc.scalar, l_sc[b.k], b.slot(16 * TB0, 0))
            nc.scalar.activation(ST[b.k][:, :, 0:C2], M[b.k][:, :, :], ACT.Copy).then_inc(l_mc, 1)
            nc.scalar.activation(ST[b.k][:, :, 3 * C2:3 * C2 + 1], flb[b.k][:, :, 3:4], ACT.Copy).then_inc(l_mc, 1)

        loop(nc.scalar, act_body, NB0, TB0, before=copy_turned)

        V = nc.vector

        def products(b, q):
            s4 = slice(4 * q, 4 * q + 4)
            hb = bc(h[b.k][:, s4, :], D, 3)
            if q == 0:
                wait(V, l_g[b.k], b.slot(16 * TB0, 16 * TB0))
                wait(V, l_ex, b.next(-2).count(2, 2))
                wait(V, l_p, b.next(-2).count(1, 1))
                wait(V, l_s, b.next(-2).count(TB0, TB0))
            wait(V, l_mm, b.count(2, q + 1))
            V.tensor_tensor(e2[b.k][:, s4, :].rearrange("p t (i o) -> p t i o", i=D),
                            PS[0:CH, 0:4, 0:C2].rearrange("p t (i o) -> p t i o", i=D), hb, ALU.mult).then_inc(l_e2, 1)
            V.tensor_tensor(PX[b.k][:, s4, C2:].rearrange("p t (i o) -> p t i o", i=D),
                            PS[0:CH, 0:4, C2:].rearrange("p t (i o) -> p t i o", i=D), hb, ALU.mult).then_inc(l_use, 1)

        def maxima(b):
            wait(V, l_fl[b.k], b.slot(16, 16))
            wait(V, l_e2, b.count(2, 2))
            wait(V, l_mc, b.next(-1).count(2, 0))
            for q in range(TB0):
                wait(V, l_fw, b.count(TB0, q))
                prev = M[b.k][:, q - 1, :] if q else M[1 - b.k][:, TB0 - 1, :]
                V.scalar_tensor_tensor(out=M[b.k][:, q, :], in0=prev, scalar=flb[b.k][:, q, 0:1],
                                       in1=e2[b.k][:, q, :], op0=ALU.add, op1=ALU.max).then_inc(l_fw, 1)
            wait(V, l_fw, b.count(TB0, TB0))
            for n, q in enumerate(range(TB0 - 2, -1, -1)):
                wait(V, l_bw, b.count(TB0 - 1, n))
                V.scalar_tensor_tensor(out=M[b.k][:, q, :], in0=M[b.k][:, q + 1, :], scalar=flb[b.k][:, q, 2:3],
                                       in1=M[b.k][:, q, :], op0=ALU.add, op1=ALU.max).then_inc(l_bw, 1)
            wait(V, l_bw, b.count(TB0 - 1, TB0 - 1))
            wait(V, l_q, b.next(-1).count(1, 0))
            V.tensor_tensor(e2[b.k][:, :, :], e2[b.k][:, :, :], M[b.k][:, :, :], ALU.subtract).then_inc(l_a, 1)
            V.scalar_tensor_tensor(out=cf[b.k][:, :], in0=M[1 - b.k][:, TB0 - 1, :], scalar=flb[b.k][:, 0, 0:1],
                                   in1=M[b.k][:, 0, :], op0=ALU.add, op1=ALU.subtract).then_inc(l_a, 1)

        def sums0(b):
            S, P = ST[b.k], PX[b.k]
            wait(V, l_ex, b.count(2, 2))
            wait(V, l_sc[b.k], b.slot(16 * TB0, 0))
            V.tensor_tensor(P[:, :, C2:], P[:, :, C2:], P[:, :, 0:C2], ALU.mult).then_inc(l_p, 1)
            wait(V, l_s, b.count(TB0, 0))
            V.tensor_tensor(S[:, 0, C2:3 * C2].rearrange("p (a c) -> p a c", a=2),
                            ST[1 - b.k][:, TB0 - 1, C2:3 * C2].rearrange("p (a c) -> p a c", a=2),
                            bc(cf[b.k][:, :], 2, 1), ALU.mult).then_inc(l_q, 1)
            wait(V, l_p, b.count(1, 1))
            wait(V, l_q, b.count(1, 1))
            V.tensor_tensor(S[:, 0, C2:3 * C2], S[:, 0, C2:3 * C2], P[:, 0, :], ALU.add).then_inc(l_s, 1)
            for q in range(1, TB0):
                wait(V, l_s, b.count(TB0, q))
                V.scalar_tensor_tensor(out=S[:, q, C2:3 * C2], in0=S[:, q - 1, C2:3 * C2],
                                       scalar=flb[b.k][:, q, 1:2], in1=P[:, q, :],
                                       op0=ALU.mult, op1=ALU.add).then_inc(l_s, 1)

        def dve_body(b):
            products(b, 0)
            if b.next(-1).exists():
                sums0(b.next(-1))
            products(b, 1)
            maxima(b)

        loop(V, dve_body, NB0, TB0, after=sums0)
        for k in two:
            for eng in (nc.gpsimd, nc.sync):
                eng.wait_ge(l_sc[k], 16 * TB0 * NB0 // 2)
        together()

        CI = PX[0]
        lastrow = ST[1][:, TB0 - 1, :]
        mT = [sb(f"mT{k}", [128, 3, CH + 1], F32, L) for k in two]
        w1 = sb("w1", [128, CH], F32, L)
        w2 = sb("w2", [128, CH], F32, L)
        rsc = sb("rsc", [128, CH], F32, L)
        inT = sb("inT", [128, 3, CH], F32, L)
        carry = sb("carry", [CH, 3 * C2], F32, L)
        got = sb("got", [CH, ROW], F32, L)
        mt = sb("mt", [CH, C2], F32, L)
        ea = sb("ea", [CH, 2, C2], F32, L)
        v(lambda e: e.tensor_scalar(rsc[:, :], cc_row[:, :], BIG, -BIG, ALU.mult, ALU.add),
          *[lambda e, k=k: e.memset(mT[k][:, :, :], 0.0) for k in two])
        for k in two:
            t(*[lambda e, c=c: e.transpose(PS[:, c, 0:CH], lastrow[:, c * C2 + 128 * k:c * C2 + 128 * k + 128],
                                           ident[0:CH, 0:CH]) for c in range(3)])
            v(lambda e: e.tensor_copy(inT[:, :, :], PS[:, 0:3, 0:CH]))
            v(lambda e: e.tensor_tensor_scan(mT[k][:, 0, 1:], rsc[:, :], inT[:, 0, :], 0.0, ALU.add, ALU.max))
            v(lambda e: e.tensor_tensor(w1[:, :], inT[:, 0, :], mT[k][:, 0, 1:], ALU.subtract),
              lambda e: e.tensor_tensor(w2[:, :], mT[k][:, 0, 0:CH], rsc[:, :], ALU.add))
            v(lambda e: e.tensor_tensor(w2[:, :], w2[:, :], mT[k][:, 0, 1:], ALU.subtract))
            a(lambda e: e.activation(w1[:, :], w1[:, :], ACT.Exp), lambda e: e.activation(w2[:, :], w2[:, :], ACT.Exp))
            v(lambda e: e.tensor_tensor(inT[:, 1:3, :], inT[:, 1:3, :], bc(w1[:, :], 2, 1), ALU.mult))
            v(*[lambda e, c=c: e.tensor_tensor_scan(mT[k][:, c, 1:], w2[:, :], inT[:, c, :], 0.0, ALU.mult, ALU.add)
                for c in (1, 2)])
            t(*[lambda e, c=c: e.transpose(PS[0:CH, 4 + c, 0:128], mT[k][:, c, 0:CH], ident[:, :]) for c in range(3)])
            v(lambda e: e.tensor_copy(carry[:, :].rearrange("p (c h n) -> p c h n", c=3, h=2)[:, :, k, :],
                                      PS[0:CH, 4:7, 0:128]))
        ch.step("rows", [lambda e: e.indirect_dma_start(got[:, :], None, rows0,
                                                          bass.IndirectOffsetOnAxis(ap=patch_src[:, 0:1], axis=0))], 16)
        v(lambda e: e.tensor_tensor(mt[:, :], got[:, 0:C2], carry[:, 0:C2], ALU.max))
        v(lambda e: e.tensor_tensor(ea[:, 0, :], got[:, 0:C2], mt[:, :], ALU.subtract),
          lambda e: e.tensor_tensor(ea[:, 1, :], carry[:, 0:C2], mt[:, :], ALU.subtract))
        a(lambda e: e.activation(ea[:, :, :], ea[:, :, :], ACT.Exp))
        two_of = lambda ap: ap.rearrange("p (a c) -> p a c", a=2)
        v(lambda e: e.tensor_tensor(two_of(got[:, C2:3 * C2]), two_of(got[:, C2:3 * C2]), bc(ea[:, 0, :], 2, 1), ALU.mult),
          lambda e: e.tensor_tensor(two_of(carry[:, C2:]), two_of(carry[:, C2:]), bc(ea[:, 1, :], 2, 1), ALU.mult))
        v(lambda e: e.tensor_tensor(got[:, C2:3 * C2], got[:, C2:3 * C2], carry[:, C2:], ALU.add),
          lambda e: e.tensor_copy(got[:, 0:C2], mt[:, :]))
        ch.wait(nc.gpsimd)
        nc.gpsimd.nop(nofuse=True)
        ch.step("rows", [lambda e: e.indirect_dma_start(rows0, bass.IndirectOffsetOnAxis(ap=patch_row[:, 0:1], axis=0),
                                                          got[:, :], None, bounds_check=lim0, oob_is_err=False)], 16)
        together()
        L.close()

        L = ExitStack()
        rb = [sb(f"rb{k}", [128, 7, ROW], F32, L) for k in range(7)]
        r_in = [L.enter_context(nc.semaphore(f"r_in{k}")) for k in range(7)]
        ch.wait(nc.sync)
        for k in range(7):
            nc.sync.dma_start(rb[k][:, :, :], rows0_j[:, 7 * k:7 * k + 7, :]).then_inc(r_in[k], 16)
        for k in range(7):
            js = slice(7 * k, 7 * k + 7)
            nc.vector.wait_ge(r_in[k], 16)
            v(lambda e: e.reciprocal(rb[k][:, :, C2:2 * C2], rb[k][:, :, C2:2 * C2]),
              lambda e: e.tensor_copy(end_idx[:, js], rb[k][:, :, 3 * C2]))
            v(lambda e: e.tensor_tensor(rb[k][:, :, C2:2 * C2], rb[k][:, :, C2:2 * C2], rb[k][:, :, 2 * C2:3 * C2],
                                        ALU.mult))
            v(lambda e: e.tensor_reduce(agg[:, js, :], rb[k][:, :, C2:2 * C2].rearrange("p j (i o) -> p j o i", i=D),
                                        X, ALU.add))
        L.close()

        def flat(ap):
            return ap.rearrange("p j f -> p (j f)")

        def add_to(dst, src):
            v(lambda e: e.tensor_tensor(flat(dst[:, :, :]), flat(dst[:, :, :]), flat(src[:, :, :]), ALU.add))

        def layernorm(x, y):
            add_to(x, y)
            v(lambda e: e.tensor_reduce(red[:, :], x[:, :, :], X, ALU.add))
            v(lambda e: e.tensor_scalar(red[:, :], red[:, :], 1.0 / D, None, ALU.mult))
            v(lambda e: e.tensor_tensor(x[:, :, :], x[:, :, :], bc(red[:, :], D, 2), ALU.subtract))
            v(lambda e: e.tensor_tensor(tn[:, :, :], x[:, :, :], x[:, :, :], ALU.mult))
            v(lambda e: e.tensor_reduce(red[:, :], tn[:, :, :], X, ALU.add))
            v(lambda e: e.tensor_scalar(red[:, :], red[:, :], 1.0 / D, EPS, ALU.mult, ALU.add))
            a(lambda e: e.activation(red[:, :], red[:, :], ACT.Sqrt))
            v(lambda e: e.reciprocal(red[:, :], red[:, :]))
            v(lambda e: e.tensor_tensor(x[:, :, :], x[:, :, :], bc(red[:, :], D, 2), ALU.mult))

        def turned(x):
            t(*[lambda e, k=k: e.transpose(PS[:, k // 4, 128 * (k % 4):128 * (k % 4) + 128],
                                           flat(x[:, 8 * k:8 * k + 8, :]), ident[:, :]) for k in range(7)])
            v(lambda e: e.tensor_copy(xT[:, :], PS[:, 0:2, :].rearrange("p b c -> p (b c)")[:, 0:896]))

        def times(w):
            dma(*[lambda e, q=q: e.dma_start(wstage[D * q:D * q + D, :], w) for q in range(8)])
            v(lambda e: e.tensor_tensor(blockdiag[:, :, :], bc(wstage[:, :], 8, 1), bc(group_mask[:, :], D, 2), ALU.mult))
            t(*[lambda e, k=k: e.matmul(PS[:, 2 + k // 4, 128 * (k % 4):128 * (k % 4) + 128],
                                        xT[:, 128 * k:128 * k + 128], blockdiag[:, :, :].rearrange("p g o -> p (g o)"))
                for k in range(7)])
            return PS[:, 2:4, :].rearrange("p b c -> p (b c)")[:, 0:896]

        def row_of(w):
            dma(lambda e: e.dma_start(row_b[:, :], w.rearrange("(a n) -> a n", a=1).to_broadcast([128, D])))
            return bc(row_b[:, :], NJ, 1)

        layernorm(xn, agg)

        coef_sb = sb("coef", [CH, T, 8])
        L = ExitStack()
        tyi = sb("tyi", [CH, T], I32, L)
        ty = sb("ty", [CH, T], F32, L)
        isf = sb("isf", [CH, T], F32, L)
        isl = sb("isl", [CH, T], F32, L)
        cnt = sb("cnt", [CH, T], F32, L)
        lastp = sb("lastp", [CH, 8], F32, L)
        firstp = sb("firstp", [CH, 8], F32, L)
        more = sb("more", [CH, 2, 8], F32, L)
        q_ = [sb(f"q{k}", [CH, CH], F32, L) for k in range(4)]
        lt = sb("lt", [CH, CH], F32, L)
        gt = sb("gt", [CH, CH], F32, L)
        fr = sb("fr", [CH, CH], F32, L)
        lr = sb("lr", [CH, CH], F32, L)
        dg = sb("dg", [CH, CH], F32, L)
        v(lambda e: e.memset(lt[:, :], 1.0), lambda e: e.memset(gt[:, :], 1.0))
        g(lambda e: e.affine_select(out=lt[:, :], in_=lt[:, :], compare_op=ALU.is_gt, fill=0.0,
                                    base=0, pattern=[[1, CH]], channel_multiplier=-1),
          lambda e: e.affine_select(out=gt[:, :], in_=gt[:, :], compare_op=ALU.is_gt, fill=0.0,
                                    base=0, pattern=[[-1, CH]], channel_multiplier=1))
        dma(lambda e: e.dma_start(tyi[:, :], io["edge_type_8"].rearrange("(p t) -> p t", p=CH)))
        for src_, dst_ in ((first_of, fr), (last_of, lr)):
            v(lambda e: e.tensor_scalar(dg[:, :], ident[0:CH, 0:CH], src_[:, 0:1], None, ALU.mult))
            t(lambda e: e.matmul(PS[0:CH, 0, 0:CH], ones[0:CH, 0:CH], dg[:, :]))
            v(lambda e: e.tensor_copy(dst_[:, :], PS[0:CH, 0, 0:CH]))
        spec = [(fr, last_of, lt), (fr, first_of, gt), (lr, last_of, lt), (lr, first_of, gt)]
        v(*[lambda e, k=k: e.tensor_scalar(q_[k][:, :], spec[k][0][:, :], spec[k][1][:, 0:1], None, ALU.is_equal)
            for k in range(4)], lambda e: e.tensor_copy(ty[:, :], tyi[:, :]),
          lambda e: e.tensor_scalar(isf[:, :], dstf[:, :], first_of[:, 0:1], None, ALU.is_equal),
          lambda e: e.tensor_scalar(isl[:, :], dstf[:, :], last_of[:, 0:1], None, ALU.is_equal))
        v(*[lambda e, k=k: e.tensor_tensor(q_[k][:, :], q_[k][:, :], spec[k][2][:, :], ALU.mult) for k in range(4)],
          lambda e: e.tensor_tensor(isl[:, :], isl[:, :], isf[:, :], ALU.is_gt))
        for r in range(8):
            cr = coef_sb[:, :, r]
            v(lambda e: e.tensor_scalar(cnt[:, :], ty[:, :], float(r), None, ALU.is_equal))
            v(lambda e: e.tensor_tensor_scan(cnt[:, :], keep[:, 0:T], cnt[:, :], 0.0, ALU.mult, ALU.add))
            v(lambda e: e.tensor_copy(lastp[:, r:r + 1], cnt[:, T - 1:T]),
              lambda e: e.tensor_tensor_scan(cr[:, ::-1], keep[:, 1:T + 1][:, ::-1], cnt[:, ::-1], 0.0, ALU.mult, ALU.max))
            v(lambda e: e.tensor_copy(firstp[:, r:r + 1], cr[:, 0:1]))
        t(lambda e: e.matmul(PS[0:CH, 0, 0:8], q_[0][:, :], lastp[:, :], start=True, stop=False),
          lambda e: e.matmul(PS[0:CH, 1, 0:8], q_[2][:, :], lastp[:, :], start=True, stop=False))
        t(lambda e: e.matmul(PS[0:CH, 0, 0:8], q_[1][:, :], firstp[:, :], start=False, stop=True),
          lambda e: e.matmul(PS[0:CH, 1, 0:8], q_[3][:, :], firstp[:, :], start=False, stop=True))
        v(lambda e: e.tensor_copy(more[:, :, :], PS[0:CH, 0:2, 0:8]))
        sel = sb("sel", [CH, T], F32, L)
        v(lambda e: e.memset(sel[:, :], 0.0))
        for r in range(8):
            cr = coef_sb[:, :, r]
            v(lambda e: e.scalar_tensor_tensor(out=cr, in0=isf[:, :], scalar=more[:, 0, r:r + 1], in1=cr,
                                               op0=ALU.mult, op1=ALU.add))
            v(lambda e: e.scalar_tensor_tensor(out=cr, in0=isl[:, :], scalar=more[:, 1, r:r + 1], in1=cr,
                                               op0=ALU.mult, op1=ALU.add))
            v(lambda e: e.scalar_tensor_tensor(out=cnt[:, :], in0=ty[:, :], scalar=float(r), in1=cr,
                                               op0=ALU.is_equal, op1=ALU.mult))
            v(lambda e: e.tensor_tensor(sel[:, :], sel[:, :], cnt[:, :], ALU.add))
        v(lambda e: e.tensor_scalar(sel[:, :], sel[:, :], 1.0, None, ALU.max))
        v(lambda e: e.reciprocal(sel[:, :], sel[:, :]))
        v(*[lambda e, r=r: e.scalar_tensor_tensor(out=coef_sb[:, :, r], in0=ty[:, :], scalar=float(r), in1=sel[:, :],
                                                  op0=ALU.is_equal, op1=ALU.mult) for r in range(8)])
        together()
        L.close()

        wc = sb("wc", [128, D])
        patch_g = sb("patch_g", [CH, D])
        parts = sb("parts", [128, 3, KT, A9 * D], BF16)
        pick = sb("pick", [128, KT], F32)
        pick_row = sb("pick_row", [128, 1], F32)
        fold = sb("fold", [128, 2, D], F32)
        g(lambda e: e.iota(pick[:, :], pattern=[[128, KT]], base=0, channel_multiplier=1,
                           allow_small_or_imprecise_dtypes=True))
        dma(*[lambda e, q=q: e.dma_start(fold[D * q:D * q + D, 0, :], ident[0:D, 0:D]) for q in range(8)])
        gi = sb("gi", [128, 8], F32)
        g(lambda e: e.iota(gi[:, :], pattern=[[1, 8]], base=0, channel_multiplier=0,
                           allow_small_or_imprecise_dtypes=True))
        v(lambda e: e.tensor_tensor(gi[:, :], gi[:, :], group_mask[:, :], ALU.mult))
        v(lambda e: e.tensor_reduce(pick_row[:, :], gi[:, :], X, ALU.add))
        lim_s = nc.gpsimd.to_reg(E - 1)

        def split_parts(x):
            r = tn[:, 0:JT, :].rearrange("p (a c) f -> p c a f", c=KT)
            xv = x[:, 0:JT, :].rearrange("p (a c) f -> p c a f", c=KT)
            pv = lambda n, c: parts[:, n, c, :].rearrange("p (a f) -> p a f", a=A9)
            src_ = xv
            for n in range(3):
                v(*[lambda e, c=c: e.tensor_copy(pv(n, c), src_[:, c, :, :]) for c in range(KT)])
                if n < 2:
                    v(*[lambda e, c=c: e.tensor_tensor(r[:, c, :, :], src_[:, c, :, :], pv(n, c), ALU.subtract)
                        for c in range(KT)])
                src_ = r

        s_row = sem("s_row")
        pieces = [0]

        def expand_nodes(name, x, weights, always=None):
            R = 9 if always is not None else 8
            table = table9 if always is not None else table8
            L = ExitStack()
            wst = sb(f"{name}wst", [128, R, D], F32, L)
            wide = sb(f"{name}wide", [128, 8, R * D], F32, L)
            rows = sb(f"{name}rows", [128, NJ, R * D], F32, L)
            dma(*[lambda e, q=q: e.dma_start(wst[D * q:D * q + D, 0:8, :], weights) for q in range(8)])
            if always is not None:
                dma(*[lambda e, q=q: e.dma_start(wst[D * q:D * q + D, 8, :], always) for q in range(8)])
                v(lambda e: e.tensor_copy(fold[:, 1, :], wst[:, 8, :]))
            v(*[lambda e, q=q: e.tensor_scalar(wide[:, q, :], wst[:, :, :].rearrange("p r o -> p (r o)"),
                                               group_mask[:, q:q + 1], None, ALU.mult) for q in range(8)])
            turned(x)
            for k in range(7):
                at = 4 * (k % 2)
                t(*[lambda e, q=q: e.matmul(PS[:, at + q, 0:2 * R * D], xT[:, 128 * k:128 * k + 128],
                                            wide[:, 2 * q:2 * q + 2, :].rearrange("p s n -> p (s n)"))
                    for q in range(4)])
                v(lambda e: e.tensor_copy(rows[:, 8 * k:8 * k + 8, :].rearrange("p (q s) n -> p q (s n)", s=2),
                                          PS[:, at:at + 4, 0:2 * R * D]))
                ch.wait(nc.sync)
                n = min(JT - 8 * k, 8)
                nc.sync.dma_start(table.rearrange("(j p) f -> p j f", p=128)[:, 8 * k:8 * k + n, :],
                                  rows[:, 8 * k:8 * k + n, :]).then_inc(s_row, 16)
                pieces[0] += 1
            nc.sync.wait_ge(s_row, 16 * pieces[0])
            together()
            L.close()

        def conv(name, index, both=False, by_source=None):
            L = ExitStack()
            lsem = lambda n: L.enter_context(nc.semaphore(f"{name}_{n}"))
            help_ = by_source is None
            hb = HB if help_ else 0
            NG = TB - hb
            R = 9 if both else 8
            W2 = 2 * D if both else D
            table = table9 if both else table8
            ix = [sb(f"{name}ix{k}", [CH, TB], I32, L) for k in two]
            yg = [sb(f"{name}yg{k}", [CH, NG, R * D], F32, L) for k in two]
            msg = [sb(f"{name}msg{k}", [CH, TB, D], F32, L) for k in two]
            c_ix = [lsem(f"ix{k}") for k in two]
            c_g = [lsem(f"g{k}") for k in two]
            c_rd = lsem("rd")
            G = TB // 4
            index_c = index.rearrange("(p t) -> p t", p=CH)
            sums_c = sums[0:E, :].rearrange("(p t) f -> p t f", p=CH)
            if help_:
                c_st = [lsem(f"st{k}") for k in two]
                c_z, c_tr, c_zt, c_mm = lsem("z"), lsem("tr"), lsem("zt"), lsem("mm")
                c_add, c_run = lsem("add"), lsem("run")
                z = [sb(f"{name}z{k}", [CH, 4, 128], F32, L) for k in range(HG)]
                zt = [sb(f"{name}zt{k}", [128, 4 * CH], F32, L) for k in two]
                pk = [sb(f"{name}pk{k}", [CH, HB, W2], F32, L) for k in two]
                run = [sb(f"{name}run{k}", [CH, TB, D], F32, L) for k in two]
                hot_ = [sb(f"{name}hot{k}", [128, KT, HB * 128], BF16, L) for k in two]
                ra = [sb(f"{name}ra{k}", [128, HB * 128], I16, L) for k in two]
                rb2 = [sb(f"{name}rb{k}", [128, HB * 128], I16, L) for k in two]
                mx = [sb(f"{name}mx{k}", [A9 * D, 512], F32, L) for k in two]
                h_row = [lsem(f"hrow{k}") for k in two]
                h_oh, h_g, h_mk, h_sel, h_cp = lsem("oh"), lsem("pg"), lsem("mk"), lsem("sel"), lsem("cp")
                v(*[lambda e, k=k: e.memset(run[k][:, :, :], 0.0) for k in two])
            else:
                av, bv = by_source
                ms = sb("ms", [CH, TB, D], F32, L)
                c_ms = lsem("ms")
                bst = sb("bst", [CH, TB], F32, L)
                lhs = [sb(f"lhs{k}", [CH, 4, 3, 128], BF16, L) for k in two]
                m3 = [sb(f"m3{k}", [CH, TB, 3, D], BF16, L) for k in two]
                mkx = [sb(f"mkx{k}", [CH, TB, 8, D], BF16, L) for k in two]
                hot = [sb(f"hot{k}", [CH, A7], BF16, L) for k in range(8)]
                io8 = sb("io8", [CH, 8], F32, L)
                mkb = sb("mkb", [CH, TB, 8], BF16, L)
                iob = sb("iob", [CH, A7], I16, L)
                zz = sb("zz", [CH, A7], BF16, L)
                c_mk, c_mkx, c_bk, c_m3 = lsem("mk"), lsem("mkx"), lsem("bk"), lsem("m3")
                c_lhs, c_hot, c_ag = lsem("lhs"), lsem("hot"), lsem("ag")
                g(lambda e: e.iota(io8[:, :], pattern=[[1, 8]], base=0, channel_multiplier=0,
                                   allow_small_or_imprecise_dtypes=True),
                  lambda e: e.iota(iob[:, :], pattern=[[1, A7]], base=0, channel_multiplier=0,
                                   allow_small_or_imprecise_dtypes=True))
                v(lambda e: e.memset(zz[:, :], 0.0))
                t(*[lambda e, k=k: e.matmul(PS[:, 6 + k, 0:A7 // 2], zz[:, 0:128], zz[:, 0:A7 // 2],
                                            start=True, stop=False) for k in two])
            together()

            def load_ix(b):
                wait(nc.sync, c_g[b.k], b.slot(16 * NG, 0))
                sp_load(ix[b.k][:, :], index_c[:, b.cols()], c_ix[b.k])

            def load_rows(b):
                wait(nc.sync, h_mk, b.next(-1).count(HG, 0))
                at = b.i * (2 * TB) + (b.k * TB + TB - HB)
                for dst_, src_ in ((ra, pick_a), (rb2, pick_b)):
                    sp_load(dst_[b.k][:, :], src_[bass.ds(at, HB), :].rearrange("(a t) c -> a (t c)", a=1)
                            .to_broadcast([128, HB * 128]), h_row[b.k])

            def sp_first(b):
                load_ix(b)
                if help_:
                    load_rows(b)
                    load_rows(b.next(1))

            def sp(b):
                if b.next(1).exists():
                    load_ix(b.next(1))
                if help_:
                    if b.next(2).exists():
                        load_rows(b.next(2))
                    wait(nc.sync, c_run, b.count(D, D))
                    sp_load(sums_c[:, b.cols(), :], run[b.k][:, :, :], c_st[b.k])

            loop(nc.sync, sp, NB, TB, before=sp_first)

            def gather(b):
                wait(nc.gpsimd, c_ix[b.k], b.slot(16, 16))
                wait(nc.gpsimd, c_rd, b.next(-1).count(2, 0))
                for q in range(NG):
                    nc.gpsimd.indirect_dma_start(yg[b.k][:, q, :], None, table,
                                                 bass.IndirectOffsetOnAxis(ap=ix[b.k][:, q:q + 1], axis=0))\
                        .then_inc(c_g[b.k], 16)

            loop(nc.gpsimd, gather, NB, TB)

            def par(b, q):
                return (HG * b.k + q) % 2

            def pick_rows(b, n):
                q, third = n // 3, n % 3
                if third == 0:
                    wait(nc.tensor, h_oh, b.count(KT, KT))
                    wait(nc.tensor, h_mk, b.count(HG, q - 1))
                for m in range(KT * third, KT * third + KT):
                    mm = nc.tensor.matmul(PS[0:A9 * D, 4 + par(b, q), :], parts[:, m % 3, m // 3, :],
                                          hot_[b.k][:, m // 3, 512 * q:512 * q + 512],
                                          start=(m == 0), stop=(m == 3 * KT - 1))
                if third == 2:
                    mm.then_inc(h_g, 1)

            def fold_rows(b, q):
                wait(nc.tensor, h_mk, b.count(HG, q + 1))
                wait(nc.tensor, h_cp, b.count(HG, q - 1))
                for r in range(4):
                    mm = nc.tensor.matmul(PS[:, 6 + par(b, q), W2 * r:W2 * r + W2],
                                          mx[par(b, q)][:, 128 * r:128 * r + 128],
                                          fold[0:A9 * D, 0:W2 // D, :].rearrange("p a o -> p (a o)"))
                mm.then_inc(h_sel, 1)

            def turn_z(b, q):
                wait(nc.tensor, c_z, b.count(HG, q + 1))
                wait(nc.tensor, c_zt, b.count(HG, q - 1))
                for r in range(4):
                    mm = nc.tensor.transpose(PS[:, par(b, q), r * CH:r * CH + CH], z[q][:, r, :], ident[0:CH, 0:CH])
                mm.then_inc(c_tr, 1)

            def multiply(b, q):
                wait(nc.tensor, c_zt, b.count(HG, q + 1))
                if q == 0:
                    wait(nc.tensor, c_add, b.next(-1).count(1, 0))
                for r in range(4):
                    o = (4 * q + r) * D
                    mm = nc.tensor.matmul(PS[0:CH, 2 + b.k, o:o + D], zt[par(b, q)][:, r * CH:r * CH + CH], wc[:, :])
                mm.then_inc(c_mm, 1)

            def spread(b, q):
                wait(nc.tensor, c_lhs, b.count(3 * G, 3 * q + 3))
                for r in range(4):
                    wait(nc.tensor, c_hot, b.count(TB, 4 * q + r + 1))
                    for part in range(3):
                        for k in two:
                            mm = nc.tensor.matmul(PS[:, 6 + k, 0:A7 // 2], lhs[q % 2][:, r, part, :],
                                                  hot[4 * (q % 2) + r][:, k * A7 // 2:(k + 1) * A7 // 2],
                                                  start=False, stop=False)
                    mm.then_inc(c_ag, 1)

            def pe(b):
                if help_:
                    nx = b.next(1) if b.next(1).exists() else None
                    for n in range(3 * HG):
                        if nx:
                            pick_rows(nx, n)
                        if n == 0:
                            fold_rows(b, HG - 1)
                        if n in (2, 3, 4):
                            turn_z(b, n - 2)
                        if n in (4, 5, 6):
                            multiply(b, n - 4)
                        if n == 7 and nx:
                            fold_rows(nx, 0)
                    if nx:
                        fold_rows(nx, 1)
                else:
                    pv_ = b.next(-1) if b.next(-1).exists() else None
                    if pv_:
                        for q in range(G):
                            spread(pv_, q)

            def pe_first(b):
                for q in range(HG):
                    for n in range(3):
                        pick_rows(b, 3 * q + n)
                    if q:
                        fold_rows(b, q - 1)

            def pe_last(b):
                for q in range(G):
                    spread(b, q)

            loop(nc.tensor, pe, NB, TB, before=pe_first if help_ else None, after=None if help_ else pe_last)

            def copy_rows(b, q):
                wait(nc.scalar, h_sel, b.count(HG, q + 1))
                wait(nc.scalar, c_add, b.next(-1).count(1, 0))
                nc.scalar.activation(pk[b.k][:, 4 * q:4 * q + 4, :].rearrange("p t f -> p (t f)"),
                                     PS[0:CH, 6 + par(b, q), 0:4 * W2], ACT.Copy).then_inc(h_cp, 1)

            def act(b):
                if help_:
                    copy_rows(b, HG - 1)
                    for q in range(HG):
                        wait(nc.scalar, c_tr, b.count(HG, q + 1))
                        wait(nc.scalar, c_mm, b.count(HG, q - 1))
                        nc.scalar.activation(zt[par(b, q)][:, :], PS[:, par(b, q), 0:4 * CH], ACT.Copy)\
                            .then_inc(c_zt, 1)
                    if b.next(1).exists():
                        copy_rows(b.next(1), 0)
                        copy_rows(b.next(1), 1)
                else:
                    wait(nc.scalar, c_mk, b.count(1, 1))
                    wait(nc.scalar, c_lhs, b.next(-1).count(3 * G, 0))
                    nc.scalar.activation(mkx[b.k][:, :, :, :].rearrange("p t a f -> p (t a) f"),
                                         bc(mkb[:, :, :].rearrange("p t a -> p (t a)"), D, 2),
                                         ACT.Copy).then_inc(c_mkx, 1)
                    wait(nc.scalar, c_rd, b.count(2, 2))
                    wait(nc.scalar, c_ms, b.count(4, 0))
                    nc.scalar.activation(ms[:, :, :], msg[b.k][:, :, :], ACT.Silu,
                                         scale=(D * 8) ** -0.5).then_inc(c_ms, 1)
                    for n in range(3):
                        if n:
                            wait(nc.scalar, c_m3, b.count(2, n))
                        else:
                            wait(nc.scalar, c_ms, b.count(4, 1))
                        nc.scalar.activation(m3[b.k][:, :, n, :], ms[:, :, :], ACT.Copy).then_inc(c_ms, 1)

            def act_first(b):
                copy_rows(b, 0)
                copy_rows(b, 1)

            loop(nc.scalar, act, NB, TB, before=act_first if help_ else None)

            def one_hot(b):
                wait(V, h_row[b.k], b.slot(32, 32))
                wait(V, h_g, b.next(-1).count(HG, 0))
                for c in range(KT):
                    V.tensor_scalar(hot_[b.k][:, c, :], rb2[b.k][:, :], pick[:, c:c + 1], None, ALU.is_equal)\
                        .then_inc(h_oh, 1)

            def mask(b, q):
                wait(V, h_g, b.count(HG, q + 1))
                wait(V, h_sel, b.count(HG, q - 1))
                V.scalar_tensor_tensor(out=mx[par(b, q)][:, :], in0=ra[b.k][0:A9 * D, 512 * q:512 * q + 512],
                                       scalar=pick_row[0:A9 * D, 0:1], in1=PS[0:A9 * D, 4 + par(b, q), :],
                                       op0=ALU.is_equal, op1=ALU.mult).then_inc(h_mk, 1)

            def outer(b):
                for q in range(HG):
                    wait(V, h_cp, b.count(HG, q + 1))
                    wait(V, c_tr, b.count(HG, q - 2))
                    co = coef_sb[:, bass.ds(b.i * (2 * TB) + (b.k * TB + NG + 4 * q), 4), :]
                    V.tensor_tensor(z[q][:, :, :].rearrange("p t (r i) -> p t r i", r=8),
                                    bc(pk[b.k][:, 4 * q:4 * q + 4, 0:D], 8, 2), bc(co, D, 3), ALU.mult)\
                        .then_inc(c_z, 1)

            def scale_rows(b):
                wait(V, c_g[b.k], b.slot(16 * NG, 16 * NG))
                prods = yg[b.k][:, :, 0:8 * D].rearrange("p t (r o) -> p t r o", r=8)
                co = coef_sb[:, bass.ds(b.i * (2 * TB) + b.k * TB, NG), :]
                V.tensor_tensor(prods, prods, bc(co, D, 3), ALU.mult).then_inc(c_rd, 1)

            def add_up(b):
                wait(V, c_rd, b.count(2, 1))
                if help_:
                    wait(V, c_run, b.next(-1).count(D, 0))
                else:
                    wait(V, c_ms, b.next(-1).count(4, 0))
                V.tensor_reduce(msg[b.k][:, 0:NG, :], yg[b.k][:, :, :].rearrange("p t (r o) -> p t o r", r=R),
                                X, ALU.add).then_inc(c_rd, 1)

            def picked_messages(b):
                wait(V, c_mm, b.count(HG, HG))
                wait(V, c_run, b.next(-1).count(D, 0))
                prods = PS[0:CH, 2 + b.k, 0:HB * D].rearrange("p (t f) -> p t f", f=D)
                if both:
                    wait(V, h_cp, b.count(HG, HG))
                    V.tensor_tensor(msg[b.k][:, NG:, :], prods, pk[b.k][:, :, D:], ALU.add).then_inc(c_add, 1)
                else:
                    V.tensor_copy(msg[b.k][:, NG:, :], prods).then_inc(c_add, 1)

            def dve_first(b):
                one_hot(b)
                for q in range(HG):
                    mask(b, q)
                one_hot(b.next(1))

            def by_destination(b):
                wait(V, c_rd, b.count(2, 2))
                wait(V, c_add, b.count(1, 1))
                wait(V, c_run, b.count(D, 0))
                wait(V, c_st[b.k], b.slot(16, 0))
                for f in range(D):
                    V.tensor_tensor_scan(run[b.k][:, :, f], keep[:, b.cols()], msg[b.k][:, :, f],
                                         run[1 - b.k][:, TB - 1, f:f + 1], ALU.mult, ALU.add).then_inc(c_run, 1)

            def masks(b):
                wait(V, c_mkx, b.count(1, 0))
                V.tensor_tensor(mkb[:, :, :], bc(av[:, b.cols()], 8, 2), bc(io8[:, :], TB, 1), ALU.is_equal)\
                    .then_inc(c_mk, 1)

            def less_part(b, n):
                wait(V, c_ms, b.count(4, 2 + n))
                V.tensor_tensor(ms[:, :, :], ms[:, :, :], m3[b.k][:, :, n, :], ALU.subtract).then_inc(c_m3, 1)

            def scatter_operands(b, q):
                if q == 0:
                    wait(V, c_bk, b.count(1, 1))
                    wait(V, c_mkx, b.count(1, 1))
                    wait(V, c_ms, b.count(4, 4))
                wait(V, c_ag, b.count(TB, 4 * q - 4))
                for n in range(3):
                    V.tensor_tensor(lhs[q % 2][:, :, n, :].rearrange("p t (a f) -> p t a f", a=8),
                                    mkx[b.k][:, 4 * q:4 * q + 4, :, :],
                                    bc(m3[b.k][:, 4 * q:4 * q + 4, n, :], 8, 2), ALU.mult).then_inc(c_lhs, 1)
                for r in range(4):
                    wait(V, c_ag, b.count(TB, 4 * q + r - 7))
                    V.tensor_scalar(hot[4 * (q % 2) + r][:, :], iob[:, :], bst[:, 4 * q + r:4 * q + r + 1], None,
                                    ALU.is_equal).then_inc(c_hot, 1)

            def dve(b):
                if help_:
                    nx = b.next(1) if b.next(1).exists() else None
                    outer(b)
                    if nx:
                        mask(nx, 0)
                    scale_rows(b)
                    if b.next(2).exists():
                        one_hot(b.next(2))
                    add_up(b)
                    if nx:
                        mask(nx, 1)
                    picked_messages(b)
                    by_destination(b)
                    if nx:
                        mask(nx, 2)
                else:
                    pv_ = b.next(-1) if b.next(-1).exists() else None
                    masks(b)
                    for q in range(G):
                        if q == 2:
                            scale_rows(b)
                        if pv_:
                            scatter_operands(pv_, q)
                        if q == 4:
                            add_up(b)
                        if q in (5, 6):
                            less_part(b, q - 5)
                    wait(V, c_hot, b.count(TB, 0))
                    V.tensor_copy(bst[:, :], bv[:, b.cols()]).then_inc(c_bk, 1)

            def dve_last(b):
                for q in range(G):
                    scatter_operands(b, q)

            loop(V, dve, NB, TB, before=dve_first if help_ else None, after=None if help_ else dve_last)
            if by_source is None:
                for k in two:
                    nc.sync.wait_ge(c_st[k], 16 * NB // 2)
            together()

            if by_source is None:
                t(lambda e: e.matmul(PS[0:CH, 0, 0:D], before[:, :], run[1][:, TB - 1, :]))
                ch.step("rows", [lambda e: e.indirect_dma_start(
                    patch_g[:, 0:D], None, sums, bass.IndirectOffsetOnAxis(ap=patch_sum_src[:, 0:1], axis=0))], 16)
                v(lambda e: e.tensor_tensor(patch_g[:, 0:D], patch_g[:, 0:D], PS[0:CH, 0, 0:D], ALU.add))
                ch.wait(nc.gpsimd)
                nc.gpsimd.nop(nofuse=True)
                ch.step("rows", [lambda e: e.indirect_dma_start(
                    sums, bass.IndirectOffsetOnAxis(ap=patch_sum[:, 0:1], axis=0), patch_g[:, 0:D], None,
                    bounds_check=lim_s, oob_is_err=False)], 16)
                ch.wait(nc.gpsimd)
                nc.gpsimd.nop(nofuse=True)
                ch.step("rows", [lambda e, j=j: e.indirect_dma_start(
                    agg[:, j, :], None, sums, bass.IndirectOffsetOnAxis(ap=end_idx[:, j:j + 1], axis=0))
                    for j in range(JT)], 16)
            else:
                t(*[lambda e, k=k: e.matmul(PS[:, 6 + k, 0:A7 // 2], zz[:, 0:128], zz[:, 0:A7 // 2],
                                            start=False, stop=True) for k in two])
                big = sb("big", [128, A7], F32, L)
                nm = sb("nm", [128, 7, 128], F32, L)
                v(*[lambda e, k=k: e.tensor_copy(big[:, k * A7 // 2:(k + 1) * A7 // 2], PS[:, 6 + k, 0:A7 // 2])
                    for k in two])
                sizes = [min(128, A7 - 128 * k) for k in range(7)]
                t(*[lambda e, k=k: e.transpose(PS[0:sizes[k], k // 4, 128 * (k % 4):128 * (k % 4) + 128],
                                               big[:, 128 * k:128 * k + sizes[k]], ident[:, :]) for k in range(7)])
                v(*[lambda e, k=k: e.tensor_copy(nm[0:sizes[k], k, :],
                                                 PS[0:sizes[k], k // 4, 128 * (k % 4):128 * (k % 4) + 128])
                    for k in range(7)])
                aggd_v = aggd.rearrange("(a b) f -> b a f", a=8)
                dma(*[lambda e, k=k: e.dma_start(aggd_v[128 * k:128 * k + sizes[k], :, :],
                                                 nm[0:sizes[k], k, :].rearrange("p (a f) -> p a f", a=8))
                      for k in range(7)])
                dma(lambda e: e.dma_start(agg[:, 0:JT, :], aggd.rearrange("(j p) f -> p j f", p=128)))
            together()
            L.close()

        def log_softmax(x):
            v(lambda e: e.tensor_reduce(red[:, :], x[:, :, :], X, ALU.max))
            v(lambda e: e.tensor_tensor(x[:, :, :], x[:, :, :], bc(red[:, :], D, 2), ALU.subtract))
            a(lambda e: e.activation(tn[:, :, :], x[:, :, :], ACT.Exp))
            v(lambda e: e.tensor_reduce(red[:, :], tn[:, :, :], X, ALU.add))
            a(lambda e: e.activation(red[:, :], red[:, :], ACT.Ln))
            v(lambda e: e.tensor_tensor(x[:, :, :], x[:, :, :], bc(red[:, :], D, 2), ALU.subtract))

        h1 = xn
        for n, (W, root, bias) in enumerate((("W1", "root1", "b1"), ("W2", "root2", "b2"))):
            expand_nodes(f"e1{n}", h1, io["L1_gnn_" + W].rearrange("r i o -> i r o"))
            dma(lambda e: e.dma_start(wc[:, :], io["L1_gnn_" + W].rearrange("r i o -> (r i) o")))
            split_parts(h1)
            conv(f"r{n}", io["src"])
            turned(h1)
            ps = times(io["L1_gnn_" + root])
            v(lambda e: e.tensor_tensor(flat(hn[:, :, :]), flat(agg[:, :, :]), ps, ALU.add))
            rb_ = row_of(io["L1_gnn_" + bias])
            v(lambda e: e.tensor_tensor(hn[:, :, :], hn[:, :, :], rb_, ALU.add))
            if n == 0:
                v(lambda e: e.tensor_scalar(hn[:, :, :], hn[:, :, :], 0.0, None, ALU.max))
            h1 = hn
        log_softmax(hn)
        layernorm(xn, hn)

        dma(lambda e: e.dma_start(coef_sb[:, :, :], io["edge_attr_8"].rearrange("(p t) f -> p t f", p=CH)))
        L2 = ExitStack()
        av = sb("av", [CH, T], F32, L2)
        bv = sb("bv", [CH, T], F32, L2)
        sr = ExitStack()
        si = sb("si", [CH, T], I32, sr)
        dma(lambda e: e.dma_start(si[:, :], src_c))
        v(lambda e: e.tensor_copy(bv[:, :], si[:, :]))
        v(lambda e: e.tensor_scalar(av[:, :], bv[:, :], float(A7), None, ALU.is_ge))
        for k in range(2, 8):
            v(lambda e: e.scalar_tensor_tensor(out=av[:, :], in0=bv[:, :], scalar=float(k * A7), in1=av[:, :],
                                               op0=ALU.is_ge, op1=ALU.add))
        v(lambda e: e.scalar_tensor_tensor(out=bv[:, :], in0=av[:, :], scalar=-float(A7), in1=bv[:, :],
                                           op0=ALU.mult, op1=ALU.add))
        sr.close()
        expand_nodes("e2", xn, io["L2_gnn_W_msg_tp"])
        conv("m", io["dst"], by_source=(av, bv))
        turned(agg)
        ps = times(io["L2_gnn_W_msg_lin"])
        v(lambda e: e.tensor_scalar(flat(agg[:, :, :]), ps, D ** -0.5, None, ALU.mult))
        zu = sb("zu", [128, 2 * C2], F32, L2)
        zuT = sb("zuT", [128, 4, 128], F32, L2)
        wu = sb("wu", [128, 2, D], F32, L2)
        dma(lambda e: e.dma_start(wu[:, :, :], io["L2_gnn_W_upd_tp"].rearrange("(a i) h k -> (i h) a k", a=2)))
        for j in range(0, NJ, 2):
            v(lambda e: e.tensor_tensor(zu[:, :].rearrange("p (j i h) -> p j i h", j=2, i=D),
                                        bc(xn[:, j:j + 2, :], D, 3), bc(agg[:, j:j + 2, :], D, 2), ALU.mult))
            t(*[lambda e, k=k: e.transpose(PS[:, 0, 128 * k:128 * k + 128], zu[:, 128 * k:128 * k + 128], ident[:, :])
                for k in range(4)])
            v(lambda e: e.tensor_copy(zuT[:, :, :].rearrange("p a c -> p (a c)"), PS[:, 0, :]))
            t(*[lambda e, k=k: e.matmul(PS[:, 4 + k // 2, (j // 2) * D:(j // 2) * D + D], zuT[:, k, :], wu[:, k % 2, :],
                                        start=(k % 2 == 0), stop=(k % 2 == 1)) for k in range(4)])
        v(*[lambda e, k=k: e.tensor_copy(hn[:, k::2, :], PS[:, 4 + k, 0:NJ // 2 * D].rearrange("p (j f) -> p j f", f=D))
            for k in two])
        a(lambda e: e.activation(hn[:, :, :], hn[:, :, :], ACT.Silu, scale=1.0 / 16))
        turned(hn)
        ps = times(io["L2_gnn_W_upd_lin"])
        v(lambda e: e.scalar_tensor_tensor(out=flat(hn[:, :, :]), in0=ps, scalar=D ** -0.5, in1=flat(xn[:, :, :]),
                                           op0=ALU.mult, op1=ALU.add))
        layernorm(xn, hn)
        together()
        L2.close()

        h3 = xn
        part = sb("part", [128, D])
        mean = sb("mean", [128, D])
        for n in range(3):
            expand_nodes(f"e3{n}", h3, io["L3_gnn_edge_w"][n, :, :].rearrange("j (i o) -> i j o", i=D),
                         io["L3_gnn_edge_b"][n, :].rearrange("(i o) -> i o", i=D))
            split_parts(h3)
            dma(lambda e: e.dma_start(wc[:, :], io["L3_gnn_edge_w"][n, :, :].rearrange("j (i o) -> (j i) o", i=D)))
            conv(f"c{n}", io["src"], both=True)
            turned(h3)
            ps = times(io["L3_gnn_root_w"][n, :, :])
            v(lambda e: e.tensor_tensor(flat(hn[:, :, :]), flat(agg[:, :, :]), ps, ALU.add))
            rb_ = row_of(io["L3_gnn_root_b"][n, :])
            v(lambda e: e.tensor_tensor(hn[:, :, :], hn[:, :, :], rb_, ALU.add))

            def column_mean():
                v(lambda e: e.tensor_tensor(tn[:, :, :], tn[:, :, :], bc(valid[:, :], D, 2), ALU.mult))
                v(lambda e: e.tensor_reduce(part[:, :], tn[:, :, :].rearrange("p j f -> p f j"), X, ALU.add))
                t(lambda e: e.matmul(PS[:, 0, 0:D], ones[:, :], part[:, :]))
                v(lambda e: e.tensor_scalar(mean[:, :], PS[:, 0, 0:D], 1.0 / N, None, ALU.mult))

            if n < 2:
                v(lambda e: e.tensor_copy(tn[:, :, :], hn[:, :, :]))
                column_mean()
                v(lambda e: e.tensor_tensor(hn[:, :, :], hn[:, :, :], bc(mean[:, :], NJ, 1), ALU.subtract))
                v(lambda e: e.tensor_tensor(tn[:, :, :], hn[:, :, :], hn[:, :, :], ALU.mult))
                column_mean()
                v(lambda e: e.tensor_scalar(mean[:, :], mean[:, :], EPS, None, ALU.add))
                a(lambda e: e.activation(mean[:, :], mean[:, :], ACT.Sqrt))
                v(lambda e: e.reciprocal(mean[:, :], mean[:, :]))
                row_of(io["L3_gnn_bn_gamma"][n, :])
                v(lambda e: e.tensor_tensor(mean[:, :], mean[:, :], row_b[:, :], ALU.mult))
                v(lambda e: e.tensor_tensor(hn[:, :, :], hn[:, :, :], bc(mean[:, :], NJ, 1), ALU.mult))
                rb_ = row_of(io["L3_gnn_bn_beta"][n, :])
                v(lambda e: e.tensor_tensor(hn[:, :, :], hn[:, :, :], rb_, ALU.add))
            v(lambda e: e.tensor_scalar(hn[:, :, :], hn[:, :, :], 0.0, None, ALU.max))
            h3 = hn
        turned(hn)
        ps = times(io["L3_gnn_pred_w"])
        rb_ = row_of(io["L3_gnn_pred_b"])
        v(lambda e: e.tensor_tensor(hn[:, :, :], ps.rearrange("p (j f) -> p j f", f=D), rb_, ALU.add))
        layernorm(xn, hn)
        dma(lambda e: e.dma_start(out[0:6144, :].rearrange("(j p) f -> p j f", p=128), xn[:, 0:48, :]),
            lambda e: e.dma_start(out[6144:N, :], xn[0:N - 6144, 48, :]))
        ch.wait(nc.sync)


NAMES = ['x', 'src', 'dst', 'edge_attr_16', 'edge_attr_8', 'edge_type_8',
         'L0_gnn_W_msg', 'L0_gnn_b_msg', 'L0_gnn_W_attn', 'L0_gnn_b_attn',
         'L1_gnn_W1', 'L1_gnn_root1', 'L1_gnn_b1', 'L1_gnn_W2', 'L1_gnn_root2', 'L1_gnn_b2',
         'L2_gnn_W_msg_tp', 'L2_gnn_W_msg_lin', 'L2_gnn_W_upd_tp', 'L2_gnn_W_upd_lin',
         'L3_gnn_edge_w', 'L3_gnn_edge_b', 'L3_gnn_root_w', 'L3_gnn_root_b',
         'L3_gnn_bn_gamma', 'L3_gnn_bn_beta', 'L3_gnn_pred_w', 'L3_gnn_pred_b']


def kernel(**inputs):
    import numpy as np
    import concourse.bacc as bacc
    from concourse.bass_utils import run_bass_kernel_spmd

    nc = bacc.Bacc("TRN2", target_bir_lowering=False, num_devices=1)
    arrays, io = {}, {}
    for name in NAMES:
        arr = np.ascontiguousarray(inputs[name])
        arrays["in_" + name] = arr
        io[name] = nc.dram_tensor("in_" + name, arr.shape, mybir.dt.from_np(arr.dtype), kind="ExternalInput").ap()
    out = nc.dram_tensor("out", (N, D), F32, kind="ExternalOutput").ap()
    program(nc, io, out)
    r = run_bass_kernel_spmd(nc, [arrays], core_ids=[0])
    return r.results[0]["out"]
```

```python
from contextlib import ExitStack

import concourse.bass as bass
from concourse import mybir

F32 = mybir.dt.float32
I32 = mybir.dt.int32
I16 = mybir.dt.int16
BF16 = mybir.dt.bfloat16
ALU = mybir.AluOpType
ACT = mybir.ActivationFunctionType
X = mybir.AxisListType.X

N, E, D = 6250, 200000, 16
NP, NJ, JT = 6272, 56, 49
CH, T = 125, 1600
C2 = D * D
ROW = 772
TB0, NB0 = 8, 200
TB, NB = 32, 50
BIG = 1e30
SKIP = 1 << 20
A7 = 784
HBS, HGS = (12, 16), (3, 4)
HG2 = sum(HGS)
A9, KT = 7, 7
EPS = 1e-5


class Chain:

    def __init__(self, nc, sem):
        self.nc, self.last = nc, None
        self.sems = {e: sem("chain_" + e) for e in ("vector", "scalar", "tensor", "gpsimd", "sync", "rows")}
        self.n = dict.fromkeys(self.sems, 0)
        self.engines = {"vector": nc.vector, "scalar": nc.scalar, "tensor": nc.tensor,
                        "gpsimd": nc.gpsimd, "sync": nc.sync, "rows": nc.gpsimd}

    def wait(self, eng):
        if self.last:
            eng.wait_ge(*self.last)

    def step(self, name, instrs, inc=1):
        eng = self.engines[name]
        self.wait(eng)
        for f in instrs:
            f(eng).then_inc(self.sems[name], inc)
            self.n[name] += inc
        self.last = (self.sems[name], self.n[name])

    def v(self, *fs):
        self.step("vector", fs)

    def a(self, *fs):
        self.step("scalar", fs)

    def t(self, *fs):
        self.step("tensor", fs)

    def g(self, *fs):
        self.step("gpsimd", fs)

    def dma(self, *fs):
        self.step("sync", fs, 16)


def program(nc, io, out):
    ctx = ExitStack()
    with ctx:
        def sem(name):
            return ctx.enter_context(nc.semaphore(name))

        def sb(name, shape, dt=F32, c=ctx):
            return c.enter_context(nc.sbuf_tensor(name, shape, dt))

        def dram(name, shape, dt=F32):
            return nc.dram_tensor(name, shape, dt, kind="Internal").ap()

        table8 = dram("node_table8", (NP, 8 * D))
        table9 = dram("node_table9", (NP, 9 * D))
        sums = dram("running_sums", (E + 8, D))
        pick_a = dram("pick_a", (T, 128), I16)
        pick_b = dram("pick_b", (T, 128), I16)
        rows0 = dram("rows0", (NP, ROW))
        flags = dram("edge_flags", (CH, T, 4))
        ends = dram("end_rows", (CH, T), I32)
        aggd = dram("agg_by_source", (8 * A7, D))

        keep = sb("keep", [CH, T + 1])
        dstf = sb("dstf", [CH, T])
        first_of = sb("chunk_first", [CH, 1])
        last_of = sb("chunk_last", [CH, 1])
        ident = sb("ident", [128, 128])
        ones = sb("ones", [128, 128])
        before = sb("chain_mask", [CH, CH])
        cc_row = sb("chain_keep_row", [128, CH])
        patch_row = sb("patch_row", [CH, 1], I32)
        patch_src = sb("patch_src", [CH, 1], I32)
        patch_sum = sb("patch_sum", [CH, 1], I32)
        patch_sum_src = sb("patch_sum_src", [CH, 1], I32)
        end_idx = sb("end_idx", [128, NJ], I32)
        valid = sb("valid", [128, NJ])
        xn = sb("xn", [128, NJ, D])
        hn = sb("hn", [128, NJ, D])
        agg = sb("agg", [128, NJ, D])
        tn = sb("tn", [128, NJ, D])
        red = sb("red", [128, NJ])
        group_mask = sb("group_mask", [128, 8])
        wstage = sb("wstage", [128, D])
        blockdiag = sb("blockdiag", [128, 8, D])
        xT = sb("xT", [128, 7 * 128])
        row_b = sb("row_b", [128, D])
        PS = ctx.enter_context(nc.psum_tensor("PS", [128, 8, 512], F32))
        ch = Chain(nc, sem)
        v, a, t, g, dma = ch.v, ch.a, ch.t, ch.g, ch.dma

        def bc(ap, n, at):
            x = ap.unsqueeze(at)
            shape = list(x.shape)
            shape[at] = n
            return x.to_broadcast(shape)

        def together():
            for eng in (nc.sync, nc.gpsimd, nc.tensor, nc.scalar, nc.vector):
                ch.wait(eng)
            nc.all_engine_barrier()

        setup = ExitStack()
        iop = sb("iop", [128, 1], F32, setup)
        iorow = sb("iorow", [128, CH], F32, setup)
        tri = sb("tri", [CH, CH], F32, setup)
        v(lambda e: e.memset(ones[:, :], 1.0), lambda e: e.memset(ident[:, :], 0.0),
          lambda e: e.memset(xn[:, :, :], 0.0), lambda e: e.memset(valid[:, :], 1.0),
          lambda e: e.memset(group_mask[:, :], 1.0), lambda e: e.memset(agg[:, :, :], 0.0),
          lambda e: e.memset(end_idx[:, :], 0), lambda e: e.memset(hn[:, :, :], 0.0))
        g(lambda e: e.affine_select(out=ident[:, :], in_=ident[:, :], compare_op=ALU.not_equal, fill=1.0,
                                    base=0, pattern=[[-1, 128]], channel_multiplier=1),
          lambda e: e.affine_select(out=valid[:, :], in_=valid[:, :], compare_op=ALU.is_ge, fill=0.0,
                                    base=N - 1, pattern=[[-128, NJ]], channel_multiplier=-1),
          lambda e: e.affine_select(out=group_mask[:, :], in_=group_mask[:, :], compare_op=ALU.is_ge, fill=0.0,
                                    base=0, pattern=[[-16, 8]], channel_multiplier=1),
          lambda e: e.iota(iop[:, :], pattern=[[0, 1]], base=0, channel_multiplier=1,
                           allow_small_or_imprecise_dtypes=True),
          lambda e: e.iota(iorow[:, :], pattern=[[1, CH]], base=0, channel_multiplier=0,
                           allow_small_or_imprecise_dtypes=True))
        g(lambda e: e.affine_select(out=group_mask[:, :], in_=group_mask[:, :], compare_op=ALU.is_ge, fill=0.0,
                                    base=15, pattern=[[16, 8]], channel_multiplier=-1))
        v(lambda e: e.tensor_scalar(tri[:, :], iorow[0:CH, :], iop[0:CH, 0:1], None, ALU.is_gt))

        dsti = sb("dsti", [CH, T], I32, setup)
        nbi = sb("nbi", [CH, 2], I32, setup)
        nb = sb("nb", [CH, 2], F32, setup)
        fl = sb("fl", [CH, T, 4], F32, setup)
        st = sb("st", [CH, T + 1], F32, setup)
        sidx = sb("sidx", [CH, T], I32, setup)
        tmp = sb("tmp", [CH, T], F32, setup)
        small = sb("small", [CH, 12], F32, setup)
        diag = sb("diag", [CH, CH], F32, setup)
        frow = sb("frow", [CH, CH], F32, setup)
        dst_c = io["dst"].rearrange("(p t) -> p t", p=CH)
        v(lambda e: e.memset(nbi[:, :], -1))
        with nc.allow_non_contiguous_dma(reason="one word per chunk"):
            dma(lambda e: e.dma_start(dsti[:, :], dst_c),
                lambda e: e.dma_start(nbi[1:CH, 0:1], dst_c[0:CH - 1, T - 1:T]),
                lambda e: e.dma_start(nbi[0:CH - 1, 1:2], dst_c[1:CH, 0:1]),
                lambda e: e.dma_start(xn[:, 0:48, :], io["x"][0:6144, :].rearrange("(j p) f -> p j f", p=128)),
                lambda e: e.dma_start(xn[0:N - 6144, 48, :], io["x"][6144:N, :]))
        v(lambda e: e.tensor_copy(dstf[:, :], dsti[:, :]), lambda e: e.tensor_copy(nb[:, :], nbi[:, :]),
          lambda e: e.memset(st[:, 0:1], 1.0))
        s = lambda k: small[:, k:k + 1]
        FIRST, LAST, CONT, CHIN, SAME, OK, EF, CCK, LEN, T0, T1 = range(11)
        v(lambda e: e.tensor_tensor(st[:, 1:T], dstf[:, 1:T], dstf[:, 0:T - 1], ALU.not_equal),
          lambda e: e.tensor_copy(first_of[:, :], dstf[:, 0:1]),
          lambda e: e.tensor_copy(last_of[:, :], dstf[:, T - 1:T]))
        v(lambda e: e.tensor_tensor(s(CONT), nb[:, 1:2], last_of[:, :], ALU.is_equal),
          lambda e: e.tensor_tensor(s(CHIN), nb[:, 0:1], first_of[:, :], ALU.is_equal),
          lambda e: e.tensor_tensor(s(SAME), first_of[:, :], last_of[:, :], ALU.is_equal),
          lambda e: e.tensor_tensor(st[:, T:T + 1], nb[:, 1:2], last_of[:, :], ALU.not_equal),
          lambda e: e.tensor_scalar(tmp[:, :], dstf[:, :], first_of[:, 0:1], None, ALU.is_equal))
        v(lambda e: e.tensor_reduce(s(LEN), tmp[:, :], X, ALU.add),
          lambda e: e.tensor_tensor(s(T0), s(SAME), s(CONT), ALU.mult),
          lambda e: e.tensor_tensor(s(CCK), s(SAME), s(CHIN), ALU.mult),
          lambda e: e.tensor_scalar(keep[:, 0:T], st[:, 0:T], -1.0, 1.0, ALU.mult, ALU.add),
          lambda e: e.memset(keep[:, T:T + 1], 0.0),
          lambda e: e.tensor_scalar(fl[:, :, 0], st[:, 0:T], -BIG, None, ALU.mult),
          lambda e: e.tensor_scalar(fl[:, :, 2], st[:, 1:T + 1], -BIG, None, ALU.mult))
        v(lambda e: e.tensor_scalar(s(T0), s(T0), -1.0, 1.0, ALU.mult, ALU.add),
          lambda e: e.tensor_copy(fl[:, :, 1], keep[:, 0:T]))
        v(lambda e: e.tensor_tensor(s(OK), s(CHIN), s(T0), ALU.mult),
          lambda e: e.tensor_scalar(s(EF), iop[0:CH, :], float(T), -1.0, ALU.mult, ALU.add),
          lambda e: e.tensor_scalar(tmp[:, :], dstf[:, :], float(-SKIP), None, ALU.add))
        v(lambda e: e.tensor_tensor(s(EF), s(EF), s(LEN), ALU.add),
          lambda e: e.tensor_tensor(tmp[:, :], tmp[:, :], st[:, 1:T + 1], ALU.mult),
          lambda e: e.tensor_scalar(s(T0), first_of[:, :], float(-SKIP), None, ALU.add))
        v(lambda e: e.tensor_scalar(s(T1), s(EF), float(-SKIP), None, ALU.add),
          lambda e: e.tensor_tensor(s(T0), s(T0), s(OK), ALU.mult),
          lambda e: e.tensor_scalar(sidx[:, :], tmp[:, :], float(SKIP), None, ALU.add),
          lambda e: e.tensor_copy(patch_sum_src[:, :], s(EF)),
          lambda e: e.tensor_copy(patch_src[:, :], first_of[:, :]))
        v(lambda e: e.tensor_tensor(s(T1), s(T1), s(OK), ALU.mult),
          lambda e: e.tensor_scalar(patch_row[:, :], s(T0), float(SKIP), None, ALU.add))
        v(lambda e: e.tensor_scalar(patch_sum[:, :], s(T1), float(SKIP), None, ALU.add),
          lambda e: e.tensor_scalar(diag[:, :], ident[0:CH, 0:CH], first_of[:, 0:1], None, ALU.mult))
        g(lambda e: e.iota(fl[:, :, 3], pattern=[[1, T]], base=0, channel_multiplier=T,
                           allow_small_or_imprecise_dtypes=True))

        def over_partitions(dst_ap, rows):
            t(lambda e: e.matmul(PS[0:rows, 0, 0:CH], ones[0:CH, 0:rows], diag[:, :]))
            v(lambda e: e.tensor_copy(dst_ap, PS[0:rows, 0, 0:CH]))

        over_partitions(frow[:, :], CH)
        v(lambda e: e.tensor_scalar(diag[:, :], ident[0:CH, 0:CH], s(CCK), None, ALU.mult))
        over_partitions(cc_row[:, :], 128)
        v(lambda e: e.tensor_scalar(before[:, :], frow[:, :], last_of[:, 0:1], None, ALU.is_equal))
        v(lambda e: e.tensor_tensor(before[:, :], before[:, :], tri[:, :], ALU.mult))

        initrow = sb("initrow", [128, 7, ROW], F32, setup)
        zrow = sb("zrow", [1, 8 * D], F32, setup)
        v(lambda e: e.memset(initrow[:, :, :], 0.0), lambda e: e.memset(zrow[:, :], 0.0))
        v(lambda e: e.memset(initrow[:, :, C2:2 * C2], 1.0), lambda e: e.memset(initrow[:, :, 3 * C2:], float(E)))
        rows0_j = rows0.rearrange("(j p) c -> p j c", p=128)
        si = sb("srci", [CH, T], I32, setup)
        dma(lambda e: e.dma_start(si[:, :], io["src"].rearrange("(p t) -> p t", p=CH)))
        s_init = sem("s_init")
        ch.wait(nc.sync)
        for k in range(7):
            nc.sync.dma_start(rows0_j[:, 7 * k:7 * k + 7, :], initrow[:, :, :]).then_inc(s_init, 16)
        nc.sync.dma_start(flags, fl[:, :, :]).then_inc(s_init, 16)
        nc.sync.dma_start(ends, sidx[:, :]).then_inc(s_init, 16)
        nc.sync.dma_start(sums[E:E + 8, :].rearrange("(a e) f -> a (e f)", a=1), zrow[:, :]).then_inc(s_init, 16)

        pab = [sb(f"pab{k}", [CH, T], F32, setup) for k in range(2)]
        NT = (T + 127) // 128
        pT = sb("pT", [128, NT, 2, 128], I16, setup)
        v(lambda e: e.tensor_copy(pab[1][:, :], si[:, :]), lambda e: e.memset(pT[:, :, :, :], -1))
        v(lambda e: e.tensor_scalar(pab[0][:, :], pab[1][:, :], float(128 * KT), None, ALU.is_ge))
        for k in range(2, A9):
            v(lambda e: e.scalar_tensor_tensor(out=pab[0][:, :], in0=pab[1][:, :], scalar=float(k * 128 * KT),
                                               in1=pab[0][:, :], op0=ALU.is_ge, op1=ALU.add))
        v(lambda e: e.scalar_tensor_tensor(out=pab[1][:, :], in0=pab[0][:, :], scalar=-128.0 * KT, in1=pab[1][:, :],
                                           op0=ALU.mult, op1=ALU.add))
        wd = [min(128, T - 128 * k) for k in range(NT)]
        at = lambda k, n: PS[0:wd[k], (2 * k + n) // 4, 128 * ((2 * k + n) % 4):128 * ((2 * k + n) % 4) + CH]
        t(*[lambda e, n=n, k=k: e.transpose(at(k, n), pab[n][:, 128 * k:128 * k + wd[k]], ident[0:CH, 0:CH])
            for k in range(NT) for n in range(2)])
        v(*[lambda e, n=n, k=k: e.tensor_copy(pT[0:wd[k], k, n, 0:CH], at(k, n)) for k in range(NT) for n in range(2)])
        full = 128 * (NT - 1)
        dma(*[lambda e, n=n, d_=d_: e.dma_start(d_[0:full, :].rearrange("(k q) c -> q k c", q=128), pT[:, 0:NT - 1, n, :])
              for n, d_ in enumerate((pick_a, pick_b))],
            *[lambda e, n=n, d_=d_: e.dma_start(d_[full:T, :], pT[0:T - full, NT - 1, n, :])
              for n, d_ in enumerate((pick_a, pick_b))])
        nc.sync.wait_ge(s_init, 16 * 10)
        together()
        setup.close()

        L = ExitStack()
        lsem = lambda n: L.enter_context(nc.semaphore(n))
        two = range(2)
        waug = sb("waug", [128, 2 * C2], F32, L)
        idx = [sb(f"idx{k}", [CH, TB0], I32, L) for k in two]
        sid = [sb(f"sid{k}", [CH, TB0], I32, L) for k in two]
        flb = [sb(f"flb{k}", [CH, TB0, 4], F32, L) for k in two]
        fls = [sb(f"fls{k}", [CH, TB0, 4], F32, L) for k in two]
        ef = [sb(f"ef{k}", [CH, TB0, 32], F32, L) for k in two]
        h = [sb(f"h{k}", [CH, TB0, D], F32, L) for k in two]
        efT = [sb(f"efT{k}", [128, 128], F32, L) for k in two]
        e2 = [sb(f"e2{k}", [CH, TB0, C2], F32, L) for k in two]
        M = [sb(f"M{k}", [CH, TB0, C2], F32, L) for k in two]
        PX = [sb(f"PX{k}", [CH, TB0, 2 * C2], F32, L) for k in two]
        ST = [sb(f"ST{k}", [CH, TB0, ROW], F32, L) for k in two]
        cf = [sb(f"cf{k}", [CH, C2], F32, L) for k in two]
        v(lambda e: e.memset(waug[:, :], 0.0), lambda e: e.memset(M[1][:, :, :], 0.0),
          lambda e: e.memset(ST[0][:, :, :], 0.0), lambda e: e.memset(ST[1][:, :, :], 0.0),
          *[lambda e, k=k: e.memset(ef[k][:, :, :], 0.0) for k in two])
        v(*[lambda e, k=k: e.memset(ef[k][:, :, D:D + 1], 1.0) for k in two])
        dma(*[lambda e, q=q, o=o, w=w: e.dma_start(waug[32 * q:32 * q + D, o:o + C2], io[w])
              for q in range(4) for o, w in ((0, "L0_gnn_W_attn"), (C2, "L0_gnn_W_msg"))],
            *[lambda e, q=q, o=o, w=w: e.dma_start(waug[32 * q + D:32 * q + D + 1, o:o + C2],
                                                   io[w].rearrange("(a n) -> a n", a=1))
              for q in range(4) for o, w in ((0, "L0_gnn_b_attn"), (C2, "L0_gnn_b_msg"))])
        together()

        l_in = [lsem(f"l_in{k}") for k in two]
        l_fl = [lsem(f"l_fl{k}") for k in two]
        l_fs = [lsem(f"l_fs{k}") for k in two]
        l_si = [lsem(f"l_si{k}") for k in two]
        l_g = [lsem(f"l_g{k}") for k in two]
        l_tr, l_et, l_mm, l_use = lsem("l_tr"), lsem("l_et"), lsem("l_mm"), lsem("l_use")
        l_e2, l_fw, l_bw, l_a = lsem("l_e2"), lsem("l_fw"), lsem("l_bw"), lsem("l_a")
        l_ex, l_mc, l_p, l_q, l_s = lsem("l_ex"), lsem("l_mc"), lsem("l_p"), lsem("l_q"), lsem("l_s")
        l_sc = [lsem(f"l_sc{k}") for k in two]
        src_c = io["src"].rearrange("(p t) -> p t", p=CH)
        ea16 = io["edge_attr_16"].rearrange("(p t) f -> p t f", p=CH)

        def sp_load(dst, src, sm):
            nc.sync.dma_start(dst, src).then_inc(sm, 16)

        class Blk:

            def __init__(self, i, k, n, tb):
                while not isinstance(i, int) and k > 1 or k < 0:
                    i, k = (i + 1, k - 2) if k > 1 else (i - 1, k + 2)
                if isinstance(i, int):
                    i, k = (2 * i + k) // 2, k % 2
                self.i, self.k, self.n, self.tb = i, k, n, tb

            def exists(self):
                return not isinstance(self.i, int) or 0 <= 2 * self.i + self.k < self.n

            def next(self, d):
                return Blk(self.i, self.k + d, self.n, self.tb)

            def count(self, per, more):
                return self.i * (2 * per) + (self.k * per + more)

            def slot(self, per, more):
                return self.i * per + more

            def cols(self):
                return bass.ds(self.i * (2 * self.tb) + self.k * self.tb, self.tb)

        def wait(e, sm, val):
            if not isinstance(val, int) or val > 0:
                e.wait_ge(sm, val)
                if e in (nc.sync, nc.gpsimd):
                    e.nop(nofuse=True)

        def loop(eng, body, n, tb, before=None, after=None):
            if before:
                before(Blk(0, 0, n, tb))
            for k in two:
                body(Blk(0, k, n, tb))
            with eng.Fori(1, n // 2 - 1) as i:
                for k in two:
                    body(Blk(i, k, n, tb))
            for k in two:
                body(Blk(n // 2 - 1, k, n, tb))
            if after:
                after(Blk(n // 2 - 1, 1, n, tb))

        e = nc.sync

        def load_in(b):
            wait(nc.sync, l_g[b.k], b.slot(16 * TB0, 0))
            wait(nc.sync, l_tr, b.next(-2).count(2, 2))
            sp_load(idx[b.k][:, :], src_c[:, b.cols()], l_in[b.k])
            sp_load(ef[b.k][:, :, 0:D], ea16[:, b.cols(), :], l_in[b.k])

        def load_fl(b):
            wait(nc.sync, l_a, b.next(-1).count(2, 0))
            wait(nc.sync, l_mc, b.next(-1).count(2, 0))
            sp_load(flb[b.k][:, :, :], flags[:, b.cols(), :], l_fl[b.k])

        def load_si(b):
            wait(nc.sync, l_s, b.next(-1).count(TB0, 0))
            sp_load(fls[b.k][:, :, :], flags[:, b.cols(), :], l_fs[b.k])
            wait(nc.sync, l_sc[b.k], b.slot(16 * TB0, 0))
            sp_load(sid[b.k][:, :], ends[:, b.cols()], l_si[b.k])

        def sp_body(b):
            if b.next(1).exists():
                load_in(b.next(1))
            load_fl(b)
            if b.next(-1).exists():
                load_si(b.next(-1))

        loop(nc.sync, sp_body, NB0, TB0, before=load_in, after=load_si)

        lim0 = nc.gpsimd.to_reg(NP - 1)

        def gather0(b):
            wait(nc.gpsimd, l_in[b.k], b.slot(32, 32))
            wait(nc.gpsimd, l_use, b.next(-1).count(4, 0))
            for q in range(TB0):
                nc.gpsimd.indirect_dma_start(h[b.k][:, q, :], None, io["x"],
                                             bass.IndirectOffsetOnAxis(ap=idx[b.k][:, q:q + 1], axis=0))\
                    .then_inc(l_g[b.k], 16)

        def scatter0(b):
            wait(nc.gpsimd, l_s, b.count(TB0, TB0))
            wait(nc.gpsimd, l_mc, b.count(2, 2))
            wait(nc.gpsimd, l_si[b.k], b.slot(16, 16))
            for q in range(TB0):
                nc.gpsimd.indirect_dma_start(rows0, bass.IndirectOffsetOnAxis(ap=sid[b.k][:, q:q + 1], axis=0),
                                             ST[b.k][:, q, :], None, bounds_check=lim0, oob_is_err=False)\
                    .then_inc(l_sc[b.k], 16)

        def pool_body(b):
            if b.next(1).exists():
                gather0(b.next(1))
            if b.next(-1).exists():
                scatter0(b.next(-1))

        loop(nc.gpsimd, pool_body, NB0, TB0, before=gather0, after=scatter0)

        def turn(b):
            for q in two:
                wait(nc.tensor, l_in[b.k], b.slot(32, 32))
                wait(nc.tensor, l_et, b.next(-1).count(2, q + 1))
                nc.tensor.transpose(PS[:, 4 + q, 0:CH], ef[b.k][:, 4 * q:4 * q + 4, :].rearrange("p a c -> p (a c)"),
                                    ident[0:CH, 0:CH]).then_inc(l_tr, 1)

        SLOT = ((0, 1, 2, 0), (1, 2, 0, 1))
        BANK = (0, 2, 6)
        BEFORE = ((-2, -1, -3, 0), (-3, -2, -1, 0))

        def weigh(b):
            for n in range(4):
                wait(nc.tensor, l_et, b.count(2, n // 2 + 1))
                wait(nc.tensor, l_use, b.count(4, BEFORE[b.k][n] + 1))
                for r in two:
                    row = 32 * (2 * (n % 2) + r)
                    mm = nc.tensor.matmul(PS[0:CH, BANK[SLOT[b.k][n]] + r, :], efT[n // 2][row:row + D + 1, 0:CH],
                                          waug[row:row + D + 1, :])
                mm.then_inc(l_mm, 1)

        def pe_body(b):
            weigh(b)
            if b.next(1).exists():
                turn(b.next(1))

        loop(nc.tensor, pe_body, NB0, TB0, before=turn)

        def copy_turned(b):
            for q in two:
                wait(nc.scalar, l_tr, b.count(2, q + 1))
                wait(nc.scalar, l_mm, b.next(-1).count(4, 2 * q + 2))
                nc.scalar.activation(efT[q][:, 0:CH], PS[:, 4 + q, 0:CH], ACT.Copy).then_inc(l_et, 1)

        def act_body(b):
            if b.next(1).exists():
                copy_turned(b.next(1))
            wait(nc.scalar, l_a, b.count(2, 2))
            nc.scalar.activation(cf[b.k][:, :], cf[b.k][:, :], ACT.Exp).then_inc(l_ex, 1)
            nc.scalar.activation(PX[b.k][:, :, 0:C2], e2[b.k][:, :, :], ACT.Exp).then_inc(l_ex, 1)
            wait(nc.scalar, l_sc[b.k], b.slot(16 * TB0, 0))
            nc.scalar.activation(ST[b.k][:, :, 0:C2], M[b.k][:, :, :], ACT.Copy).then_inc(l_mc, 1)
            nc.scalar.activation(ST[b.k][:, :, 3 * C2:3 * C2 + 1], flb[b.k][:, :, 3:4], ACT.Copy).then_inc(l_mc, 1)

        loop(nc.scalar, act_body, NB0, TB0, before=copy_turned)

        V = nc.vector

        def product(b, n, message):
            ts = slice(2 * n, 2 * n + 2)
            hb = bc(h[b.k][:, ts, :], D, 3)
            bank = BANK[SLOT[b.k][n]]
            if n == 0 and not message:
                wait(V, l_g[b.k], b.slot(16 * TB0, 16 * TB0))
                wait(V, l_ex, b.next(-2).count(2, 2))
                wait(V, l_p, b.next(-2).count(1, 1))
                wait(V, l_s, b.next(-2).count(TB0, TB0))
            if not message:
                wait(V, l_mm, b.count(4, n + 1))
            w = PS[0:CH, bank:bank + 2, C2:] if message else PS[0:CH, bank:bank + 2, 0:C2]
            to = PX[b.k][:, ts, C2:] if message else e2[b.k][:, ts, :]
            V.tensor_tensor(to.rearrange("p t (i o) -> p t i o", i=D), w.rearrange("p t (i o) -> p t i o", i=D),
                            hb, ALU.mult).then_inc(l_use if message else l_e2, 1)

        def forward(b, q):
            if q == 0:
                wait(V, l_fl[b.k], b.slot(16, 16))
                wait(V, l_mc, b.next(-1).count(2, 0))
            wait(V, l_e2, b.count(4, q // 2 + 1))
            wait(V, l_fw, b.count(TB0, q))
            prev = M[b.k][:, q - 1, :] if q else M[1 - b.k][:, TB0 - 1, :]
            V.scalar_tensor_tensor(out=M[b.k][:, q, :], in0=prev, scalar=flb[b.k][:, q, 0:1],
                                   in1=e2[b.k][:, q, :], op0=ALU.add, op1=ALU.max).then_inc(l_fw, 1)

        def backward(b, n):
            q = TB0 - 2 - n
            wait(V, l_fw, b.count(TB0, TB0))
            wait(V, l_bw, b.count(TB0 - 1, n))
            V.scalar_tensor_tensor(out=M[b.k][:, q, :], in0=M[b.k][:, q + 1, :], scalar=flb[b.k][:, q, 2:3],
                                   in1=M[b.k][:, q, :], op0=ALU.add, op1=ALU.max).then_inc(l_bw, 1)

        def less_maxima(b):
            wait(V, l_bw, b.count(TB0 - 1, TB0 - 1))
            wait(V, l_q, b.next(-1).count(1, 0))
            V.tensor_tensor(e2[b.k][:, :, :], e2[b.k][:, :, :], M[b.k][:, :, :], ALU.subtract).then_inc(l_a, 1)
            V.scalar_tensor_tensor(out=cf[b.k][:, :], in0=M[1 - b.k][:, TB0 - 1, :], scalar=flb[b.k][:, 0, 0:1],
                                   in1=M[b.k][:, 0, :], op0=ALU.add, op1=ALU.subtract).then_inc(l_a, 1)

        def weighted(b):
            P = PX[b.k]
            wait(V, l_ex, b.count(2, 2))
            V.tensor_tensor(P[:, :, C2:], P[:, :, C2:], P[:, :, 0:C2], ALU.mult).then_inc(l_p, 1)

        def carried(b):
            wait(V, l_sc[b.k], b.slot(16 * TB0, 0))
            wait(V, l_s, b.count(TB0, 0))
            V.tensor_tensor(ST[b.k][:, 0, C2:3 * C2].rearrange("p (a c) -> p a c", a=2),
                            ST[1 - b.k][:, TB0 - 1, C2:3 * C2].rearrange("p (a c) -> p a c", a=2),
                            bc(cf[b.k][:, :], 2, 1), ALU.mult).then_inc(l_q, 1)

        def sum_step(b, q):
            S, P = ST[b.k], PX[b.k]
            if q == 0:
                wait(V, l_fs[b.k], b.slot(16, 16))
                wait(V, l_p, b.count(1, 1))
                wait(V, l_q, b.count(1, 1))
                V.tensor_tensor(S[:, 0, C2:3 * C2], S[:, 0, C2:3 * C2], P[:, 0, :], ALU.add).then_inc(l_s, 1)
            else:
                wait(V, l_s, b.count(TB0, q))
                V.scalar_tensor_tensor(out=S[:, q, C2:3 * C2], in0=S[:, q - 1, C2:3 * C2],
                                       scalar=fls[b.k][:, q, 1:2], in1=P[:, q, :],
                                       op0=ALU.mult, op1=ALU.add).then_inc(l_s, 1)

        def sums_alone(b):
            weighted(b)
            carried(b)
            for q in range(TB0):
                sum_step(b, q)

        def dve_body(b):
            last = b.next(-1) if b.next(-1).exists() else None
            product(b, 0, False)
            product(b, 0, True)
            for n in (1, 2, 3):
                product(b, n, False)
                forward(b, 2 * n - 2)
                product(b, n, True)
                forward(b, 2 * n - 1)
            if last:
                weighted(last)
            forward(b, TB0 - 2)
            if last:
                carried(last)
            forward(b, TB0 - 1)
            for q in range(TB0):
                if last:
                    sum_step(last, q)
                if q < TB0 - 1:
                    backward(b, q)
            less_maxima(b)

        loop(V, dve_body, NB0, TB0, after=sums_alone)
        for k in two:
            for eng in (nc.gpsimd, nc.sync):
                eng.wait_ge(l_sc[k], 16 * TB0 * NB0 // 2)
        together()

        CI = PX[0]
        lastrow = ST[1][:, TB0 - 1, :]
        mT = [sb(f"mT{k}", [128, 3, CH + 1], F32, L) for k in two]
        w1 = sb("w1", [128, CH], F32, L)
        w2 = sb("w2", [128, CH], F32, L)
        rsc = sb("rsc", [128, CH], F32, L)
        inT = sb("inT", [128, 3, CH], F32, L)
        carry = sb("carry", [CH, 3 * C2], F32, L)
        got = sb("got", [CH, ROW], F32, L)
        mt = sb("mt", [CH, C2], F32, L)
        ea = sb("ea", [CH, 2, C2], F32, L)
        v(lambda e: e.tensor_scalar(rsc[:, :], cc_row[:, :], BIG, -BIG, ALU.mult, ALU.add),
          *[lambda e, k=k: e.memset(mT[k][:, :, :], 0.0) for k in two])
        for k in two:
            t(*[lambda e, c=c: e.transpose(PS[:, c, 0:CH], lastrow[:, c * C2 + 128 * k:c * C2 + 128 * k + 128],
                                           ident[0:CH, 0:CH]) for c in range(3)])
            v(lambda e: e.tensor_copy(inT[:, :, :], PS[:, 0:3, 0:CH]))
            v(lambda e: e.tensor_tensor_scan(mT[k][:, 0, 1:], rsc[:, :], inT[:, 0, :], 0.0, ALU.add, ALU.max))
            v(lambda e: e.tensor_tensor(w1[:, :], inT[:, 0, :], mT[k][:, 0, 1:], ALU.subtract),
              lambda e: e.tensor_tensor(w2[:, :], mT[k][:, 0, 0:CH], rsc[:, :], ALU.add))
            v(lambda e: e.tensor_tensor(w2[:, :], w2[:, :], mT[k][:, 0, 1:], ALU.subtract))
            a(lambda e: e.activation(w1[:, :], w1[:, :], ACT.Exp), lambda e: e.activation(w2[:, :], w2[:, :], ACT.Exp))
            v(lambda e: e.tensor_tensor(inT[:, 1:3, :], inT[:, 1:3, :], bc(w1[:, :], 2, 1), ALU.mult))
            v(*[lambda e, c=c: e.tensor_tensor_scan(mT[k][:, c, 1:], w2[:, :], inT[:, c, :], 0.0, ALU.mult, ALU.add)
                for c in (1, 2)])
            t(*[lambda e, c=c: e.transpose(PS[0:CH, 4 + c, 0:128], mT[k][:, c, 0:CH], ident[:, :]) for c in range(3)])
            v(lambda e: e.tensor_copy(carry[:, :].rearrange("p (c h n) -> p c h n", c=3, h=2)[:, :, k, :],
                                      PS[0:CH, 4:7, 0:128]))
        ch.step("rows", [lambda e: e.indirect_dma_start(got[:, :], None, rows0,
                                                          bass.IndirectOffsetOnAxis(ap=patch_src[:, 0:1], axis=0))], 16)
        v(lambda e: e.tensor_tensor(mt[:, :], got[:, 0:C2], carry[:, 0:C2], ALU.max))
        v(lambda e: e.tensor_tensor(ea[:, 0, :], got[:, 0:C2], mt[:, :], ALU.subtract),
          lambda e: e.tensor_tensor(ea[:, 1, :], carry[:, 0:C2], mt[:, :], ALU.subtract))
        a(lambda e: e.activation(ea[:, :, :], ea[:, :, :], ACT.Exp))
        two_of = lambda ap: ap.rearrange("p (a c) -> p a c", a=2)
        v(lambda e: e.tensor_tensor(two_of(got[:, C2:3 * C2]), two_of(got[:, C2:3 * C2]), bc(ea[:, 0, :], 2, 1), ALU.mult),
          lambda e: e.tensor_tensor(two_of(carry[:, C2:]), two_of(carry[:, C2:]), bc(ea[:, 1, :], 2, 1), ALU.mult))
        v(lambda e: e.tensor_tensor(got[:, C2:3 * C2], got[:, C2:3 * C2], carry[:, C2:], ALU.add),
          lambda e: e.tensor_copy(got[:, 0:C2], mt[:, :]))
        ch.wait(nc.gpsimd)
        nc.gpsimd.nop(nofuse=True)
        ch.step("rows", [lambda e: e.indirect_dma_start(rows0, bass.IndirectOffsetOnAxis(ap=patch_row[:, 0:1], axis=0),
                                                          got[:, :], None, bounds_check=lim0, oob_is_err=False)], 16)
        together()
        L.close()

        L = ExitStack()
        rb = [sb(f"rb{k}", [128, 7, ROW], F32, L) for k in range(7)]
        r_in = [L.enter_context(nc.semaphore(f"r_in{k}")) for k in range(7)]
        ch.wait(nc.sync)
        for k in range(7):
            nc.sync.dma_start(rb[k][:, :, :], rows0_j[:, 7 * k:7 * k + 7, :]).then_inc(r_in[k], 16)
        for k in range(7):
            js = slice(7 * k, 7 * k + 7)
            nc.vector.wait_ge(r_in[k], 16)
            v(lambda e: e.reciprocal(rb[k][:, :, C2:2 * C2], rb[k][:, :, C2:2 * C2]),
              lambda e: e.tensor_copy(end_idx[:, js], rb[k][:, :, 3 * C2]))
            v(lambda e: e.tensor_tensor(rb[k][:, :, C2:2 * C2], rb[k][:, :, C2:2 * C2], rb[k][:, :, 2 * C2:3 * C2],
                                        ALU.mult))
            v(lambda e: e.tensor_reduce(agg[:, js, :], rb[k][:, :, C2:2 * C2].rearrange("p j (i o) -> p j o i", i=D),
                                        X, ALU.add))
        L.close()

        def flat(ap):
            return ap.rearrange("p j f -> p (j f)")

        def add_to(dst, src):
            v(lambda e: e.tensor_tensor(flat(dst[:, :, :]), flat(dst[:, :, :]), flat(src[:, :, :]), ALU.add))

        def layernorm(x, y):
            add_to(x, y)
            v(lambda e: e.tensor_reduce(red[:, :], x[:, :, :], X, ALU.add))
            v(lambda e: e.tensor_scalar(red[:, :], red[:, :], 1.0 / D, None, ALU.mult))
            v(lambda e: e.tensor_tensor(x[:, :, :], x[:, :, :], bc(red[:, :], D, 2), ALU.subtract))
            v(lambda e: e.tensor_tensor(tn[:, :, :], x[:, :, :], x[:, :, :], ALU.mult))
            v(lambda e: e.tensor_reduce(red[:, :], tn[:, :, :], X, ALU.add))
            v(lambda e: e.tensor_scalar(red[:, :], red[:, :], 1.0 / D, EPS, ALU.mult, ALU.add))
            a(lambda e: e.activation(red[:, :], red[:, :], ACT.Sqrt))
            v(lambda e: e.reciprocal(red[:, :], red[:, :]))
            v(lambda e: e.tensor_tensor(x[:, :, :], x[:, :, :], bc(red[:, :], D, 2), ALU.mult))

        def turned(x):
            t(*[lambda e, k=k: e.transpose(PS[:, k // 4, 128 * (k % 4):128 * (k % 4) + 128],
                                           flat(x[:, 8 * k:8 * k + 8, :]), ident[:, :]) for k in range(7)])
            v(lambda e: e.tensor_copy(xT[:, :], PS[:, 0:2, :].rearrange("p b c -> p (b c)")[:, 0:896]))

        def times(w):
            dma(*[lambda e, q=q: e.dma_start(wstage[D * q:D * q + D, :], w) for q in range(8)])
            v(lambda e: e.tensor_tensor(blockdiag[:, :, :], bc(wstage[:, :], 8, 1), bc(group_mask[:, :], D, 2), ALU.mult))
            t(*[lambda e, k=k: e.matmul(PS[:, 2 + k // 4, 128 * (k % 4):128 * (k % 4) + 128],
                                        xT[:, 128 * k:128 * k + 128], blockdiag[:, :, :].rearrange("p g o -> p (g o)"))
                for k in range(7)])
            return PS[:, 2:4, :].rearrange("p b c -> p (b c)")[:, 0:896]

        def row_of(w):
            dma(lambda e: e.dma_start(row_b[:, :], w.rearrange("(a n) -> a n", a=1).to_broadcast([128, D])))
            return bc(row_b[:, :], NJ, 1)

        layernorm(xn, agg)

        coef_sb = sb("coef", [CH, T, 8])
        L = ExitStack()
        tyi = sb("tyi", [CH, T], I32, L)
        ty = sb("ty", [CH, T], F32, L)
        isf = sb("isf", [CH, T], F32, L)
        isl = sb("isl", [CH, T], F32, L)
        cnt = sb("cnt", [CH, T], F32, L)
        lastp = sb("lastp", [CH, 8], F32, L)
        firstp = sb("firstp", [CH, 8], F32, L)
        more = sb("more", [CH, 2, 8], F32, L)
        q_ = [sb(f"q{k}", [CH, CH], F32, L) for k in range(4)]
        lt = sb("lt", [CH, CH], F32, L)
        gt = sb("gt", [CH, CH], F32, L)
        fr = sb("fr", [CH, CH], F32, L)
        lr = sb("lr", [CH, CH], F32, L)
        dg = sb("dg", [CH, CH], F32, L)
        v(lambda e: e.memset(lt[:, :], 1.0), lambda e: e.memset(gt[:, :], 1.0))
        g(lambda e: e.affine_select(out=lt[:, :], in_=lt[:, :], compare_op=ALU.is_gt, fill=0.0,
                                    base=0, pattern=[[1, CH]], channel_multiplier=-1),
          lambda e: e.affine_select(out=gt[:, :], in_=gt[:, :], compare_op=ALU.is_gt, fill=0.0,
                                    base=0, pattern=[[-1, CH]], channel_multiplier=1))
        dma(lambda e: e.dma_start(tyi[:, :], io["edge_type_8"].rearrange("(p t) -> p t", p=CH)))
        for src_, dst_ in ((first_of, fr), (last_of, lr)):
            v(lambda e: e.tensor_scalar(dg[:, :], ident[0:CH, 0:CH], src_[:, 0:1], None, ALU.mult))
            t(lambda e: e.matmul(PS[0:CH, 0, 0:CH], ones[0:CH, 0:CH], dg[:, :]))
            v(lambda e: e.tensor_copy(dst_[:, :], PS[0:CH, 0, 0:CH]))
        spec = [(fr, last_of, lt), (fr, first_of, gt), (lr, last_of, lt), (lr, first_of, gt)]
        v(*[lambda e, k=k: e.tensor_scalar(q_[k][:, :], spec[k][0][:, :], spec[k][1][:, 0:1], None, ALU.is_equal)
            for k in range(4)], lambda e: e.tensor_copy(ty[:, :], tyi[:, :]),
          lambda e: e.tensor_scalar(isf[:, :], dstf[:, :], first_of[:, 0:1], None, ALU.is_equal),
          lambda e: e.tensor_scalar(isl[:, :], dstf[:, :], last_of[:, 0:1], None, ALU.is_equal))
        v(*[lambda e, k=k: e.tensor_tensor(q_[k][:, :], q_[k][:, :], spec[k][2][:, :], ALU.mult) for k in range(4)],
          lambda e: e.tensor_tensor(isl[:, :], isl[:, :], isf[:, :], ALU.is_gt))
        for r in range(8):
            cr = coef_sb[:, :, r]
            v(lambda e: e.tensor_scalar(cnt[:, :], ty[:, :], float(r), None, ALU.is_equal))
            v(lambda e: e.tensor_tensor_scan(cnt[:, :], keep[:, 0:T], cnt[:, :], 0.0, ALU.mult, ALU.add))
            v(lambda e: e.tensor_copy(lastp[:, r:r + 1], cnt[:, T - 1:T]),
              lambda e: e.tensor_tensor_scan(cr[:, ::-1], keep[:, 1:T + 1][:, ::-1], cnt[:, ::-1], 0.0, ALU.mult, ALU.max))
            v(lambda e: e.tensor_copy(firstp[:, r:r + 1], cr[:, 0:1]))
        t(lambda e: e.matmul(PS[0:CH, 0, 0:8], q_[0][:, :], lastp[:, :], start=True, stop=False),
          lambda e: e.matmul(PS[0:CH, 1, 0:8], q_[2][:, :], lastp[:, :], start=True, stop=False))
        t(lambda e: e.matmul(PS[0:CH, 0, 0:8], q_[1][:, :], firstp[:, :], start=False, stop=True),
          lambda e: e.matmul(PS[0:CH, 1, 0:8], q_[3][:, :], firstp[:, :], start=False, stop=True))
        v(lambda e: e.tensor_copy(more[:, :, :], PS[0:CH, 0:2, 0:8]))
        sel = sb("sel", [CH, T], F32, L)
        v(lambda e: e.memset(sel[:, :], 0.0))
        for r in range(8):
            cr = coef_sb[:, :, r]
            v(lambda e: e.scalar_tensor_tensor(out=cr, in0=isf[:, :], scalar=more[:, 0, r:r + 1], in1=cr,
                                               op0=ALU.mult, op1=ALU.add))
            v(lambda e: e.scalar_tensor_tensor(out=cr, in0=isl[:, :], scalar=more[:, 1, r:r + 1], in1=cr,
                                               op0=ALU.mult, op1=ALU.add))
            v(lambda e: e.scalar_tensor_tensor(out=cnt[:, :], in0=ty[:, :], scalar=float(r), in1=cr,
                                               op0=ALU.is_equal, op1=ALU.mult))
            v(lambda e: e.tensor_tensor(sel[:, :], sel[:, :], cnt[:, :], ALU.add))
        v(lambda e: e.tensor_scalar(sel[:, :], sel[:, :], 1.0, None, ALU.max))
        v(lambda e: e.reciprocal(sel[:, :], sel[:, :]))
        v(*[lambda e, r=r: e.scalar_tensor_tensor(out=coef_sb[:, :, r], in0=ty[:, :], scalar=float(r), in1=sel[:, :],
                                                  op0=ALU.is_equal, op1=ALU.mult) for r in range(8)])
        together()
        L.close()

        patch_g = sb("patch_g", [CH, D])
        parts = sb("parts", [128, 3, KT, A9 * D], BF16)
        pick = sb("pick", [128, KT], F32)
        pick_row = sb("pick_row", [128, 1], F32)
        every = sb("every_weight", [128, 9, D], F32)
        g(lambda e: e.iota(pick[:, :], pattern=[[128, KT]], base=0, channel_multiplier=1,
                           allow_small_or_imprecise_dtypes=True))
        gi = sb("gi", [128, 8], F32)
        g(lambda e: e.iota(gi[:, :], pattern=[[1, 8]], base=0, channel_multiplier=0,
                           allow_small_or_imprecise_dtypes=True))
        v(lambda e: e.tensor_tensor(gi[:, :], gi[:, :], group_mask[:, :], ALU.mult))
        v(lambda e: e.tensor_reduce(pick_row[:, :], gi[:, :], X, ALU.add))
        lim_s = nc.gpsimd.to_reg(E - 1)

        def split_parts(x):
            r = tn[:, 0:JT, :].rearrange("p (a c) f -> p c a f", c=KT)
            xv = x[:, 0:JT, :].rearrange("p (a c) f -> p c a f", c=KT)
            pv = lambda n, c: parts[:, n, c, :].rearrange("p (a f) -> p a f", a=A9)
            src_ = xv
            for n in range(3):
                v(*[lambda e, c=c: e.tensor_copy(pv(n, c), src_[:, c, :, :]) for c in range(KT)])
                if n < 2:
                    v(*[lambda e, c=c: e.tensor_tensor(r[:, c, :, :], src_[:, c, :, :], pv(n, c), ALU.subtract)
                        for c in range(KT)])
                src_ = r

        s_row = sem("s_row")
        s_agg = sem("s_agg")
        pieces, aggs = [0], [0]

        def expand_nodes(name, x, weights, always=None):
            R = 9 if always is not None else 8
            table = table9 if always is not None else table8
            L = ExitStack()
            wide = sb(f"{name}wide", [128, 8, R * D], F32, L)
            rows = sb(f"{name}rows", [128, NJ, R * D], F32, L)
            dma(*[lambda e, q=q: e.dma_start(every[D * q:D * q + D, 0:8, :], weights) for q in range(8)])
            if always is not None:
                dma(*[lambda e, q=q: e.dma_start(every[D * q:D * q + D, 8, :], always) for q in range(8)])
            v(*[lambda e, q=q: e.tensor_scalar(wide[:, q, :], every[:, 0:R, :].rearrange("p r o -> p (r o)"),
                                               group_mask[:, q:q + 1], None, ALU.mult) for q in range(8)])
            turned(x)
            for k in range(7):
                at = 4 * (k % 2)
                t(*[lambda e, q=q: e.matmul(PS[:, at + q, 0:2 * R * D], xT[:, 128 * k:128 * k + 128],
                                            wide[:, 2 * q:2 * q + 2, :].rearrange("p s n -> p (s n)"))
                    for q in range(4)])
                v(lambda e: e.tensor_copy(rows[:, 8 * k:8 * k + 8, :].rearrange("p (q s) n -> p q (s n)", s=2),
                                          PS[:, at:at + 4, 0:2 * R * D]))
                ch.wait(nc.sync)
                n = min(JT - 8 * k, 8)
                nc.sync.dma_start(table.rearrange("(j p) f -> p j f", p=128)[:, 8 * k:8 * k + n, :],
                                  rows[:, 8 * k:8 * k + n, :]).then_inc(s_row, 16)
                pieces[0] += 1
            nc.sync.wait_ge(s_row, 16 * pieces[0])
            together()
            L.close()

        def conv(name, index, both=False, by_source=None):
            L = ExitStack()
            lsem = lambda n: L.enter_context(nc.semaphore(f"{name}_{n}"))
            help_ = by_source is None
            NGS = [TB - HBS[k] if help_ else TB for k in two]
            R = 9 if both else 8
            table = table9 if both else table8
            ix = [sb(f"{name}ix{k}", [CH, TB], I32, L) for k in two]
            yg = [sb(f"{name}yg{k}", [CH, TB, R * D], F32, L) for k in two]
            msg = [sb(f"{name}msg{k}", [CH, TB, D], F32, L) for k in two]
            c_ix = [lsem(f"ix{k}") for k in two]
            c_g = [lsem(f"g{k}") for k in two]
            c_rd = lsem("rd")
            G = TB // 4
            index_c = index.rearrange("(p t) -> p t", p=CH)
            sums_c = sums[0:E, :].rearrange("(p t) f -> p t f", p=CH)
            if help_:
                c_st = [lsem(f"st{k}") for k in two]
                c_run = lsem("run")
                run = [sb(f"{name}run{k}", [CH, TB, D], F32, L) for k in two]
                hot_ = [sb(f"{name}hot{k}", [128, KT, HBS[k] * 128], BF16, L) for k in two]
                ra = [sb(f"{name}ra{k}", [128, HBS[k] * 128], I16, L) for k in two]
                rb2 = [sb(f"{name}rb{k}", [128, HBS[k] * 128], I16, L) for k in two]
                mx = [sb(f"{name}mx{k}", [A9 * D, 512], F32, L) for k in two]
                h_row = [lsem(f"hrow{k}") for k in two]
                h_oh, h_g, h_mk, h_sel, h_cp = lsem("oh"), lsem("pg"), lsem("mk"), lsem("sel"), lsem("cp")
                v(*[lambda e, k=k: e.memset(run[k][:, :, :], 0.0) for k in two])
            else:
                av, bv = by_source
                ms = sb("ms", [CH, TB, D], F32, L)
                c_ms = lsem("ms")
                bst = sb("bst", [CH, TB], F32, L)
                lhs = [sb(f"lhs{k}", [CH, 4, 3, 128], BF16, L) for k in two]
                m3 = [sb(f"m3{k}", [CH, TB, 3, D], BF16, L) for k in two]
                mkx = [sb(f"mkx{k}", [CH, TB, 8, D], BF16, L) for k in two]
                hot = [sb(f"hot{k}", [CH, A7], BF16, L) for k in range(8)]
                io8 = sb("io8", [CH, 8], F32, L)
                mkb = sb("mkb", [CH, TB, 8], BF16, L)
                iob = sb("iob", [CH, A7], I16, L)
                zz = sb("zz", [CH, A7], BF16, L)
                c_mk, c_mkx, c_bk, c_m3 = lsem("mk"), lsem("mkx"), lsem("bk"), lsem("m3")
                c_lhs, c_hot, c_ag = lsem("lhs"), lsem("hot"), lsem("ag")
                g(lambda e: e.iota(io8[:, :], pattern=[[1, 8]], base=0, channel_multiplier=0,
                                   allow_small_or_imprecise_dtypes=True),
                  lambda e: e.iota(iob[:, :], pattern=[[1, A7]], base=0, channel_multiplier=0,
                                   allow_small_or_imprecise_dtypes=True))
                v(lambda e: e.memset(zz[:, :], 0.0))
                t(*[lambda e, k=k: e.matmul(PS[:, 6 + k, 0:A7 // 2], zz[:, 0:128], zz[:, 0:A7 // 2],
                                            start=True, stop=False) for k in two])
            together()

            def groups(b, more):
                return b.i * HG2 + ((0, HGS[0])[b.k] + more)

            def par(b, q):
                return (HGS[0] * b.k + q) % 2

            def slot_free(b, q):
                return groups(b, {(0, 0): 0, (0, 1): -1}.get((b.k, q), q - 1))

            def load_ix(b):
                wait(nc.sync, c_g[b.k], b.slot(16 * NGS[b.k], 0))
                sp_load(ix[b.k][:, :], index_c[:, b.cols()], c_ix[b.k])

            def load_rows(b):
                wait(nc.sync, h_mk, groups(b.next(-1), 0))
                at = b.i * (2 * TB) + (b.k * TB + TB - HBS[b.k])
                for dst_, src_ in ((ra, pick_a), (rb2, pick_b)):
                    sp_load(dst_[b.k][:, :], src_[bass.ds(at, HBS[b.k]), :].rearrange("(a t) c -> a (t c)", a=1)
                            .to_broadcast([128, HBS[b.k] * 128]), h_row[b.k])

            def sp_first(b):
                load_ix(b)
                if help_:
                    load_rows(b)
                    load_rows(b.next(1))

            def store_sums(b):
                wait(nc.sync, c_run, b.count(D, D))
                sp_load(sums_c[:, b.cols(), :], run[b.k][:, :, :], c_st[b.k])

            def sp(b):
                if b.next(1).exists():
                    load_ix(b.next(1))
                if help_:
                    if b.next(2).exists():
                        load_rows(b.next(2))
                    if b.next(-1).exists():
                        store_sums(b.next(-1))

            loop(nc.sync, sp, NB, TB, before=sp_first, after=store_sums if help_ else None)

            def gather(b):
                wait(nc.gpsimd, c_ix[b.k], b.slot(16, 16))
                wait(nc.gpsimd, c_rd, b.next(-1).count(2, 0))
                for q in range(NGS[b.k]):
                    nc.gpsimd.indirect_dma_start(yg[b.k][:, q, :], None, table,
                                                 bass.IndirectOffsetOnAxis(ap=ix[b.k][:, q:q + 1], axis=0))\
                        .then_inc(c_g[b.k], 16)

            loop(nc.gpsimd, gather, NB, TB)

            def pick_rows(b, n):
                q, third = n // 3, n % 3
                if third == 0:
                    wait(nc.tensor, h_oh, b.count(KT, KT))
                    wait(nc.tensor, h_mk, slot_free(b, q))
                for m in range(KT * third, KT * third + KT):
                    mm = nc.tensor.matmul(PS[0:A9 * D, 4 + par(b, q), :], parts[:, m % 3, m // 3, :],
                                          hot_[b.k][:, m // 3, 512 * q:512 * q + 512],
                                          start=(m == 0), stop=(m == 3 * KT - 1))
                if third == 2:
                    mm.then_inc(h_g, 1)

            def weigh_rows(b, q):
                wait(nc.tensor, h_mk, groups(b, q + 1))
                wait(nc.tensor, h_cp, slot_free(b, q))
                for r in range(4):
                    mm = nc.tensor.matmul(PS[:, (6, 0)[par(b, q)] + r // 2, R * D * (r % 2):R * D * (r % 2) + R * D],
                                          mx[par(b, q)][:, 128 * r:128 * r + 128],
                                          every[0:A9 * D, 0:R, :].rearrange("p r o -> p (r o)"))
                mm.then_inc(h_sel, 1)

            def spread(b, q):
                wait(nc.tensor, c_lhs, b.count(3 * G, 3 * q + 3))
                for r in range(4):
                    wait(nc.tensor, c_hot, b.count(TB, 4 * q + r + 1))
                    for part in range(3):
                        for k in two:
                            mm = nc.tensor.matmul(PS[:, 6 + k, 0:A7 // 2], lhs[q % 2][:, r, part, :],
                                                  hot[4 * (q % 2) + r][:, k * A7 // 2:(k + 1) * A7 // 2],
                                                  start=False, stop=False)
                    mm.then_inc(c_ag, 1)

            def pe(b):
                if help_:
                    nx = b.next(1) if b.next(1).exists() else None
                    if nx:
                        pick_rows(nx, 0)
                    weigh_rows(b, HGS[b.k] - 1)
                    if nx:
                        for n in range(1, 3 * HGS[nx.k]):
                            pick_rows(nx, n)
                            if n > 3 and n % 3 == 1:
                                weigh_rows(nx, n // 3 - 1)
                else:
                    pv_ = b.next(-1) if b.next(-1).exists() else None
                    if pv_:
                        for q in range(G):
                            spread(pv_, q)

            def pe_first(b):
                for q in range(HGS[0]):
                    for n in range(3):
                        pick_rows(b, 3 * q + n)
                    if q:
                        weigh_rows(b, q - 1)

            def pe_last(b):
                for q in range(G):
                    spread(b, q)

            loop(nc.tensor, pe, NB, TB, before=pe_first if help_ else None, after=None if help_ else pe_last)

            def copy_rows(b, q):
                wait(nc.scalar, h_sel, groups(b, q + 1))
                wait(nc.scalar, c_rd, b.next(-1).count(2, 0))
                at, bank = NGS[b.k] + 4 * q, (6, 0)[par(b, q)]
                nc.scalar.activation(yg[b.k][:, at:at + 4, :].rearrange("p (g t) n -> p g (t n)", g=2),
                                     PS[0:CH, bank:bank + 2, 0:2 * R * D], ACT.Copy).then_inc(h_cp, 1)

            def act(b):
                if help_:
                    copy_rows(b, HGS[b.k] - 1)
                    if b.next(1).exists():
                        for q in range(HGS[b.next(1).k] - 1):
                            copy_rows(b.next(1), q)
                else:
                    wait(nc.scalar, c_mk, b.count(1, 1))
                    wait(nc.scalar, c_lhs, b.next(-1).count(3 * G, 0))
                    nc.scalar.activation(mkx[b.k][:, :, :, :].rearrange("p t a f -> p (t a) f"),
                                         bc(mkb[:, :, :].rearrange("p t a -> p (t a)"), D, 2),
                                         ACT.Copy).then_inc(c_mkx, 1)
                    wait(nc.scalar, c_rd, b.count(2, 2))
                    wait(nc.scalar, c_ms, b.count(4, 0))
                    nc.scalar.activation(ms[:, :, :], msg[b.k][:, :, :], ACT.Silu,
                                         scale=(D * 8) ** -0.5).then_inc(c_ms, 1)
                    for n in range(3):
                        if n:
                            wait(nc.scalar, c_m3, b.count(2, n))
                        else:
                            wait(nc.scalar, c_ms, b.count(4, 1))
                        nc.scalar.activation(m3[b.k][:, :, n, :], ms[:, :, :], ACT.Copy).then_inc(c_ms, 1)

            def act_first(b):
                for q in range(HGS[0] - 1):
                    copy_rows(b, q)

            loop(nc.scalar, act, NB, TB, before=act_first if help_ else None)

            def one_hot(b):
                wait(V, h_row[b.k], b.slot(32, 32))
                wait(V, h_g, groups(b.next(-1), 0))
                for c in range(KT):
                    V.tensor_scalar(hot_[b.k][:, c, :], rb2[b.k][:, :], pick[:, c:c + 1], None, ALU.is_equal)\
                        .then_inc(h_oh, 1)

            def mask(b, q):
                wait(V, h_g, groups(b, q + 1))
                wait(V, h_sel, slot_free(b, q))
                V.scalar_tensor_tensor(out=mx[par(b, q)][:, :], in0=ra[b.k][0:A9 * D, 512 * q:512 * q + 512],
                                       scalar=pick_row[0:A9 * D, 0:1], in1=PS[0:A9 * D, 4 + par(b, q), :],
                                       op0=ALU.is_equal, op1=ALU.mult).then_inc(h_mk, 1)

            def scale_rows(b):
                wait(V, c_g[b.k], b.slot(16 * NGS[b.k], 16 * NGS[b.k]))
                if help_:
                    wait(V, h_cp, groups(b, HGS[b.k]))
                prods = yg[b.k][:, :, 0:8 * D].rearrange("p t (r o) -> p t r o", r=8)
                co = coef_sb[:, b.cols(), :]
                V.tensor_tensor(prods, prods, bc(co, D, 3), ALU.mult).then_inc(c_rd, 1)

            def add_up(b):
                wait(V, c_rd, b.count(2, 1))
                if help_:
                    wait(V, c_run, b.next(-1).count(D, 0))
                else:
                    wait(V, c_ms, b.next(-1).count(4, 0))
                V.tensor_reduce(msg[b.k][:, :, :], yg[b.k][:, :, :].rearrange("p t (r o) -> p t o r", r=R),
                                X, ALU.add).then_inc(c_rd, 1)

            def dve_first(b):
                one_hot(b)
                for q in range(HGS[0]):
                    mask(b, q)
                one_hot(b.next(1))

            def by_destination(b):
                wait(V, c_rd, b.count(2, 2))
                wait(V, c_run, b.count(D, 0))
                wait(V, c_st[b.k], b.slot(16, 0))
                for f in range(D):
                    V.tensor_tensor_scan(run[b.k][:, :, f], keep[:, b.cols()], msg[b.k][:, :, f],
                                         run[1 - b.k][:, TB - 1, f:f + 1], ALU.mult, ALU.add).then_inc(c_run, 1)

            def masks(b):
                wait(V, c_mkx, b.count(1, 0))
                V.tensor_tensor(mkb[:, :, :], bc(av[:, b.cols()], 8, 2), bc(io8[:, :], TB, 1), ALU.is_equal)\
                    .then_inc(c_mk, 1)

            def less_part(b, n):
                wait(V, c_ms, b.count(4, 2 + n))
                V.tensor_tensor(ms[:, :, :], ms[:, :, :], m3[b.k][:, :, n, :], ALU.subtract).then_inc(c_m3, 1)

            def scatter_operands(b, q):
                if q == 0:
                    wait(V, c_bk, b.count(1, 1))
                    wait(V, c_mkx, b.count(1, 1))
                    wait(V, c_ms, b.count(4, 4))
                wait(V, c_ag, b.count(TB, 4 * q - 4))
                for n in range(3):
                    V.tensor_tensor(lhs[q % 2][:, :, n, :].rearrange("p t (a f) -> p t a f", a=8),
                                    mkx[b.k][:, 4 * q:4 * q + 4, :, :],
                                    bc(m3[b.k][:, 4 * q:4 * q + 4, n, :], 8, 2), ALU.mult).then_inc(c_lhs, 1)
                for r in range(4):
                    wait(V, c_ag, b.count(TB, 4 * q + r - 7))
                    V.tensor_scalar(hot[4 * (q % 2) + r][:, :], iob[:, :], bst[:, 4 * q + r:4 * q + r + 1], None,
                                    ALU.is_equal).then_inc(c_hot, 1)

            def dve(b):
                if help_:
                    nx = b.next(1) if b.next(1).exists() else None
                    if b.next(-1).exists():
                        by_destination(b.next(-1))
                    if nx:
                        mask(nx, 0)
                    scale_rows(b)
                    if nx:
                        mask(nx, 1)
                    if b.next(2).exists():
                        one_hot(b.next(2))
                    if nx:
                        mask(nx, 2)
                    add_up(b)
                    if nx and HGS[nx.k] > 3:
                        mask(nx, 3)
                else:
                    pv_ = b.next(-1) if b.next(-1).exists() else None
                    masks(b)
                    for q in range(G):
                        if q == 2:
                            scale_rows(b)
                        if pv_:
                            scatter_operands(pv_, q)
                        if q == 4:
                            add_up(b)
                        if q in (5, 6):
                            less_part(b, q - 5)
                    wait(V, c_hot, b.count(TB, 0))
                    V.tensor_copy(bst[:, :], bv[:, b.cols()]).then_inc(c_bk, 1)

            def dve_last(b):
                for q in range(G):
                    scatter_operands(b, q)

            loop(V, dve, NB, TB, before=dve_first if help_ else None, after=by_destination if help_ else dve_last)
            if by_source is None:
                for k in two:
                    nc.sync.wait_ge(c_st[k], 16 * NB // 2)
            together()

            if by_source is None:
                t(lambda e: e.matmul(PS[0:CH, 0, 0:D], before[:, :], run[1][:, TB - 1, :]))
                ch.step("rows", [lambda e: e.indirect_dma_start(
                    patch_g[:, 0:D], None, sums, bass.IndirectOffsetOnAxis(ap=patch_sum_src[:, 0:1], axis=0))], 16)
                v(lambda e: e.tensor_tensor(patch_g[:, 0:D], patch_g[:, 0:D], PS[0:CH, 0, 0:D], ALU.add))
                ch.wait(nc.gpsimd)
                nc.gpsimd.nop(nofuse=True)
                ch.step("rows", [lambda e: e.indirect_dma_start(
                    sums, bass.IndirectOffsetOnAxis(ap=patch_sum[:, 0:1], axis=0), patch_g[:, 0:D], None,
                    bounds_check=lim_s, oob_is_err=False)], 16)
            else:
                t(*[lambda e, k=k: e.matmul(PS[:, 6 + k, 0:A7 // 2], zz[:, 0:128], zz[:, 0:A7 // 2],
                                            start=False, stop=True) for k in two])
                big = sb("big", [128, A7], F32, L)
                nm = sb("nm", [128, 7, 128], F32, L)
                v(*[lambda e, k=k: e.tensor_copy(big[:, k * A7 // 2:(k + 1) * A7 // 2], PS[:, 6 + k, 0:A7 // 2])
                    for k in two])
                sizes = [min(128, A7 - 128 * k) for k in range(7)]
                t(*[lambda e, k=k: e.transpose(PS[0:sizes[k], k // 4, 128 * (k % 4):128 * (k % 4) + 128],
                                               big[:, 128 * k:128 * k + sizes[k]], ident[:, :]) for k in range(7)])
                v(*[lambda e, k=k: e.tensor_copy(nm[0:sizes[k], k, :],
                                                 PS[0:sizes[k], k // 4, 128 * (k % 4):128 * (k % 4) + 128])
                    for k in range(7)])
                aggd_v = aggd.rearrange("(a b) f -> b a f", a=8)
                dma(*[lambda e, k=k: e.dma_start(aggd_v[128 * k:128 * k + sizes[k], :, :],
                                                 nm[0:sizes[k], k, :].rearrange("p (a f) -> p a f", a=8))
                      for k in range(7)])
                dma(lambda e: e.dma_start(agg[:, 0:JT, :], aggd.rearrange("(j p) f -> p j f", p=128)))
            together()
            L.close()
            if by_source is None:
                for j in range(JT):
                    nc.gpsimd.indirect_dma_start(agg[:, j, :], None, sums,
                                                 bass.IndirectOffsetOnAxis(ap=end_idx[:, j:j + 1], axis=0))\
                        .then_inc(s_agg, 16)
                aggs[0] += JT

        def add_aggregated():
            nc.vector.wait_ge(s_agg, 16 * aggs[0])
            v(lambda e: e.tensor_tensor(hn[:, :, :], hn[:, :, :], agg[:, :, :], ALU.add))

        def log_softmax(x):
            v(lambda e: e.tensor_reduce(red[:, :], x[:, :, :], X, ALU.max))
            v(lambda e: e.tensor_tensor(x[:, :, :], x[:, :, :], bc(red[:, :], D, 2), ALU.subtract))
            a(lambda e: e.activation(tn[:, :, :], x[:, :, :], ACT.Exp))
            v(lambda e: e.tensor_reduce(red[:, :], tn[:, :, :], X, ALU.add))
            a(lambda e: e.activation(red[:, :], red[:, :], ACT.Ln))
            v(lambda e: e.tensor_tensor(x[:, :, :], x[:, :, :], bc(red[:, :], D, 2), ALU.subtract))

        h1 = xn
        L2 = ExitStack()
        s_coef = sem("s_coef")
        for n, (W, root, bias) in enumerate((("W1", "root1", "b1"), ("W2", "root2", "b2"))):
            expand_nodes(f"e1{n}", h1, io["L1_gnn_" + W].rearrange("r i o -> i r o"))
            split_parts(h1)
            conv(f"r{n}", io["src"])
            if n == 1:
                ch.wait(nc.sync)
                nc.sync.dma_start(coef_sb[:, :, :], io["edge_attr_8"].rearrange("(p t) f -> p t f", p=CH))\
                    .then_inc(s_coef, 16)
                av = sb("av", [CH, T], F32, L2)
                bv = sb("bv", [CH, T], F32, L2)
                sr = ExitStack()
                si = sb("si", [CH, T], I32, sr)
                dma(lambda e: e.dma_start(si[:, :], src_c))
                v(lambda e: e.tensor_copy(bv[:, :], si[:, :]))
                v(lambda e: e.tensor_scalar(av[:, :], bv[:, :], float(A7), None, ALU.is_ge))
                for k in range(2, 8):
                    v(lambda e: e.scalar_tensor_tensor(out=av[:, :], in0=bv[:, :], scalar=float(k * A7), in1=av[:, :],
                                                       op0=ALU.is_ge, op1=ALU.add))
                v(lambda e: e.scalar_tensor_tensor(out=bv[:, :], in0=av[:, :], scalar=-float(A7), in1=bv[:, :],
                                                   op0=ALU.mult, op1=ALU.add))
                sr.close()
            turned(h1)
            ps = times(io["L1_gnn_" + root])
            rb_ = row_of(io["L1_gnn_" + bias])
            v(lambda e: e.tensor_tensor(hn[:, :, :], ps.rearrange("p (j f) -> p j f", f=D), rb_, ALU.add))
            add_aggregated()
            if n == 0:
                v(lambda e: e.tensor_scalar(hn[:, :, :], hn[:, :, :], 0.0, None, ALU.max))
            h1 = hn
        log_softmax(hn)
        layernorm(xn, hn)

        nc.sync.wait_ge(s_coef, 16)
        expand_nodes("e2", xn, io["L2_gnn_W_msg_tp"])
        conv("m", io["dst"], by_source=(av, bv))
        turned(agg)
        ps = times(io["L2_gnn_W_msg_lin"])
        v(lambda e: e.tensor_scalar(flat(agg[:, :, :]), ps, D ** -0.5, None, ALU.mult))
        zu = sb("zu", [128, 2 * C2], F32, L2)
        zuT = sb("zuT", [128, 4, 128], F32, L2)
        wu = sb("wu", [128, 2, D], F32, L2)
        dma(lambda e: e.dma_start(wu[:, :, :], io["L2_gnn_W_upd_tp"].rearrange("(a i) h k -> (i h) a k", a=2)))
        for j in range(0, NJ, 2):
            v(lambda e: e.tensor_tensor(zu[:, :].rearrange("p (j i h) -> p j i h", j=2, i=D),
                                        bc(xn[:, j:j + 2, :], D, 3), bc(agg[:, j:j + 2, :], D, 2), ALU.mult))
            t(*[lambda e, k=k: e.transpose(PS[:, 0, 128 * k:128 * k + 128], zu[:, 128 * k:128 * k + 128], ident[:, :])
                for k in range(4)])
            v(lambda e: e.tensor_copy(zuT[:, :, :].rearrange("p a c -> p (a c)"), PS[:, 0, :]))
            t(*[lambda e, k=k: e.matmul(PS[:, 4 + k // 2, (j // 2) * D:(j // 2) * D + D], zuT[:, k, :], wu[:, k % 2, :],
                                        start=(k % 2 == 0), stop=(k % 2 == 1)) for k in range(4)])
        v(*[lambda e, k=k: e.tensor_copy(hn[:, k::2, :], PS[:, 4 + k, 0:NJ // 2 * D].rearrange("p (j f) -> p j f", f=D))
            for k in two])
        a(lambda e: e.activation(hn[:, :, :], hn[:, :, :], ACT.Silu, scale=1.0 / 16))
        turned(hn)
        ps = times(io["L2_gnn_W_upd_lin"])
        v(lambda e: e.scalar_tensor_tensor(out=flat(hn[:, :, :]), in0=ps, scalar=D ** -0.5, in1=flat(xn[:, :, :]),
                                           op0=ALU.mult, op1=ALU.add))
        layernorm(xn, hn)
        together()
        L2.close()

        h3 = xn
        part = sb("part", [128, D])
        mean = sb("mean", [128, D])
        for n in range(3):
            expand_nodes(f"e3{n}", h3, io["L3_gnn_edge_w"][n, :, :].rearrange("j (i o) -> i j o", i=D),
                         io["L3_gnn_edge_b"][n, :].rearrange("(i o) -> i o", i=D))
            split_parts(h3)
            conv(f"c{n}", io["src"], both=True)
            turned(h3)
            ps = times(io["L3_gnn_root_w"][n, :, :])
            rb_ = row_of(io["L3_gnn_root_b"][n, :])
            v(lambda e: e.tensor_tensor(hn[:, :, :], ps.rearrange("p (j f) -> p j f", f=D), rb_, ALU.add))
            add_aggregated()

            def column_mean():
                v(lambda e: e.tensor_tensor(tn[:, :, :], tn[:, :, :], bc(valid[:, :], D, 2), ALU.mult))
                v(lambda e: e.tensor_reduce(part[:, :], tn[:, :, :].rearrange("p j f -> p f j"), X, ALU.add))
                t(lambda e: e.matmul(PS[:, 0, 0:D], ones[:, :], part[:, :]))
                v(lambda e: e.tensor_scalar(mean[:, :], PS[:, 0, 0:D], 1.0 / N, None, ALU.mult))

            if n < 2:
                v(lambda e: e.tensor_copy(tn[:, :, :], hn[:, :, :]))
                column_mean()
                v(lambda e: e.tensor_tensor(hn[:, :, :], hn[:, :, :], bc(mean[:, :], NJ, 1), ALU.subtract))
                v(lambda e: e.tensor_tensor(tn[:, :, :], hn[:, :, :], hn[:, :, :], ALU.mult))
                column_mean()
                v(lambda e: e.tensor_scalar(mean[:, :], mean[:, :], EPS, None, ALU.add))
                a(lambda e: e.activation(mean[:, :], mean[:, :], ACT.Sqrt))
                v(lambda e: e.reciprocal(mean[:, :], mean[:, :]))
                row_of(io["L3_gnn_bn_gamma"][n, :])
                v(lambda e: e.tensor_tensor(mean[:, :], mean[:, :], row_b[:, :], ALU.mult))
                v(lambda e: e.tensor_tensor(hn[:, :, :], hn[:, :, :], bc(mean[:, :], NJ, 1), ALU.mult))
                rb_ = row_of(io["L3_gnn_bn_beta"][n, :])
                v(lambda e: e.tensor_tensor(hn[:, :, :], hn[:, :, :], rb_, ALU.add))
            v(lambda e: e.tensor_scalar(hn[:, :, :], hn[:, :, :], 0.0, None, ALU.max))
            h3 = hn
        turned(hn)
        ps = times(io["L3_gnn_pred_w"])
        rb_ = row_of(io["L3_gnn_pred_b"])
        v(lambda e: e.tensor_tensor(hn[:, :, :], ps.rearrange("p (j f) -> p j f", f=D), rb_, ALU.add))
        layernorm(xn, hn)
        dma(lambda e: e.dma_start(out[0:6144, :].rearrange("(j p) f -> p j f", p=128), xn[:, 0:48, :]),
            lambda e: e.dma_start(out[6144:N, :], xn[0:N - 6144, 48, :]))
        ch.wait(nc.sync)


NAMES = ['x', 'src', 'dst', 'edge_attr_16', 'edge_attr_8', 'edge_type_8',
         'L0_gnn_W_msg', 'L0_gnn_b_msg', 'L0_gnn_W_attn', 'L0_gnn_b_attn',
         'L1_gnn_W1', 'L1_gnn_root1', 'L1_gnn_b1', 'L1_gnn_W2', 'L1_gnn_root2', 'L1_gnn_b2',
         'L2_gnn_W_msg_tp', 'L2_gnn_W_msg_lin', 'L2_gnn_W_upd_tp', 'L2_gnn_W_upd_lin',
         'L3_gnn_edge_w', 'L3_gnn_edge_b', 'L3_gnn_root_w', 'L3_gnn_root_b',
         'L3_gnn_bn_gamma', 'L3_gnn_bn_beta', 'L3_gnn_pred_w', 'L3_gnn_pred_b']


def kernel(**inputs):
    import numpy as np
    import concourse.bacc as bacc
    from concourse.bass_utils import run_bass_kernel_spmd

    nc = bacc.Bacc("TRN2", target_bir_lowering=False, num_devices=1)
    arrays, io = {}, {}
    for name in NAMES:
        arr = np.ascontiguousarray(inputs[name])
        arrays["in_" + name] = arr
        io[name] = nc.dram_tensor("in_" + name, arr.shape, mybir.dt.from_np(arr.dtype), kind="ExternalInput").ap()
    out = nc.dram_tensor("out", (N, D), F32, kind="ExternalOutput").ap()
    program(nc, io, out)
    r = run_bass_kernel_spmd(nc, [arrays], core_ids=[0])
    return r.results[0]["out"]
```
